# Optimizing a Trainium2 kernel written in Bass

```python
import numpy as np
import jax
import jax.numpy as jnp

def _softmax(x, axis=-1):
    return jax.nn.softmax(x, axis=axis)

def _gelu(x):
    return jax.nn.gelu(x, approximate=True)

def _silu(x):
    return jax.nn.silu(x)

def _sigmoid(x):
    return jax.nn.sigmoid(x)

def _layernorm(x, axis=-1, eps=1e-05):
    m = jnp.mean(x, axis=axis, keepdims=True)
    v = jnp.var(x, axis=axis, keepdims=True)
    return (x - m) / jnp.sqrt(v + eps)

def _scatter_add(tgt, idx, src, axis=0):
    return tgt.at[idx].add(src)

def _segment_sum(src, seg, n):
    return jax.ops.segment_sum(src, seg, n)
kernel_name = 'mk_adj_ffn_d2_adj_r2_1663c5'

def setup_inputs(seed: int=0):
    np.random.seed(seed)
    _w = jnp.asarray

    def _rec_inputs():
        import jax
        import jax.numpy as jnp
        _gk = jax.random.key(seed)
        x = -7.109e-05 + 0.9999 * jax.random.normal(jax.random.fold_in(_gk, 1), (128, 64, 128), jnp.float32)
        _a = jax.random.bernoulli(jax.random.fold_in(_gk, 2), 0.0625, (64, 64))
        _a = jnp.logical_or(_a, jnp.eye(64, dtype=bool))
        adj = _a.astype(jnp.int32)
        return (x, adj)
    x, adj = _rec_inputs()

    def _L0_gnn_setup():
        import jax, jax.numpy as jnp
        import numpy as np
        EPS = 1e-05

        def _layernorm(x, g, b):
            mu = jnp.mean(x, axis=-1, keepdims=True)
            var = jnp.mean(jnp.square(x - mu), axis=-1, keepdims=True)
            return (x - mu) * jax.lax.rsqrt(var + EPS) * g + b
        key = jax.random.key(seed)
        ks = jax.random.split(key, 8)
        F, N, C, H = (2048, 64, 128, 8)
        x = jax.random.normal(ks[0], (F, N, C), dtype=jnp.float32)
        adj = jax.random.randint(ks[1], (N, N), 0, 2, dtype=jnp.int32)
        adj = jnp.maximum(adj, jnp.eye(N, dtype=jnp.int32))
        s = 1.0 / np.sqrt(C)
        w_qkv = jax.random.normal(ks[2], (C, 3 * C), dtype=jnp.float32) * s
        w1 = jax.random.normal(ks[3], (C, C), dtype=jnp.float32) * s
        b1 = jnp.zeros((C,), dtype=jnp.float32)
        w2 = jax.random.normal(ks[4], (C, C), dtype=jnp.float32) * s
        b2 = jnp.zeros((C,), dtype=jnp.float32)
        ln1_g = jnp.ones((C,), jnp.float32)
        ln1_b = jnp.zeros((C,), jnp.float32)
        ln2_g = jnp.ones((C,), jnp.float32)
        ln2_b = jnp.zeros((C,), jnp.float32)
        return {'x': x, 'adj': adj, 'w_qkv': w_qkv, 'ln1_g': ln1_g, 'ln1_b': ln1_b, 'ln2_g': ln2_g, 'ln2_b': ln2_b, 'w1': w1, 'b1': b1, 'w2': w2, 'b2': b2}
    _L0_gnn_all = _L0_gnn_setup()
    _L0_gnn_in = {k: v for k, v in _L0_gnn_all.items() if k in ('w_qkv', 'ln1_g', 'ln1_b', 'ln2_g', 'ln2_b', 'w1', 'b1', 'w2', 'b2')}
    del _L0_gnn_all

    def _L0_ffn_setup():
        import jax, jax.numpy as jnp
        import numpy as np
        B, T, C = (64, 192, 128)
        NH, NKV = (4, 2)
        HD = C // NH
        NREP = NH // NKV
        NE, TOPK = (8, 2)
        HID = int(8 / 3 * C)
        EPS_RMS = 1e-06

        def _rope_tables(t_len):
            inv_freq = 1.0 / 10000.0 ** (np.arange(0, HD, 2, dtype=np.float32) / HD)
            t = np.arange(t_len, dtype=np.float32)
            freqs = np.outer(t, inv_freq)
            emb = np.concatenate([freqs, freqs], axis=-1)
            return (jnp.asarray(np.cos(emb)), jnp.asarray(np.sin(emb)))

        def _rotate_half(x):
            h = x.shape[-1] // 2
            return jnp.concatenate([-x[..., h:], x[..., :h]], axis=-1)

        def _rmsnorm(v, w):
            return v * jax.lax.rsqrt(jnp.mean(v * v, axis=-1, keepdims=True) + EPS_RMS) * w
        key = jax.random.key(seed)
        ks = jax.random.split(key, 10)
        s = lambda k, shape: jax.random.normal(k, shape, jnp.float32) * 0.02
        return {'x': jax.random.normal(ks[0], (B, T, C), jnp.float32), 'ln1_w': jnp.ones((C,), jnp.float32), 'ln2_w': jnp.ones((C,), jnp.float32), 'wq': s(ks[1], (NH * HD, C)), 'wk': s(ks[2], (NKV * HD, C)), 'wv': s(ks[3], (NKV * HD, C)), 'wo': s(ks[4], (C, C)), 'router_w': s(ks[5], (NE, C)), 'w1': s(ks[6], (NE, HID, C)), 'w2': s(ks[7], (NE, C, HID)), 'w3': s(ks[8], (NE, HID, C))}
    _L0_ffn_all = _L0_ffn_setup()
    _L0_ffn_in = {k: v for k, v in _L0_ffn_all.items() if k in ('ln1_w', 'ln2_w', 'wq', 'wk', 'wv', 'wo', 'router_w', 'w1', 'w2', 'w3')}
    del _L0_ffn_all

    def _L1_gnn_setup():
        import jax, jax.numpy as jnp
        import numpy as np
        ALPHA = 0.2
        NEG_INF = -1000000000000.0
        key = jax.random.key(seed)
        k1, k2, k3, k4, k5 = jax.random.split(key, 5)
        B, N, C_in, C_out = (8, 1024, 128, 128)
        inp = jax.random.normal(k1, (B, N, C_in), dtype=jnp.float32)
        adj = jax.random.randint(k2, (N, N), 0, 2, dtype=jnp.int32)
        limit = 1.414 * np.sqrt(6.0 / (C_in + C_out))
        W1 = jax.random.uniform(k3, (C_in, C_out), jnp.float32, -limit, limit)
        W2 = jax.random.uniform(k4, (C_in, C_out), jnp.float32, -limit, limit)
        W3 = jax.random.uniform(k5, (C_in, C_out), jnp.float32, -limit, limit)
        return {'inp': inp, 'adj': adj, 'W1': W1, 'W2': W2, 'W3': W3}
    _L1_gnn_all = _L1_gnn_setup()
    _L1_gnn_in = {k: v for k, v in _L1_gnn_all.items() if k in ('W1', 'W2', 'W3')}
    del _L1_gnn_all

    def _L1_ffn_setup():
        import jax, jax.numpy as jnp
        import numpy as np
        TOP_K = 2
        key = jax.random.key(seed)
        ks = jax.random.split(key, 4)
        B, L, D, H, E = (8, 2048, 128, 512, 8)
        s = 0.02
        return {'x': jax.random.normal(ks[0], (B, L, D), jnp.float32), 'Wg': jax.random.normal(ks[1], (D, E), jnp.float32) * s, 'bg': jnp.zeros((E,), jnp.float32), 'W1': jax.random.normal(ks[2], (E, D, H), jnp.float32) * s, 'b1': jnp.zeros((E, H), jnp.float32), 'W2': jax.random.normal(ks[3], (E, H, D), jnp.float32) * s, 'b2': jnp.zeros((E, D), jnp.float32)}
    _L1_ffn_all = _L1_ffn_setup()
    _L1_ffn_in = {k: v for k, v in _L1_ffn_all.items() if k in ('Wg', 'bg', 'W1', 'b1', 'W2', 'b2')}
    del _L1_ffn_all
    return {'x': x, 'adj': adj, 'L0_gnn_w_qkv': _L0_gnn_in['w_qkv'], 'L0_gnn_ln1_g': _L0_gnn_in['ln1_g'], 'L0_gnn_ln1_b': _L0_gnn_in['ln1_b'], 'L0_gnn_ln2_g': _L0_gnn_in['ln2_g'], 'L0_gnn_ln2_b': _L0_gnn_in['ln2_b'], 'L0_gnn_w1': _L0_gnn_in['w1'], 'L0_gnn_b1': _L0_gnn_in['b1'], 'L0_gnn_w2': _L0_gnn_in['w2'], 'L0_gnn_b2': _L0_gnn_in['b2'], 'L0_ffn_ln1_w': _L0_ffn_in['ln1_w'], 'L0_ffn_ln2_w': _L0_ffn_in['ln2_w'], 'L0_ffn_wq': _L0_ffn_in['wq'], 'L0_ffn_wk': _L0_ffn_in['wk'], 'L0_ffn_wv': _L0_ffn_in['wv'], 'L0_ffn_wo': _L0_ffn_in['wo'], 'L0_ffn_router_w': _L0_ffn_in['router_w'], 'L0_ffn_w1': _L0_ffn_in['w1'], 'L0_ffn_w2': _L0_ffn_in['w2'], 'L0_ffn_w3': _L0_ffn_in['w3'], 'L1_gnn_W1': _L1_gnn_in['W1'], 'L1_gnn_W2': _L1_gnn_in['W2'], 'L1_gnn_W3': _L1_gnn_in['W3'], 'L1_ffn_Wg': _L1_ffn_in['Wg'], 'L1_ffn_bg': _L1_ffn_in['bg'], 'L1_ffn_W1': _L1_ffn_in['W1'], 'L1_ffn_b1': _L1_ffn_in['b1'], 'L1_ffn_W2': _L1_ffn_in['W2'], 'L1_ffn_b2': _L1_ffn_in['b2']}

def reference(x, adj, L0_gnn_w_qkv, L0_gnn_ln1_g, L0_gnn_ln1_b, L0_gnn_ln2_g, L0_gnn_ln2_b, L0_gnn_w1, L0_gnn_b1, L0_gnn_w2, L0_gnn_b2, L0_ffn_ln1_w, L0_ffn_ln2_w, L0_ffn_wq, L0_ffn_wk, L0_ffn_wv, L0_ffn_wo, L0_ffn_router_w, L0_ffn_w1, L0_ffn_w2, L0_ffn_w3, L1_gnn_W1, L1_gnn_W2, L1_gnn_W3, L1_ffn_Wg, L1_ffn_bg, L1_ffn_W1, L1_ffn_b1, L1_ffn_W2, L1_ffn_b2):
    import jax
    import jax.numpy as jnp

    def _L0_gnn_ref(x, adj, w_qkv, ln1_g, ln1_b, ln2_g, ln2_b, w1, b1, w2, b2):
        import jax, jax.numpy as jnp
        import numpy as np
        EPS = 1e-05

        def _layernorm(x, g, b):
            mu = jnp.mean(x, axis=-1, keepdims=True)
            var = jnp.mean(jnp.square(x - mu), axis=-1, keepdims=True)
            return (x - mu) * jax.lax.rsqrt(var + EPS) * g + b
        F, N, C = x.shape
        H = 8
        D = C // H
        qkv = jnp.einsum('fnc,ck->fnk', x, w_qkv)
        q, k, v = jnp.split(qkv, 3, axis=-1)
        q = q.reshape(F, N, H, D)
        k = k.reshape(F, N, H, D)
        v = v.reshape(F, N, H, D)
        scores = jnp.einsum('fnhd,fmhd->fhnm', q, k) / jnp.sqrt(jnp.asarray(D, x.dtype))
        mask = (adj > 0)[None, None, :, :]
        scores = jnp.where(mask, scores, jnp.asarray(-1000000000.0, x.dtype))
        attn = jax.nn.softmax(scores, axis=-1)
        t = jnp.einsum('fhnm,fmhd->fnhd', attn, v).reshape(F, N, C)
        x = _layernorm(x + t, ln1_g, ln1_b)
        h = jax.nn.relu(jnp.einsum('fnc,cd->fnd', x, w1) + b1)
        f_out = jnp.einsum('fnd,dc->fnc', h, w2) + b2
        x = _layernorm(x + f_out, ln2_g, ln2_b)
        return x

    def _L0_ffn_ref(x, ln1_w, ln2_w, wq, wk, wv, wo, router_w, w1, w2, w3):
        import jax, jax.numpy as jnp
        import numpy as np
        B, T, C = (64, 192, 128)
        NH, NKV = (4, 2)
        HD = C // NH
        NREP = NH // NKV
        NE, TOPK = (8, 2)
        HID = int(8 / 3 * C)
        EPS_RMS = 1e-06

        def _rope_tables(t_len):
            inv_freq = 1.0 / 10000.0 ** (np.arange(0, HD, 2, dtype=np.float32) / HD)
            t = np.arange(t_len, dtype=np.float32)
            freqs = np.outer(t, inv_freq)
            emb = np.concatenate([freqs, freqs], axis=-1)
            return (jnp.asarray(np.cos(emb)), jnp.asarray(np.sin(emb)))

        def _rotate_half(x):
            h = x.shape[-1] // 2
            return jnp.concatenate([-x[..., h:], x[..., :h]], axis=-1)

        def _rmsnorm(v, w):
            return v * jax.lax.rsqrt(jnp.mean(v * v, axis=-1, keepdims=True) + EPS_RMS) * w
        Bx, Tx, Cx = x.shape
        h = _rmsnorm(x, ln1_w)
        q = (h @ wq.T).reshape(Bx, Tx, NH, HD).transpose(0, 2, 1, 3)
        k = (h @ wk.T).reshape(Bx, Tx, NKV, HD).transpose(0, 2, 1, 3)
        v = (h @ wv.T).reshape(Bx, Tx, NKV, HD).transpose(0, 2, 1, 3)
        cos, sin = _rope_tables(Tx)
        cos, sin = (cos[None, None], sin[None, None])
        q = q * cos + _rotate_half(q) * sin
        k = k * cos + _rotate_half(k) * sin
        k = jnp.repeat(k, NREP, axis=1)
        v = jnp.repeat(v, NREP, axis=1)
        scores = jnp.einsum('bhtd,bhsd->bhts', q, k) / jnp.sqrt(jnp.float32(HD))
        causal = jnp.tril(jnp.ones((Tx, Tx), dtype=bool))
        scores = jnp.where(causal[None, None], scores, jnp.float32(-1e+30))
        att = jax.nn.softmax(scores, axis=-1)
        y = jnp.einsum('bhts,bhsd->bhtd', att, v).transpose(0, 2, 1, 3).reshape(Bx, Tx, Cx)
        x = x + y @ wo.T
        flat = _rmsnorm(x, ln2_w).reshape(-1, Cx)
        probs = jax.nn.softmax(flat @ router_w.T, axis=-1)
        tp, ti = jax.lax.top_k(probs, TOPK)
        tp = tp / (jnp.sum(tp, axis=-1, keepdims=True) + 1e-09)
        weights = jnp.sum(tp[..., None] * jax.nn.one_hot(ti, NE, dtype=flat.dtype), axis=1)
        out = jnp.zeros_like(flat)
        for e in range(NE):
            hh = jax.nn.silu(flat @ w1[e].T) * (flat @ w3[e].T)
            out = out + weights[:, e:e + 1] * (hh @ w2[e].T)
        return x + out.reshape(Bx, Tx, Cx)

    def _L1_gnn_ref(inp, adj, W1, W2, W3):
        import jax, jax.numpy as jnp
        import numpy as np
        ALPHA = 0.2
        NEG_INF = -1000000000000.0
        h1 = jnp.einsum('bnc,cd->bnd', inp, W1)
        h2 = jnp.einsum('bnc,cd->bnd', inp, W2)
        h3 = jnp.einsum('bnc,cd->bnd', inp, W3)
        e = jnp.einsum('bnd,bmd->bnm', h1, h2)
        e = jax.nn.leaky_relu(e, ALPHA)
        e = jnp.where(adj[None, :, :] > 0, e, NEG_INF)
        attention = jax.nn.softmax(e, axis=-1)
        h_prime = jnp.einsum('bnm,bmd->bnd', attention, h3)
        return jax.nn.relu(h_prime)

    def _L1_ffn_ref(x, Wg, bg, W1, b1, W2, b2):
        import jax, jax.numpy as jnp
        import numpy as np
        TOP_K = 2
        B, L, D = x.shape
        E = W1.shape[0]
        xf = x.reshape(-1, D)
        gate_logits = xf @ Wg + bg
        top_w, top_i = jax.lax.top_k(gate_logits, TOP_K)
        top_w = jax.nn.softmax(top_w, axis=-1)
        w_dense = jnp.sum(jax.nn.one_hot(top_i, E, dtype=xf.dtype) * top_w[..., None], axis=1)
        out = jnp.zeros_like(xf)
        for e in range(E):
            h = jax.nn.gelu(xf @ W1[e] + b1[e], approximate=False)
            out = out + w_dense[:, e:e + 1] * (h @ W2[e] + b2[e])
        return out.reshape(B, L, D)
    x = x + _L0_gnn_ref(_layernorm(x, axis=-1), adj, L0_gnn_w_qkv, L0_gnn_ln1_g, L0_gnn_ln1_b, L0_gnn_ln2_g, L0_gnn_ln2_b, L0_gnn_w1, L0_gnn_b1, L0_gnn_w2, L0_gnn_b2)
    x = x + _L0_ffn_ref(_layernorm(x, axis=-1), L0_ffn_ln1_w, L0_ffn_ln2_w, L0_ffn_wq, L0_ffn_wk, L0_ffn_wv, L0_ffn_wo, L0_ffn_router_w, L0_ffn_w1, L0_ffn_w2, L0_ffn_w3)
    x = x + _L1_gnn_ref(_layernorm(x, axis=-1), adj, L1_gnn_W1, L1_gnn_W2, L1_gnn_W3)
    x = x + _L1_ffn_ref(_layernorm(x, axis=-1), L1_ffn_Wg, L1_ffn_bg, L1_ffn_W1, L1_ffn_b1, L1_ffn_W2, L1_ffn_b2)
    return x

_drawn_inputs = setup_inputs


def setup_inputs(seed=0):
    import zlib

    import numpy as np

    out = dict(_drawn_inputs(seed))
    spreads = {'L0_gnn_ln1_g': (1.0, 0.2),
     'L0_gnn_ln1_b': (0.0, 0.1),
     'L0_gnn_ln2_g': (1.0, 0.2),
     'L0_gnn_ln2_b': (0.0, 0.1),
     'L0_gnn_b1': (0.0, 0.1),
     'L0_gnn_b2': (0.0, 0.1),
     'L0_ffn_ln1_w': (1.0, 0.6),
     'L0_ffn_ln2_w': (1.0, 0.6),
     'L1_ffn_bg': (0.0, 0.44),
     'L1_ffn_b1': (0.0, 0.8),
     'L1_ffn_b2': (0.0, 1.555)}
    factors = {'L0_ffn_wq': 8.0,
     'L0_ffn_wk': 8.0,
     'L0_ffn_wv': 5.999,
     'L0_ffn_wo': 6.098,
     'L0_ffn_router_w': 8.0,
     'L0_ffn_w1': 8.0,
     'L0_ffn_w2': 8.0,
     'L0_ffn_w3': 8.0,
     'L1_ffn_W1': 4.528,
     'L1_ffn_W2': 4.12}
    for name, (base, spread) in spreads.items():
        noise = np.random.default_rng([zlib.crc32(name.encode()), seed]).standard_normal(out[name].shape)
        drawn = base * np.exp(spread * noise) if base else spread * noise
        out[name] = jnp.asarray(drawn.astype(out[name].dtype))
    for name, factor in factors.items():
        out[name] = (out[name] * factor).astype(out[name].dtype)
    return out
```

```python
from contextlib import ExitStack

import concourse.bass as bass
from concourse import mybir

F32 = mybir.dt.float32
BF16 = mybir.dt.bfloat16
I32 = mybir.dt.int32
U32 = mybir.dt.uint32
ALU = mybir.AluOpType
ACT = mybir.ActivationFunctionType
AX = mybir.AxisListType

FRAMES, NODES, C = 128, 64, 128
PAIRS = FRAMES // 2
PG = 4
GROUPS = PAIRS // PG
GT = PG * 128
EPS_LN = 1e-5
EPS_RMS = 1e-6
H0, D0 = 8, 16
H1, KV1, D1 = 4, 2, 32
NE = 8
HID1 = 341
HID2 = 512
TILE = 256
CAP = PAIRS * 128 + TILE
TILES = 2 * PAIRS * 128 // TILE + NE
UN = 4
CH1 = [(0, 128), (128, 128), (256, 85)]
CH2 = [(128 * i, 128) for i in range(4)]


TAKEN = []


class Signal:

    def __init__(self, sem, per):
        self.sem, self.per = sem, per

    def now(self, g, j=0):
        return self.sem, (g + 1) * self.per + (j + 1)

    def before(self, g, j=None):
        return self.sem, g * self.per + (self.per if j is None else j + 1)


def take_semaphore(ctx, nc, name):
    sem = ctx.enter_context(nc.semaphore(name))
    TAKEN.append(sem)
    return sem


def clear_taken(nc):
    with nc.Block() as block:
        @block.gpsimd
        def _(pool):
            nums = sorted(s.num for s in TAKEN)
            while nums:
                n = 1
                while n < len(nums) and nums[n] == nums[0] + n:
                    n += 1
                pool.sem_clear(range(nums[0], nums[0] + n))
                del nums[:n]
    TAKEN.clear()


def open_signals(eng, signals):
    for s in signals:
        eng.sem_inc(s.sem, s.per)


def turns(eng, first, last, body):
    with eng.Fori(first, last) as g:
        body(g)


def row_bcast(vec, rows=128):
    n = vec.shape[-1]
    return bass.AP(vec.tensor, vec.offset, [[0, rows], [1, n]])


def build(nc, A, out):
    TAKEN.clear()
    with ExitStack() as ctx:
        def sb(name, shape, dt=F32):
            return ctx.enter_context(nc.sbuf_tensor(name, shape, dt))

        x = sb("x", [128, PAIRS, C])
        ident = sb("ident", [128, 128])
        identb = sb("identb", [128, 128], BF16)
        half = sb("half", [128, 8])
        rev = sb("rev", [128, NE])
        tri = sb("tri", [128, 128], BF16)
        tri32 = sb("tri32", [128, 128])
        ones = sb("ones", [128, 128], BF16)
        maskb = sb("maskb", [128, NODES], BF16)
        adj = sb("adj_sb", [128, NODES], I32)
        load_sem = ctx.enter_context(nc.semaphore("load_sem"))
        setup_sem = ctx.enter_context(nc.semaphore("setup_sem"))
        banks = [ctx.enter_context(nc.psum_tensor(f"bank{i}", [128, 512], F32)) for i in range(8)]
        x_dram = A["x"].rearrange("(t f) n c -> (f n) t c", f=2)
        out_dram = out.rearrange("(t f) n c -> (f n) t c", f=2)

        with nc.Block() as block:
            @block.sync
            def _(sp):
                sp.dma_start(ident[:, :], A["c_ident"]).then_inc(load_sem, 16)
                sp.dma_start(rev[:, :], A["c_rev"]).then_inc(load_sem, 16)
                sp.dma_start(tri32[:, :], A["c_tri"]).then_inc(load_sem, 16)
                for f in range(2):
                    sp.dma_start(adj[64 * f:64 * f + 64, :], A["adj"]).then_inc(load_sem, 16)
                for i in range(4):
                    n = PAIRS // 4
                    sp.dma_start(x[:, n * i:n * i + n, :], x_dram[:, n * i:n * i + n, :]).then_inc(load_sem, 16)
                sp.wait_ge(load_sem, 16 * 9)

            @block.vector
            def _(dve):
                dve.wait_ge(load_sem, 16 * 9)
                dve.tensor_copy(identb[:, :], ident[:, :])
                dve.tensor_copy(tri[:, :], tri32[:, :])

            @block.gpsimd
            def _(pool):
                pool.memset(half[:, :], -0.5).then_inc(setup_sem, 1)
                pool.memset(ones[:, :], 1.0).then_inc(setup_sem, 1)

        common = dict(x=x, ident=ident, identb=identb, half=half, maskb=maskb, adj=adj, banks=banks)
        phase_gnn0(nc, A, **common)
        list1 = nc.dram_tensor("dispatch1", ((NE + 1) * CAP, C), F32, kind="Internal").ap()
        c = dict(ident=ident, identb=identb, half=half, rev=rev, tri=tri, ones=ones, adj=adj)
        state = dict(base=sb("base1", [128, NE]), posf=sb("posf1", [128, 2, PAIRS]), pos=sb("pos1", [128, 2, PAIRS], I32), w=sb("w1", [128, 2, PAIRS]))
        phase_attn1(nc, A, x, banks, c, state, list1)
        rows1 = nc.dram_tensor("rows1", (TILES * TILE, C), F32, kind="Internal").ap()
        phase_experts(nc, A, banks, c, state, list1, rows1, A["c_wall1"], True, "m1")
        list2 = nc.dram_tensor("dispatch2", ((NE + 1) * CAP, C), F32, kind="Internal").ap()
        state2 = dict(base=sb("base2", [128, NE]), posf=sb("posf2", [128, 2, PAIRS]), pos=sb("pos2", [128, 2, PAIRS], I32), w=sb("w2", [128, 2, PAIRS]))
        phase_gnn1(nc, A, x, banks, c, state, rows1, state2, list2)
        rows2 = nc.dram_tensor("rows2", (TILES * TILE, C), F32, kind="Internal").ap()
        phase_experts(nc, A, banks, c, state2, list2, rows2, A["c_wall2"], False, "m2")
        phase_finish(nc, x, c, state2, rows2, out_dram)


def norm_stats(dve, src, st, mean, ve, bn, part, vs, g, eps, waits=(), gate=None):
    for w in waits:
        dve.wait_ge(*w)
    if gate is not None:
        dve.sem_inc(gate.sem, 1)
    for p in range(PG):
        dve.bn_stats(st[:, p, 0:6], src(p)).then_inc(bn.sem, 1)
    dve.wait_ge(*bn.now(g, PG - 1))
    dve.tensor_tensor(st[:, :, 6], st[:, :, 1], st[:, :, 4], ALU.add).then_inc(part.sem, 1)
    dve.tensor_tensor(st[:, :, 7], st[:, :, 1], st[:, :, 4], ALU.subtract).then_inc(part.sem, 1)
    dve.tensor_tensor(st[:, :, 8], st[:, :, 2], st[:, :, 5], ALU.add).then_inc(part.sem, 1)
    dve.wait_ge(*part.now(g, 1))
    dve.tensor_scalar(mean[:, :], st[:, :, 6], 0.5, None, ALU.mult).then_inc(part.sem, 1)
    dve.scalar_tensor_tensor(out=st[:, :, 9], in0=st[:, :, 7], scalar=0.25, in1=st[:, :, 7],
                             op0=ALU.mult, op1=ALU.mult).then_inc(part.sem, 1)
    dve.wait_ge(*part.now(g, 2))
    dve.tensor_scalar(st[:, :, 10], st[:, :, 8], 1.0 / C, eps, ALU.mult, ALU.add).then_inc(part.sem, 1)
    dve.wait_ge(*part.now(g, 5))
    dve.tensor_tensor(ve[:, :], st[:, :, 9], st[:, :, 10], ALU.add).then_inc(vs.sem, 1)


def phase_gnn0(nc, A, x, ident, identb, half, maskb, adj, banks):
    with ExitStack() as ctx:
        def sb(name, shape, dt=F32):
            return ctx.enter_context(nc.sbuf_tensor("g0_" + name, shape, dt))

        def sig(name, per=1):
            return Signal(take_semaphore(ctx, nc, "g0_" + name), per)

        wqkv = sb("wqkv", [128, 3 * C])
        wq = sb("wq", [128, 2, 2, 128])
        wk = sb("wk", [128, 2, 2, 128])
        w1 = sb("w1", [128, C])
        w2 = sb("w2", [128, C])
        vecs = sb("vecs", [128, 5, C])
        b1 = sb("b1", [128, 1])
        xn = [sb(f"xn{i}", [128, PG, C]) for i in range(2)]
        mv = sb("mv", [128, PG]); st6 = sb("st6", [128, PG, 11]); ve = sb("ve", [128, PG]); rs = sb("rs", [128, PG])
        mv1 = sb("mv1", [128, PG]); st61 = sb("st61", [128, PG, 11]); ve1 = sb("ve1", [128, PG]); rs1 = sb("rs1", [128, PG])
        mv2 = sb("mv2", [128, PG]); st62 = sb("st62", [128, PG, 11]); ve2 = sb("ve2", [128, PG]); rs2 = sb("rs2", [128, PG])
        xT = sb("xT", [128, GT])
        q = sb("q", [128, 2, PG, 2, NODES])
        k = sb("k", [128, 2, PG, 4, NODES])
        v = sb("v", [128, 2 * PG, 4, 2, D0 + 1])
        s = sb("s", [128, 2, H0, NODES])
        mx = sb("mx", [128, 2, H0])
        pt = sb("pt", [128, 2, 4, 128])
        rc = sb("rc", [128, 2, H0])
        t = sb("t", [128, PG, C])
        y1 = sb("y1", [128, PG, C])
        y1b = sb("y1b", [128, PG, C])
        y1T = sb("y1T", [128, GT])
        hT = sb("hT", [128, GT])
        u = sb("u", [128, PG, C])

        load = take_semaphore(ctx, nc, "g0_load")
        setup = take_semaphore(ctx, nc, "g0_setup")
        bn0, ag0, ve0 = sig("bn0", PG), sig("ag0", 6), sig("ve0")
        bn1, ag1, vs1 = sig("bn1", PG), sig("ag1", 6), sig("vs1")
        bn2, ag2, vs2 = sig("bn2", PG), sig("ag2", 6), sig("vs2")
        xn_ready = sig("xn_ready", PG)
        kd_ready = sig("kd_ready", 2)
        v_ready = sig("v_ready", 2)
        mx_ready = sig("mx_ready", PG)
        s_ready = sig("s_ready", PG)
        rc_ready = sig("rc_ready", PG)
        o_ready = sig("o_ready", PG)
        t_ready = sig("t_ready")
        n1_ready = sig("n1_ready", PG)
        u_ready = sig("u_ready")
        n2_ready = sig("n2_ready", PG)
        dve_signals = [bn0, ag0, ve0, bn1, ag1, vs1, bn2, ag2, vs2, xn_ready, kd_ready, v_ready, mx_ready,
                       s_ready, rc_ready, o_ready, t_ready, n1_ready, u_ready, n2_ready]
        xT_ready, q_ready, ka_ready = sig("xT_ready"), sig("q_ready", 2), sig("ka_ready", 2)
        e_ready, pt_ready = sig("e_ready", PG), sig("pt_ready", PG)
        y1T_ready, hT_ready = sig("y1T_ready"), sig("hT_ready")
        act_signals = [xT_ready, q_ready, ka_ready, e_ready, pt_ready, y1T_ready, hT_ready]
        rs0_ready, rs1_ready, rs2_ready = sig("rs0_ready"), sig("rs1_ready"), sig("rs2_ready")
        y1m, y1_ready, y1b_ready = sig("y1m"), sig("y1_ready"), sig("y1b_ready")
        fin = sig("fin", 3)
        pool_signals = [rs0_ready, rs1_ready, rs2_ready, y1m, y1_ready, y1b_ready, fin]
        pe_xT, pe_q, pe_k, pe_v = sig("pe_xT"), sig("pe_q", 2), sig("pe_k"), sig("pe_v")
        pe_s, pe_pt, pe_o = sig("pe_s", PG), sig("pe_pt", PG), sig("pe_o", PG)
        pe_y1T, pe_h, pe_f = sig("pe_y1T"), sig("pe_h"), sig("pe_f")
        pe_signals = [pe_xT, pe_q, pe_k, pe_v, pe_s, pe_pt, pe_o, pe_y1T, pe_h, pe_f]

        bT, bQ0, bQ1, bV1, bS0, bS1, bPT, bO = banks

        with nc.Block() as block:
            @block.sync
            def _(sp):
                sp.dma_start(wqkv[:, :], A["L0_gnn_w_qkv"]).then_inc(load, 16)
                sp.dma_start(w1[:, :], A["L0_gnn_w1"]).then_inc(load, 16)
                sp.dma_start(w2[:, :], A["L0_gnn_w2"]).then_inc(load, 16)
                for i, name in enumerate(["ln1_g", "ln1_b", "ln2_g", "ln2_b", "b2"]):
                    sp.dma_start(vecs[:, i, :], row_bcast(A["L0_gnn_" + name])).then_inc(load, 16)
                sp.dma_start(b1[:, :], A["L0_gnn_b1"].rearrange("(c a) -> c a", a=1)).then_inc(load, 16)
                sp.wait_ge(load, 16 * 9)

            @block.gpsimd
            def _(pool):
                for i, z in enumerate([wq, wk]):
                    pool.memset(z[:, :, :, :], 0.0).then_inc(setup, 1)
                pool.memset(k[:, :, :, :, :], 0.0).then_inc(setup, 1)
                pool.memset(v[:, :, :, :, :], 0.0).then_inc(setup, 1)
                pool.wait_ge(setup, 4)
                for h2 in range(2):
                    pool.memset(v[64 * h2:64 * h2 + 64, :, :, h2, D0:D0 + 1], 1.0).then_inc(setup, 1)
                    pool.wait_ge(setup, 5 + h2)
                pool.wait_ge(load, 16 * 9)
                for n, w in enumerate([wq, wk]):
                    for j in range(2):
                        for f in range(2):
                            dst = w[:, j, f, :].rearrange("c (h f d) -> c h f d", h=4, f=2)[:, :, f, :]
                            src = wqkv[:, n * C + 64 * j:n * C + 64 * j + 64].rearrange("c (h d) -> c h d", h=4)
                            pool.tensor_copy(dst, src).then_inc(setup, 1)
                open_signals(pool, pool_signals)

            @block.vector
            def _(dve):
                dve.tensor_scalar(maskb[:, :], adj[:, :], 0.0, -4e9, ALU.is_le, ALU.mult)
                open_signals(dve, dve_signals)

            @block.scalar
            def _(act):
                open_signals(act, act_signals)

            @block.tensor
            def _(pe):
                open_signals(pe, pe_signals)

        def xg(g):
            return x[:, bass.ds(g * PG, PG), :]

        with nc.Block() as block:
            @block.tensor
            def _(pe):
                def head(g):
                    pe.wait_ge(*xn_ready.now(g, PG - 1))
                    pe.wait_ge(*y1T_ready.before(g))
                    for p in range(PG):
                        i = pe.transpose(bT[:, 128 * p:128 * p + 128], xn_at(g)[:, p, :], ident[:, :])
                    i.then_inc(pe_xT.sem, 1)
                    xTv = xT[:, :].rearrange("c (p f n) -> c p f n", p=PG, f=2)
                    pe.wait_ge(*xT_ready.now(g))
                    for j, bank in enumerate([bQ0, bQ1]):
                        bv = bank[:, :].rearrange("c (p f n) -> c p f n", p=PG, f=2)
                        pe.wait_ge(*(kd_ready.before(g) if j == 0 else v_ready.before(g)))
                        if j == 0:
                            pe.wait_ge(*ka_ready.before(g))
                        for f in range(2):
                            i = pe.matmul(bv[:, :, f, :], wq[:, j, f, :], xTv[:, :, f, :], start=(f == 0), stop=True,
                                          skip_group_check=True)
                        i.then_inc(pe_q.sem, 1)
                    pe.wait_ge(*q_ready.now(g, 0))
                    kv = bQ0[:, :].rearrange("c (j p n) -> c j p n", j=2, p=PG)
                    for j in range(2):
                        for f in range(2):
                            i = pe.matmul(kv[:, j, :, :], wk[:, j, f, :], xTv[:, :, f, :], start=(f == 0), stop=(f == 1),
                                          skip_group_check=True)
                    i.then_inc(pe_k.sem, 1)
                    pe.wait_ge(*q_ready.now(g, 1))
                    wv = wqkv[:, 2 * C:3 * C].rearrange("c (hp h2 d) -> c hp h2 d", hp=4, h2=2)
                    for fr in range(2 * PG):
                        for h2 in range(2):
                            i = pe.matmul(bQ1[64 * h2:64 * h2 + 64, 64 * fr:64 * fr + 64], xT[:, 64 * fr:64 * fr + 64],
                                          wv[:, :, h2, :], start=(fr == 0), stop=True, skip_group_check=True)
                    i.then_inc(pe_v.sem, 1)

                def scores(g, p):
                    bank = [bS0, bS1][p % 2]
                    pe.wait_ge(*kd_ready.now(g, 1))
                    pe.wait_ge(*ka_ready.now(g, 1))
                    pe.wait_ge(*(s_ready.now(g, p - 2) if p >= 2 else s_ready.before(g, PG - 2 + p)))
                    mk = bass.AP(maskb, 0, [maskb[:, :].ap[0], [0, H0], [1, NODES]])
                    pe.matmul(bank[:, :], identb[:, :], mk, start=True, stop=False, skip_group_check=True)
                    for j in range(2):
                        i = pe.matmul(bank[:, 256 * j:256 * j + 256], q[:, j, p, :, :].rearrange("c f n -> c (f n)"),
                                      k[:, j, p, :, :].rearrange("c h m -> c (h m)"), start=False, stop=True,
                                      skip_group_check=True)
                    i.then_inc(pe_s.sem, 1)

                def probs_T(g, p):
                    pe.wait_ge(*e_ready.now(g, p))
                    pe.wait_ge(*(pt_ready.now(g, p - 1) if p else pt_ready.before(g)))
                    for hp in range(4):
                        i = pe.transpose(bPT[:, 128 * hp:128 * hp + 128],
                                         s[:, p % 2, 2 * hp:2 * hp + 2, :].rearrange("p h m -> p (h m)"), ident[:, :])
                    i.then_inc(pe_pt.sem, 1)

                def mix(g, p):
                    pe.wait_ge(*pt_ready.now(g, p))
                    pe.wait_ge(*v_ready.now(g, 1))
                    pe.wait_ge(*(o_ready.now(g, p - 1) if p else o_ready.before(g)))
                    for f in range(2):
                        for hp in range(4):
                            w = 2 * (D0 + 1)
                            i = pe.matmul(bO[64 * f:64 * f + 64, w * hp:w * hp + w],
                                          pt[:, p % 2, hp, 64 * f:64 * f + 64],
                                          v[:, 2 * p + f, hp, :, :].rearrange("m h d -> m (h d)"),
                                          start=(hp == 0), stop=True, skip_group_check=True)
                    i.then_inc(pe_o.sem, 1)

                def tail_T(g):
                    pe.wait_ge(*y1_ready.now(g))
                    pe.wait_ge(*xT_ready.now(g))
                    for p in range(PG):
                        i = pe.transpose(bT[:, 128 * p:128 * p + 128], y1[:, p, :], ident[:, :])
                    i.then_inc(pe_y1T.sem, 1)

                def tail_1(g):
                    pe.wait_ge(*y1T_ready.now(g))
                    pe.wait_ge(*v_ready.now(g, 1))
                    pe.matmul(bV1[:, :], w1[:, :], y1T[:, :], start=True, stop=True).then_inc(pe_h.sem, 1)

                def tail_2(g):
                    pe.wait_ge(*hT_ready.now(g))
                    for p in range(PG):
                        i = pe.matmul(bV1[:, 128 * p:128 * p + 128], hT[:, 128 * p:128 * p + 128], w2[:, :],
                                      start=(p == 0), stop=True, skip_group_check=True)
                    i.then_inc(pe_f.sem, 1)

                def body(g):
                    head(g)
                    scores(g, 0)
                    scores(g, 1)
                    probs_T(g, 0)
                    mix(g, 0)
                    scores(g, 2)
                    probs_T(g, 1)
                    mix(g, 1)
                    scores(g, 3)
                    probs_T(g, 2)
                    mix(g, 2)
                    probs_T(g, 3)
                    mix(g, 3)
                    tail_T(g)
                    tail_1(g)
                    tail_2(g)

                def xn_at(g):
                    return xn[0]
                turns(pe, 0, GROUPS, body)

            @block.scalar
            def _(act):
                def body(g):
                    act.wait_ge(*pe_xT.now(g))
                    act.activation(xT[:, :], bT[:, :], ACT.Copy).then_inc(xT_ready.sem, 1)
                    for j, bank in enumerate([bQ0, bQ1]):
                        act.wait_ge(*pe_q.now(g, j))
                        act.wait_ge(*pe_s.before(g))
                        act.activation(q[:, j, :, :, :].rearrange("c p f n -> c (p f n)"), bank[:, :], ACT.Copy)\
                           .then_inc(q_ready.sem, 1)
                    kv = bQ0[:, :].rearrange("c (j p n) -> c j p n", j=2, p=PG)
                    act.wait_ge(*kd_ready.now(g, 1))
                    for h4 in (2, 3):
                        r = slice(32 * h4, 32 * h4 + 32)
                        act.activation(k[r, :, :, h4, :], kv[r, :, :, :], ACT.Copy).then_inc(ka_ready.sem, 1)
                    for p in range(PG):
                        act.wait_ge(*s_ready.now(g, p))
                        act.activation(s[:, p % 2, :, :], s[:, p % 2, :, :], ACT.Exp, scale=0.25)\
                           .then_inc(e_ready.sem, 1)
                        act.wait_ge(*pe_pt.now(g, p))
                        act.wait_ge(*(pe_o.now(g, p - 2) if p >= 2 else pe_o.before(g, PG - 2 + p)))
                        act.activation(pt[:, p % 2, :, :].rearrange("m h n -> m (h n)"), bPT[:, :], ACT.Copy)\
                           .then_inc(pt_ready.sem, 1)
                    act.wait_ge(*pe_y1T.now(g))
                    act.activation(y1T[:, :], bT[:, :], ACT.Copy).then_inc(y1T_ready.sem, 1)
                    act.wait_ge(*pe_h.now(g))
                    act.wait_ge(*pe_f.before(g))
                    act.activation(hT[:, :], bV1[:, :], ACT.Relu, bias=b1[:, 0:1]).then_inc(hT_ready.sem, 1)
                turns(act, 0, GROUPS, body)

            @block.vector
            def _(dve):
                def body(g):
                    norm_stats(dve, lambda p: x[:, bass.ds(g * PG + p, 1), :].rearrange("p a c -> p (a c)"),
                               st6, mv, ve, bn0, ag0, ve0, g, EPS_LN, [rs0_ready.before(g)])
                    dve.wait_ge(*rs0_ready.now(g))
                    dve.wait_ge(*pe_xT.before(g))
                    dve.wait_ge(*t_ready.before(g))
                    for p in range(PG):
                        dve.tensor_scalar(xn[0][:, p, :], x[:, bass.ds(g * PG + p, 1), :].rearrange("p a c -> p (a c)"),
                                          mv[:, p:p + 1], rs[:, p:p + 1], ALU.subtract, ALU.mult).then_inc(xn_ready.sem, 1)
                    kv = bQ0[:, :].rearrange("c (j p n) -> c j p n", j=2, p=PG)
                    dve.wait_ge(*pe_k.now(g))
                    dve.wait_ge(*pe_s.before(g))
                    for h4 in (0, 1):
                        r = slice(32 * h4, 32 * h4 + 32)
                        dve.tensor_copy(k[r, :, :, h4, :], kv[r, :, :, :]).then_inc(kd_ready.sem, 1)
                    dve.wait_ge(*pe_o.before(g))
                    dve.wait_ge(*pe_v.now(g))
                    bv = bQ1[:, :].rearrange("m (f hp d) -> m f hp d", f=2 * PG, hp=4)
                    for h2 in range(2):
                        r = slice(64 * h2, 64 * h2 + 64)
                        dve.tensor_copy(v[r, :, :, h2, 0:D0], bv[r, :, :, :]).then_inc(v_ready.sem, 1)

                    def soft(p):
                        bank = [bS0, bS1][p % 2]
                        bv = bank[:, :].rearrange("p (h m) -> p h m", h=H0)
                        dve.wait_ge(*pe_s.now(g, p))
                        dve.wait_ge(*(s_ready.now(g, p - 2) if p >= 2 else s_ready.before(g, PG - 2 + p)))
                        dve.tensor_reduce(mx[:, p % 2, :], bv, AX.X, ALU.max).then_inc(mx_ready.sem, 1)
                        dve.wait_ge(*mx_ready.now(g, p))
                        dve.wait_ge(*(pe_pt.now(g, p - 2) if p >= 2 else pe_pt.before(g, PG - 2 + p)))
                        m = mx[:, p % 2, :]
                        dve.tensor_tensor(s[:, p % 2, :, :], bv, bass.AP(m.tensor, m.offset, [m.ap[0], [1, H0], [0, NODES]]),
                                          ALU.subtract).then_inc(s_ready.sem, 1)

                    def norm(p):
                        bv = bO[:, 0:H0 * (D0 + 1)].rearrange("n (h d) -> n h d", h=H0)
                        dve.wait_ge(*pe_o.now(g, p))
                        dve.wait_ge(*(o_ready.now(g, p - 2) if p >= 2 else o_ready.before(g, PG - 2 + p)))
                        dve.reciprocal(rc[:, p % 2, :], bv[:, :, D0]).then_inc(rc_ready.sem, 1)
                        dve.wait_ge(*rc_ready.now(g, p))
                        if p == 0:
                            dve.wait_ge(*n1_ready.before(g))
                        m = rc[:, p % 2, :]
                        dve.tensor_tensor(t[:, p, :].rearrange("n (h d) -> n h d", h=H0), bv[:, :, 0:D0],
                                          bass.AP(m.tensor, m.offset, [m.ap[0], [1, H0], [0, D0]]), ALU.mult)\
                           .then_inc(o_ready.sem, 1)

                    soft(0)
                    soft(1)
                    norm(0)
                    soft(2)
                    norm(1)
                    soft(3)
                    norm(2)
                    norm(3)
                    dve.wait_ge(*o_ready.now(g, PG - 1))
                    dve.tensor_tensor(t[:, :, :], t[:, :, :], xn[0][:, :, :], ALU.add).then_inc(t_ready.sem, 1)
                    norm_stats(dve, lambda p: t[:, p, :], st61, mv1, ve1, bn1, ag1, vs1, g, EPS_LN,
                               [t_ready.now(g), rs1_ready.before(g)])
                    dve.wait_ge(*rs1_ready.now(g))
                    for p in range(PG):
                        dve.tensor_scalar(t[:, p, :], t[:, p, :], mv1[:, p:p + 1], rs1[:, p:p + 1],
                                          ALU.subtract, ALU.mult).then_inc(n1_ready.sem, 1)
                    dve.wait_ge(*pe_f.now(g))
                    dve.wait_ge(*y1b_ready.now(g))
                    dve.tensor_tensor(u[:, :, :], bV1[:, :].rearrange("p (t c) -> p t c", t=PG), y1b[:, :, :], ALU.add)\
                       .then_inc(u_ready.sem, 1)
                    norm_stats(dve, lambda p: u[:, p, :], st62, mv2, ve2, bn2, ag2, vs2, g, EPS_LN,
                               [u_ready.now(g), rs2_ready.before(g)])
                    dve.wait_ge(*rs2_ready.now(g))
                    for p in range(PG):
                        dve.tensor_scalar(u[:, p, :], u[:, p, :], mv2[:, p:p + 1], rs2[:, p:p + 1],
                                          ALU.subtract, ALU.mult).then_inc(n2_ready.sem, 1)
                turns(dve, 0, GROUPS, body)

            @block.gpsimd
            def _(pool):
                def vec(i):
                    w = vecs[:, i, :]
                    return bass.AP(w.tensor, w.offset, [w.ap[0], [0, PG], [1, C]])

                def body(g):
                    pool.wait_ge(*ve0.now(g))
                    pool.wait_ge(*xn_ready.before(g))
                    pool.tensor_tensor(rs[:, :], ve[:, :], half[:, 0:PG], ALU.pow).then_inc(rs0_ready.sem, 1)
                    pool.wait_ge(*vs1.now(g))
                    pool.tensor_tensor(rs1[:, :], ve1[:, :], half[:, 0:PG], ALU.pow).then_inc(rs1_ready.sem, 1)
                    pool.wait_ge(*n1_ready.now(g, PG - 1))
                    pool.wait_ge(*pe_y1T.before(g))
                    pool.tensor_tensor(y1[:, :, :], t[:, :, :], vec(0), ALU.mult).then_inc(y1m.sem, 1)
                    pool.wait_ge(*y1m.now(g))
                    pool.tensor_tensor(y1[:, :, :], y1[:, :, :], vec(1), ALU.add).then_inc(y1_ready.sem, 1)
                    pool.wait_ge(*y1_ready.now(g))
                    pool.wait_ge(*u_ready.before(g))
                    pool.tensor_tensor(y1b[:, :, :], y1[:, :, :], vec(4), ALU.add).then_inc(y1b_ready.sem, 1)
                    pool.wait_ge(*vs2.now(g))
                    pool.tensor_tensor(rs2[:, :], ve2[:, :], half[:, 0:PG], ALU.pow).then_inc(rs2_ready.sem, 1)
                    pool.wait_ge(*n2_ready.now(g, PG - 1))
                    pool.tensor_tensor(u[:, :, :], u[:, :, :], vec(2), ALU.mult).then_inc(fin.sem, 1)
                    pool.wait_ge(*fin.now(g, 0))
                    pool.tensor_tensor(u[:, :, :], u[:, :, :], vec(3), ALU.add).then_inc(fin.sem, 1)
                    pool.wait_ge(*fin.now(g, 1))
                    pool.tensor_tensor(xg(g), xg(g), u[:, :, :], ALU.add).then_inc(fin.sem, 1)
                turns(pool, 0, GROUPS, body)
        clear_taken(nc)


class Routing:

    def __init__(self, ctx, nc, name, consts, state):
        def sb(n, shape, dt=F32):
            return ctx.enter_context(nc.sbuf_tensor(f"{name}_{n}", shape, dt))

        def sig(n, per=1):
            return Signal(take_semaphore(ctx, nc, f"{name}_{n}"), per)

        self.c, self.state = consts, state
        self.lg = sb("lg", [128, PG, NE])
        self.eq = sb("eq", [128, PG, NE])
        self.m = sb("m", [128, 2, PG])
        self.key = sb("key", [128, 2, PG])
        self.oh = sb("oh", [128, 2, PG, NE])
        self.both = sb("both", [128, PG, NE], BF16)
        self.d = sb("d", [128, PG, NE + 1])
        self.e = sb("e", [128, PG, NE + 1])
        self.z = sb("z", [128, PG])
        self.den = sb("den", [128, PG])
        self.rows = sb("rows", [128, PG + 1, NE])
        self.pick = sb("pick", [128, 2, PG, NE])
        self.posf = sb("posf", [128, 2, PG])
        self.pos = sb("pos", [128, 2, PG], I32)
        self.step = sig("step", 12)
        self.both_ready = sig("both_ready")
        self.d_ready = sig("d_ready", 2)
        self.e_ready = sig("e_ready")
        self.wstep = sig("wstep", 6)
        self.pstep = sig("pstep", 7)
        self.pe_logits = sig("pe_logits")
        self.pe_rank = sig("pe_rank")
        self.gate = sig("gate")
        self.landed = take_semaphore(ctx, nc, f"{name}_landed")
        self.scattered = sig("scattered")
        self.dve_signals = [self.step, self.both_ready, self.d_ready, self.wstep, self.pstep]
        self.act_signals = [self.e_ready]
        self.pe_signals = [self.pe_logits, self.pe_rank]
        self.pool_signals = [self.scattered]

    def tensor_logits(self, pe, g, bank, flatT, wr):
        for p in range(PG):
            i = pe.matmul(bank[:, NE * p:NE * p + NE], flatT[:, 128 * p:128 * p + 128], wr[:, :],
                          start=(p == 0), stop=True, skip_group_check=True)
        i.then_inc(self.pe_logits.sem, 1)

    def tensor_rank(self, pe, g, bank):
        pe.wait_ge(*self.both_ready.now(g))
        pe.wait_ge(*self.step.now(g, 0))
        r = bank[:, 64:64 + NE * (PG + 1)]
        pe.matmul(r[:, 0:NE * PG], self.c["tri"][:, :], self.both[:, :, :].rearrange("t p e -> t (p e)"),
                  start=True, stop=False, skip_group_check=True)
        for q in range(PG):
            m = self.both[:, q, :]
            i = pe.matmul(r[:, NE * (q + 1):NE * (PG + 1)], self.c["ones"][:, :],
                          bass.AP(m.tensor, m.offset, [m.ap[0], [0, PG - q], [1, NE]]),
                          start=False, stop=(q == PG - 1), skip_group_check=True)
        i.then_inc(self.pe_rank.sem, 1)

    def vector_choose(self, dve, g, bank, with_z):
        c = self.c

        def over_e(ap):
            return bass.AP(ap.tensor, ap.offset, [ap.ap[0], [1, PG], [0, NE]])

        rev = bass.AP(c["rev"], 0, [c["rev"][:, :].ap[0], [0, PG], [1, NE]])
        s = self.step
        dve.wait_ge(*self.pe_logits.now(g))
        dve.wait_ge(*self.wstep.before(g))
        bv = bank[:, 0:NE * PG].rearrange("t (p e) -> t p e", p=PG)
        if self.state.get("bias") is not None:
            b = self.state["bias"]
            dve.tensor_tensor(self.lg[:, :, :], bv, bass.AP(b, 0, [b[:, :].ap[0], [0, PG], [1, NE]]), ALU.add)\
               .then_inc(s.sem, 1)
        else:
            dve.tensor_copy(self.lg[:, :, :], bv).then_inc(s.sem, 1)
        src = self.lg[:, :, :]
        n = 1
        for k in range(2):
            dve.wait_ge(*s.now(g, n - 1))
            dve.tensor_reduce(self.m[:, k, :], src, AX.X, ALU.max).then_inc(s.sem, 1)
            dve.wait_ge(*s.now(g, n))
            dve.tensor_tensor(self.eq[:, :, :], src, over_e(self.m[:, k, :]), ALU.is_equal).then_inc(s.sem, 1)
            dve.wait_ge(*s.now(g, n + 1))
            dve.tensor_tensor(self.eq[:, :, :], self.eq[:, :, :], rev, ALU.mult).then_inc(s.sem, 1)
            dve.wait_ge(*s.now(g, n + 2))
            dve.tensor_reduce(self.key[:, k, :], self.eq[:, :, :], AX.X, ALU.max).then_inc(s.sem, 1)
            dve.wait_ge(*s.now(g, n + 3))
            if k == 0:
                dve.wait_ge(*self.pstep.before(g))
            dve.tensor_tensor(self.oh[:, k, :, :], rev, over_e(self.key[:, k, :]), ALU.is_equal).then_inc(s.sem, 1)
            n += 5
            if k == 0:
                dve.wait_ge(*s.now(g, n - 1))
                dve.scalar_tensor_tensor(out=self.eq[:, :, :].rearrange("t p e -> t (p e)"),
                                         in0=self.oh[:, 0, :, :].rearrange("t p e -> t (p e)"), scalar=-1e30,
                                         in1=self.lg[:, :, :].rearrange("t p e -> t (p e)"),
                                         op0=ALU.mult, op1=ALU.add).then_inc(s.sem, 1)
                n += 1
                src = self.eq[:, :, :]
        dve.wait_ge(*s.now(g, n - 1))
        dve.wait_ge(*self.pe_rank.before(g))
        dve.tensor_tensor(self.both[:, :, :], self.oh[:, 0, :, :], self.oh[:, 1, :, :], ALU.add)\
           .then_inc(self.both_ready.sem, 1)
        dve.wait_ge(*self.e_ready.before(g))
        dve.tensor_tensor(self.d[:, :, NE], self.m[:, 1, :], self.m[:, 0, :], ALU.subtract).then_inc(self.d_ready.sem, 1)
        if with_z:
            dve.tensor_tensor(self.d[:, :, 0:NE], self.lg[:, :, :], over_e(self.m[:, 0, :]), ALU.subtract)\
               .then_inc(self.d_ready.sem, 1)
        else:
            dve.tensor_copy(self.d[:, :, 0:NE], self.lg[:, :, :]).then_inc(self.d_ready.sem, 1)

    def scalar_exp(self, act, g, with_z):
        act.wait_ge(*self.d_ready.now(g, 1))
        act.wait_ge(*self.wstep.before(g))
        lo = 0 if with_z else NE
        act.activation(self.e[:, :, lo:NE + 1], self.d[:, :, lo:NE + 1], ACT.Exp).then_inc(self.e_ready.sem, 1)

    def vector_weights(self, dve, g, with_z):
        w = self.state["w"]
        s = self.wstep
        dve.wait_ge(*self.e_ready.now(g))
        e2 = self.e[:, :, NE]
        if with_z:
            dve.tensor_reduce(self.z[:, :], self.e[:, :, 0:NE], AX.X, ALU.add).then_inc(s.sem, 1)
            dve.wait_ge(*s.now(g, 0))
            dve.scalar_tensor_tensor(out=self.den[:, :], in0=self.z[:, :], scalar=1e-9, in1=e2,
                                     op0=ALU.mult, op1=ALU.add).then_inc(s.sem, 1)
        else:
            dve.tensor_copy(self.z[:, :], e2).then_inc(s.sem, 1)
            dve.wait_ge(*s.now(g, 0))
            dve.tensor_copy(self.den[:, :], self.z[:, :]).then_inc(s.sem, 1)
        dve.wait_ge(*s.now(g, 1))
        dve.tensor_scalar(self.den[:, :], self.den[:, :], 1.0, None, ALU.add).then_inc(s.sem, 1)
        dve.wait_ge(*s.now(g, 2))
        dve.reciprocal(self.z[:, :], self.den[:, :]).then_inc(s.sem, 1)
        dve.wait_ge(*s.now(g, 3))
        dve.tensor_copy(w[:, 0, bass.ds(g * PG, PG)], self.z[:, :]).then_inc(s.sem, 1)
        dve.tensor_tensor(w[:, 1, bass.ds(g * PG, PG)], self.z[:, :], e2, ALU.mult).then_inc(s.sem, 1)

    def vector_rows(self, dve, g, bank):
        base, posf = self.state["base"], self.state["posf"]
        s = self.pstep
        dve.wait_ge(*self.pe_rank.now(g))
        dve.wait_ge(*s.before(g))
        b = base[:, :]
        dve.tensor_tensor(self.rows[:, :, :], bank[:, 64:64 + NE * (PG + 1)].rearrange("t (p e) -> t p e", e=NE),
                          bass.AP(b.tensor, b.offset, [b.ap[0], [0, PG + 1], [1, NE]]), ALU.add).then_inc(s.sem, 1)
        dve.wait_ge(*s.now(g, 0))
        dve.tensor_copy(base[:, :], self.rows[:, PG, :]).then_inc(s.sem, 1)
        for k in range(2):
            dve.tensor_tensor(self.pick[:, k, :, :], self.oh[:, k, :, :], self.rows[:, 0:PG, :], ALU.mult).then_inc(s.sem, 1)
        dve.wait_ge(*s.now(g, 3))
        dve.tensor_reduce(self.posf[:, :, :], self.pick[:, :, :, :], AX.X, ALU.add).then_inc(s.sem, 1)
        dve.wait_ge(*s.now(g, 4))
        dve.wait_ge(*self.scattered.before(g))
        dve.tensor_copy(self.pos[:, :, :], self.posf[:, :, :]).then_inc(s.sem, 1)
        dve.tensor_copy(posf[:, :, bass.ds(g * PG, PG)], self.posf[:, :, :]).then_inc(s.sem, 1)

    def pool_scatter(self, pool, g, flat, dest):
        pool.wait_ge(*self.pstep.now(g, 5))
        pool.sem_inc(self.gate.sem, 1)
        for p in range(PG):
            for k in range(2):
                pool.indirect_dma_start(out=dest, out_offset=bass.IndirectOffsetOnAxis(ap=self.pos[:, k, p:p + 1], axis=0),
                                        in_=flat[:, p, :], in_offset=None).then_inc(self.landed, 16)
        pool.wait_ge(self.landed, (g + 1) * (16 * 2 * PG))
        pool.sem_inc(self.scattered.sem, 1)


def phase_attn1(nc, A, x, banks, c, state, dest):
    ident, identb, half = c["ident"], c["identb"], c["half"]
    with ExitStack() as ctx:
        def sb(name, shape, dt=F32):
            return ctx.enter_context(nc.sbuf_tensor("a1_" + name, shape, dt))

        def sig(name, per=1):
            return Signal(take_semaphore(ctx, nc, "a1_" + name), per)

        FR = 2 * PG
        wq = sb("wq", [128, 2, 128])
        wk = sb("wk", [128, 2, 128])
        wv = sb("wv", [128, 64])
        wo = sb("wo", [128, 128])
        wr = sb("wr", [128, NE])
        lnw = sb("lnw", [128, 1])
        ln2w = sb("ln2w", [128, C])
        rope = sb("rope", [128, 2, NODES])
        causal = sb("causal", [128, NODES], BF16)
        causal32 = sb("causal32", [128, NODES])
        st = sb("st", [128, PG, 11]); mean = sb("mean", [128, PG]); ve = sb("ve", [128, PG]); rs = sb("rs", [128, PG])
        rr = sb("rr", [128, 4, PG])
        ms = sb("ms", [128, 3, PG])
        vn = sb("vn", [128, PG, C])
        h = sb("h", [128, PG, C])
        hT = sb("hT", [128, GT])
        q1, q2, q = sb("q1", [128, FR, NODES]), sb("q2", [128, FR, NODES]), sb("q", [128, FR, NODES])
        k1, k2 = sb("k1", [128, FR, NODES]), sb("k2", [128, FR, NODES])
        k = sb("k", [128, FR, H1, NODES])
        v = sb("v", [128, FR, KV1, 2, D1 + 1])
        s = sb("s", [128, 2, 2, H1, NODES])
        mx = sb("mx", [128, 2, 2, H1])
        pt = sb("pt", [128, 2, 2, KV1, 128])
        rc = sb("rc", [128, 2, 2, H1])
        y = sb("y", [128, PG, C])
        yT = sb("yT", [128, GT])
        x2 = sb("x2", [128, PG, C])
        sq = sb("sq", [128, PG, C])
        flat = sb("flat", [128, PG, C])
        fT = sb("fT", [128, GT])
        load = take_semaphore(ctx, nc, "a1_load")
        setup = take_semaphore(ctx, nc, "a1_setup")
        R = Routing(ctx, nc, "a1r", c, state)

        bn, part, vs = sig("bn", PG), sig("part", 6), sig("vs")
        vn_ready, h_ready = sig("vn_ready", PG), sig("h_ready", PG)
        rms_in = sig("rms_in", 3)
        rope_q, rope_k = sig("rope_q", 2), sig("rope_k", 2)
        q_ready, kd_ready = sig("q_ready"), sig("kd_ready", 2)
        mx_ready, s_ready = sig("mx_ready", 2), sig("s_ready", 2)
        rc_ready, y_ready = sig("rc_ready", 2), sig("y_ready", 2)
        x2_ready, ms_ready = sig("x2_ready"), sig("ms_ready", 2)
        f0_ready, flat_ready = sig("f0_ready", PG), sig("flat_ready")
        dve_signals = [bn, part, vs, vn_ready, h_ready, rms_in, rope_q, rope_k, q_ready, kd_ready, mx_ready, s_ready,
                       rc_ready, y_ready, x2_ready, ms_ready, f0_ready, flat_ready] + R.dve_signals
        hT_ready, v_ready, e_ready, pt_ready = sig("hT_ready"), sig("v_ready", 2), sig("e_ready", 2), sig("pt_ready", 2)
        yT_ready, fT_ready = sig("yT_ready"), sig("fT_ready")
        act_signals = [hT_ready, v_ready, e_ready, pt_ready, yT_ready, fT_ready] + R.act_signals
        rs_ready, r2_ready, rh_ready = sig("rs_ready"), sig("r2_ready"), sig("rh_ready")
        kp_ready, sq_ready, rms2_ready, fin = sig("kp_ready", 2), sig("sq_ready"), sig("rms2_ready"), sig("fin")
        pool_signals = [rs_ready, r2_ready, rh_ready, kp_ready, sq_ready, rms2_ready, fin]
        pe_hT, pe_q, pe_k, pe_v = sig("pe_hT"), sig("pe_q"), sig("pe_k"), sig("pe_v")
        pe_s, pe_pt, pe_o = sig("pe_s", 2), sig("pe_pt", 2), sig("pe_o", 2)
        pe_yT, pe_x, pe_fT = sig("pe_yT"), sig("pe_x"), sig("pe_fT")
        pe_signals = [pe_hT, pe_q, pe_k, pe_v, pe_s, pe_pt, pe_o, pe_yT, pe_x, pe_fT] + R.pe_signals
        bT, bQ, bQr, bK, bKr, bV, bR, bPT = banks
        S_BANKS = [bQ, bQr]
        PT_BANKS = [bPT, bK]
        bO = bKr

        with nc.Block() as block:
            @block.sync
            def _(sp):
                n = 0
                for i, t in enumerate(["c_wq", "c_wq_x"]):
                    sp.dma_start(wq[:, i, :], A[t]).then_inc(load, 16)
                for i, t in enumerate(["c_wk", "c_wk_x"]):
                    sp.dma_start(wk[:, i, :], A[t]).then_inc(load, 16)
                sp.dma_start(wv[:, :], A["c_wv"]).then_inc(load, 16)
                sp.dma_start(wo[:, :], A["c_wo"]).then_inc(load, 16)
                sp.dma_start(wr[:, :], A["c_wr"]).then_inc(load, 16)
                sp.dma_start(lnw[:, :], A["L0_ffn_ln1_w"].rearrange("(c a) -> c a", a=1)).then_inc(load, 16)
                sp.dma_start(ln2w[:, :], row_bcast(A["L0_ffn_ln2_w"])).then_inc(load, 16)
                sp.dma_start(rope[:, :, :], A["c_rope"]).then_inc(load, 16)
                sp.dma_start(causal32[:, :], A["c_causal"]).then_inc(load, 16)
                sp.wait_ge(load, 16 * 11)

            @block.gpsimd
            def _(pool):
                pool.memset(k[:, :, :, :], 0.0).then_inc(setup, 1)
                pool.memset(v[:, :, :, :, :], 0.0).then_inc(setup, 1)
                pool.wait_ge(setup, 2)
                for h2 in range(2):
                    pool.memset(v[64 * h2:64 * h2 + 64, :, :, h2, D1:D1 + 1], 1.0).then_inc(setup, 1)
                    pool.wait_ge(setup, 3 + h2)
                open_signals(pool, pool_signals)
                open_signals(pool, R.pool_signals)

            @block.vector
            def _(dve):
                dve.wait_ge(load, 16 * 11)
                dve.tensor_copy(causal[:, :], causal32[:, :])
                dve.wait_ge(load, 16 * 11)
                for w in [wq[:, :, :], wk[:, :, :], wv[:, :]]:
                    dve.tensor_scalar(w, w, lnw[:, 0:1], None, ALU.mult)
                dve.tensor_scalar(state["base"][:, :], c["rev"][:, :], -float(CAP), float(NE * CAP), ALU.mult, ALU.add)
                open_signals(dve, dve_signals)

            @block.scalar
            def _(act):
                open_signals(act, act_signals)

            @block.tensor
            def _(pe):
                open_signals(pe, pe_signals)

        def xt(g, p):
            return x[:, bass.ds(g * PG + p, 1), :].rearrange("p a c -> p (a c)")

        with nc.Block() as block:
            @block.tensor
            def _(pe):
                def body(g):
                    pe.wait_ge(*h_ready.now(g, PG - 1))
                    pe.wait_ge(*fT_ready.before(g))
                    for p in range(PG):
                        i = pe.transpose(bT[:, 128 * p:128 * p + 128], h[:, p, :], ident[:, :])
                    i.then_inc(pe_hT.sem, 1)
                    pe.wait_ge(*hT_ready.now(g))
                    pe.wait_ge(*s_ready.before(g))
                    for n, bank in enumerate([bQ, bQr]):
                        i = pe.matmul(bank[:, :], wq[:, n, :], hT[:, :], start=True, stop=True)
                    i.then_inc(pe_q.sem, 1)
                    pe.wait_ge(*pt_ready.before(g))
                    pe.wait_ge(*y_ready.before(g))
                    for n, bank in enumerate([bK, bKr]):
                        i = pe.matmul(bank[:, :], wk[:, n, :], hT[:, :], start=True, stop=True)
                    i.then_inc(pe_k.sem, 1)
                    pe.wait_ge(*x2_ready.before(g))
                    for fr in range(FR):
                        for h2 in range(2):
                            i = pe.matmul(bV[64 * h2:64 * h2 + 64, 64 * fr:64 * fr + 64], hT[:, 64 * fr:64 * fr + 64],
                                          wv[:, :], start=(fr == 0), stop=True, skip_group_check=True)
                    i.then_inc(pe_v.sem, 1)
                    pe.wait_ge(*kd_ready.now(g, 1))
                    pe.wait_ge(*kp_ready.now(g, 1))
                    pe.wait_ge(*q_ready.now(g))
                    for u in range(2):
                        mk = bass.AP(causal, 0, [causal[:, :].ap[0], [0, 2 * H1], [1, NODES]])
                        pe.matmul(S_BANKS[u][:, :], identb[:, :], mk, start=True, stop=False, skip_group_check=True)
                        for fr in range(4):
                            f, pr = fr % 2, fr // 2
                            i = pe.matmul(S_BANKS[u][64 * f:64 * f + 64, 256 * pr:256 * pr + 256], q[:, 4 * u + fr, :],
                                          k[:, 4 * u + fr, :, :].rearrange("c h m -> c (h m)"), start=False, stop=True,
                                          skip_group_check=True)
                        i.then_inc(pe_s.sem, 1)
                    pe.wait_ge(*v_ready.now(g, 1))
                    for u in range(2):
                        pe.wait_ge(*e_ready.now(g, u))
                        for pr in range(2):
                            for kv in range(KV1):
                                n = 2 * pr + kv
                                i = pe.transpose(PT_BANKS[u][:, 128 * n:128 * n + 128],
                                                 s[:, u, pr, 2 * kv:2 * kv + 2, :].rearrange("n h m -> n (h m)"), ident[:, :])
                        i.then_inc(pe_pt.sem, 1)
                    for u in range(2):
                        pe.wait_ge(*pt_ready.now(g, u))
                        if u == 1:
                            pe.wait_ge(*y_ready.now(g, 0))
                        w = 2 * (D1 + 1)
                        for pr in range(2):
                            for kv in range(KV1):
                                for f in range(2):
                                    o = w * (KV1 * pr + kv)
                                    i = pe.matmul(bO[64 * f:64 * f + 64, o:o + w], pt[:, u, pr, kv, 64 * f:64 * f + 64],
                                                  v[:, 4 * u + 2 * pr + f, kv, :, :].rearrange("m h d -> m (h d)"),
                                                  start=(pr == 0 and kv == 0), stop=True, skip_group_check=True)
                        i.then_inc(pe_o.sem, 1)
                    pe.wait_ge(*y_ready.now(g, 1))
                    for p in range(PG):
                        i = pe.transpose(bT[:, 128 * p:128 * p + 128], y[:, p, :], ident[:, :])
                    i.then_inc(pe_yT.sem, 1)
                    pe.wait_ge(*yT_ready.now(g))
                    for p in range(PG):
                        i = pe.matmul(bV[:, 128 * p:128 * p + 128], yT[:, 128 * p:128 * p + 128], wo[:, :],
                                      start=(p == 0), stop=True, skip_group_check=True)
                    i.then_inc(pe_x.sem, 1)
                    pe.wait_ge(*flat_ready.now(g))
                    for p in range(PG):
                        i = pe.transpose(bT[:, 128 * p:128 * p + 128], flat[:, p, :], ident[:, :])
                    i.then_inc(pe_fT.sem, 1)
                    pe.wait_ge(*fT_ready.now(g))
                    pe.wait_ge(*R.pstep.before(g, 0))
                    R.tensor_logits(pe, g, bR, fT, wr)
                    R.tensor_rank(pe, g, bR)
                turns(pe, 0, GROUPS, body)

            @block.scalar
            def _(act):
                def body(g):
                    act.wait_ge(*pe_hT.now(g))
                    act.activation(hT[:, :], bT[:, :], ACT.Copy).then_inc(hT_ready.sem, 1)
                    act.wait_ge(*pe_v.now(g))
                    act.wait_ge(*pe_o.before(g))
                    bv = bV[:, :].rearrange("m (f kv d) -> m f kv d", f=FR, kv=KV1)
                    for h2 in range(2):
                        r = slice(64 * h2, 64 * h2 + 64)
                        act.activation(v[r, :, :, h2, 0:D1], bv[r, :, :, :], ACT.Copy).then_inc(v_ready.sem, 1)
                    for u in range(2):
                        act.wait_ge(*s_ready.now(g, u))
                        su = s[:, u, :, :, :].rearrange("n p h m -> n (p h m)")
                        act.activation(su, su, ACT.Exp, scale=float(D1) ** -0.5).then_inc(e_ready.sem, 1)
                    for u in range(2):
                        act.wait_ge(*pe_pt.now(g, u))
                        act.wait_ge(*pe_o.before(g, u))
                        act.activation(pt[:, u, :, :, :].rearrange("m p k n -> m (p k n)"), PT_BANKS[u][:, :], ACT.Copy)\
                           .then_inc(pt_ready.sem, 1)
                    act.wait_ge(*pe_yT.now(g))
                    act.wait_ge(*pe_x.before(g))
                    act.activation(yT[:, :], bT[:, :], ACT.Copy).then_inc(yT_ready.sem, 1)
                    act.wait_ge(*pe_fT.now(g))
                    act.wait_ge(*R.pe_logits.before(g))
                    act.activation(fT[:, :], bT[:, :], ACT.Copy).then_inc(fT_ready.sem, 1)
                    R.scalar_exp(act, g, True)
                turns(act, 0, GROUPS, body)

            @block.vector
            def _(dve):
                def table(i, rows=slice(0, 128), n=FR):
                    t = rope[rows, i, :]
                    return bass.AP(t.tensor, t.offset, [t.ap[0], [0, n], [1, NODES]])

                def fview(bank):
                    return bank[:, :].rearrange("c (f n) -> c f n", f=FR)

                def body(g):
                    norm_stats(dve, lambda p: xt(g, p), st, mean, ve, bn, part, vs, g, EPS_LN,
                               [rs_ready.before(g), rms_in.before(g)])
                    dve.wait_ge(*rs_ready.now(g))
                    dve.wait_ge(*x2_ready.before(g))
                    for p in range(PG):
                        dve.tensor_scalar(vn[:, p, :], xt(g, p), mean[:, p:p + 1], rs[:, p:p + 1],
                                          ALU.subtract, ALU.mult).then_inc(vn_ready.sem, 1)
                    dve.wait_ge(*vs.now(g))
                    dve.tensor_tensor(rr[:, 0, :], rs[:, :], rs[:, :], ALU.mult).then_inc(rms_in.sem, 1)
                    dve.wait_ge(*rms_in.now(g, 0))
                    dve.scalar_tensor_tensor(out=rr[:, 1, :], in0=ve[:, :], scalar=-EPS_LN, in1=rr[:, 0, :],
                                             op0=ALU.add, op1=ALU.mult).then_inc(rms_in.sem, 1)
                    dve.wait_ge(*rms_in.now(g, 1))
                    dve.wait_ge(*rh_ready.before(g))
                    dve.tensor_scalar(rr[:, 2, :], rr[:, 1, :], EPS_RMS, None, ALU.add).then_inc(rms_in.sem, 1)
                    dve.wait_ge(*rh_ready.now(g))
                    dve.wait_ge(*vn_ready.now(g, PG - 1))
                    dve.wait_ge(*pe_hT.before(g))
                    for p in range(PG):
                        dve.tensor_scalar(h[:, p, :], vn[:, p, :], rr[:, 3, p:p + 1], None, ALU.mult).then_inc(h_ready.sem, 1)
                    dve.wait_ge(*pe_q.now(g))
                    dve.wait_ge(*q_ready.before(g))
                    dve.tensor_tensor(q1[:, :, :], fview(bQ), table(0), ALU.mult).then_inc(rope_q.sem, 1)
                    dve.tensor_tensor(q2[:, :, :], fview(bQr), table(1), ALU.mult).then_inc(rope_q.sem, 1)
                    dve.wait_ge(*pe_k.now(g))
                    dve.wait_ge(*kd_ready.before(g))
                    dve.wait_ge(*kp_ready.before(g))
                    dve.tensor_tensor(k1[:, :, :], fview(bK), table(0), ALU.mult).then_inc(rope_k.sem, 1)
                    dve.tensor_tensor(k2[:, :, :], fview(bKr), table(1), ALU.mult).then_inc(rope_k.sem, 1)
                    dve.wait_ge(*rope_q.now(g, 1))
                    dve.wait_ge(*pe_s.before(g))
                    dve.tensor_tensor(q[:, :, :], q1[:, :, :], q2[:, :, :], ALU.add).then_inc(q_ready.sem, 1)
                    dve.wait_ge(*rope_k.now(g, 1))
                    for h4 in (0, 1):
                        r = slice(32 * h4, 32 * h4 + 32)
                        dve.tensor_tensor(k[r, :, h4, :], k1[r, :, :], k2[r, :, :], ALU.add).then_inc(kd_ready.sem, 1)
                    for u in range(2):
                        sv = S_BANKS[u][:, :].rearrange("n (h m) -> n h m", m=NODES)
                        m = mx[:, u, :, :].rearrange("n p h -> n (p h)")
                        dve.wait_ge(*pe_s.now(g, u))
                        dve.wait_ge(*s_ready.before(g, u))
                        dve.tensor_reduce(m, sv, AX.X, ALU.max).then_inc(mx_ready.sem, 1)
                        dve.wait_ge(*mx_ready.now(g, u))
                        dve.wait_ge(*pe_pt.before(g, u))
                        dve.tensor_tensor(s[:, u, :, :, :].rearrange("n p h m -> n (p h) m"), sv,
                                          bass.AP(m.tensor, m.offset, [m.ap[0], [1, 2 * H1], [0, NODES]]), ALU.subtract)\
                           .then_inc(s_ready.sem, 1)
                    for u in range(2):
                        ov = bO[:, 0:2 * H1 * (D1 + 1)].rearrange("n (h d) -> n h d", d=D1 + 1)
                        m = rc[:, u, :, :].rearrange("n p h -> n (p h)")
                        dve.wait_ge(*pe_o.now(g, u))
                        dve.wait_ge(*y_ready.before(g, u))
                        dve.reciprocal(m, ov[:, :, D1]).then_inc(rc_ready.sem, 1)
                        dve.wait_ge(*rc_ready.now(g, u))
                        dve.wait_ge(*pe_yT.before(g))
                        dve.tensor_tensor(y[:, 2 * u:2 * u + 2, :].rearrange("n p (h d) -> n (p h) d", h=H1), ov[:, :, 0:D1],
                                          bass.AP(m.tensor, m.offset, [m.ap[0], [1, 2 * H1], [0, D1]]), ALU.mult)\
                           .then_inc(y_ready.sem, 1)
                    dve.wait_ge(*pe_x.now(g))
                    dve.wait_ge(*fin.before(g))
                    dve.wait_ge(*f0_ready.before(g))
                    dve.tensor_tensor(x2[:, :, :], bV[:, :].rearrange("n (p c) -> n p c", p=PG), vn[:, :, :], ALU.add)\
                       .then_inc(x2_ready.sem, 1)
                    dve.wait_ge(*sq_ready.now(g))
                    dve.wait_ge(*rms2_ready.before(g))
                    dve.tensor_reduce(ms[:, 0, :], sq[:, :, :], AX.X, ALU.add).then_inc(ms_ready.sem, 1)
                    dve.wait_ge(*ms_ready.now(g, 0))
                    dve.tensor_scalar(ms[:, 1, :], ms[:, 0, :], 1.0 / C, EPS_RMS, ALU.mult, ALU.add).then_inc(ms_ready.sem, 1)
                    dve.wait_ge(*rms2_ready.now(g))
                    dve.wait_ge(*pe_fT.before(g))
                    dve.wait_ge(*R.scattered.before(g))
                    w = ln2w[:, :]
                    for p in range(PG):
                        dve.scalar_tensor_tensor(out=flat[:, p, :], in0=x2[:, p, :], scalar=ms[:, 2, p:p + 1], in1=w,
                                                 op0=ALU.mult, op1=ALU.mult).then_inc(f0_ready.sem, 1)
                    dve.wait_ge(*f0_ready.now(g, PG - 1))
                    dve.tensor_copy(ms[:, 1, 0:1], ms[:, 0, 0:1]).then_inc(flat_ready.sem, 1)
                    R.vector_choose(dve, g, bR, True)
                    R.vector_rows(dve, g, bR)
                    R.vector_weights(dve, g, True)
                turns(dve, 0, GROUPS, body)

            @block.gpsimd
            def _(pool):
                def body(g):
                    pool.wait_ge(*vs.now(g))
                    pool.wait_ge(*vn_ready.before(g))
                    pool.wait_ge(*rms_in.before(g, 0))
                    pool.tensor_tensor(rs[:, :], ve[:, :], half[:, 0:PG], ALU.pow).then_inc(rs_ready.sem, 1)
                    pool.wait_ge(*rms_in.now(g, 2))
                    pool.wait_ge(*h_ready.before(g))
                    pool.tensor_tensor(rr[:, 3, :], rr[:, 2, :], half[:, 0:PG], ALU.pow).then_inc(rh_ready.sem, 1)
                    pool.wait_ge(*rope_k.now(g, 1))
                    pool.wait_ge(*pe_s.before(g))
                    for n, h4 in enumerate((2, 3)):
                        r = slice(32 * h4, 32 * h4 + 32)
                        if n:
                            pool.wait_ge(*kp_ready.now(g, n - 1))
                        pool.tensor_tensor(k[r, :, h4, :], k1[r, :, :], k2[r, :, :], ALU.add).then_inc(kp_ready.sem, 1)
                    pool.wait_ge(*kp_ready.now(g, 1))
                    pool.wait_ge(*x2_ready.now(g))
                    pool.wait_ge(*ms_ready.before(g, 0))
                    pool.tensor_tensor(sq[:, :, :], x2[:, :, :], x2[:, :, :], ALU.mult).then_inc(sq_ready.sem, 1)
                    pool.wait_ge(*ms_ready.now(g, 1))
                    pool.wait_ge(*f0_ready.before(g))
                    pool.tensor_tensor(ms[:, 2, :], ms[:, 1, :], half[:, 0:PG], ALU.pow).then_inc(rms2_ready.sem, 1)
                    xg = x[:, bass.ds(g * PG, PG), :]
                    pool.tensor_tensor(xg, xg, x2[:, :, :], ALU.add).then_inc(fin.sem, 1)
                    pool.wait_ge(*flat_ready.now(g))
                    R.pool_scatter(pool, g, flat, dest)
                turns(pool, 0, GROUPS, body)
        clear_taken(nc)


def phase_experts(nc, A, banks, c, state, rows_in, rows_out, wall, swiglu, name):
    chunks = CH1 if swiglu else CH2
    HID = HID1 if swiglu else HID2
    NK = len(chunks)
    NW = wall.shape[-1]
    W2 = 2 * HID if swiglu else HID
    ident = c["ident"]
    with ExitStack() as ctx:
        def sb(n, shape, dt=F32):
            return ctx.enter_context(nc.sbuf_tensor(f"{name}_{n}", shape, dt))

        def sig(n, per=UN):
            return Signal(take_semaphore(ctx, nc, f"{name}_{n}"), per)

        def raw(n):
            return take_semaphore(ctx, nc, f"{name}_{n}")

        w = [sb(f"w{i}", [128, NW]) for i in range(UN)]
        xg = [sb(f"xg{i}", [128, 2, C]) for i in range(UN)]
        yb = [sb(f"yb{i}", [128, 2, C]) for i in range(UN)]
        xT = [sb(f"xT{i}", [128, TILE]) for i in range(2)]
        sg = [sb(f"sg{i}", [128, NK, TILE]) for i in range(2)]
        hT = [sb(f"hT{i}", [128, NK, TILE]) for i in range(2)] if swiglu else sg
        zero = sb("zero", [128, C])
        tail = sb("tail", [128, NE, 2], I32)
        tailf = sb("tailf", [128, NE, 2])
        le = sb("le", [128, NE, NE])
        iota = sb("iota", [1, TILES])
        cneg = sb("cneg", [128, NE])
        ti, tj = sb("ti", [128, NE], I32), sb("tj", [128, NE], I32)
        tf = sb("tf", [128, NE])
        cm, cum = sb("cm", [128, NE, NE]), sb("cum", [128, NE])
        shift = sb("shift", [128, NE])
        moved = sb("moved", [128, 2, PAIRS])
        posf2 = sb("posf2", [128, 2, PAIRS])
        ge, go = sb("ge", [1, TILES, NE]), sb("go", [1, TILES, NE])
        ei, off = sb("ei", [1, TILES]), sb("off", [1, TILES])
        table = sb("table", [1, 2, TILES], I32)
        prow = sb("prow", [128, 2])
        load, chain, zeroed, zlist, tsem = raw("load"), raw("chain"), raw("zeroed"), raw("zlist"), raw("tails")
        loaded = [raw(f"loaded{i}") for i in range(UN)]
        stored = [raw(f"stored{i}") for i in range(UN)]
        pe_x, pe_up, pe_down = sig("pe_x"), sig("pe_up", UN * NK), sig("pe_down")
        xT_ready, act_done = sig("xT_ready"), sig("act_done", UN * NK)
        h_ready = sig("h_ready", UN * NK) if swiglu else act_done
        y_ready = sig("y_ready")
        list_tiles = rows_in.rearrange("(a t p) c -> a p t c", t=2, p=128)
        y_tiles = rows_out.rearrange("(a t p) c -> a p t c", t=2, p=128)
        TPE = CAP // TILE

        with nc.Block() as block:
            @block.sync
            def _(sp):
                sp.dma_start(le[:, :, :], A["c_le"]).then_inc(load, 16)
                sp.dma_start(iota[:, :], A["c_iota"]).then_inc(load, 16)
                sp.dma_start(prow[:, :], A["c_prow"]).then_inc(load, 16)
                sp.wait_ge(zeroed, 1)
                for i in range(TILES - 2 * PAIRS * 128 // TILE):
                    for t in range(2):
                        sp.dma_start(list_tiles[NE * TPE + i, :, t, :], zero[:, :]).then_inc(zlist, 16)
                sp.wait_ge(zlist, 16 * 2 * (TILES - 2 * PAIRS * 128 // TILE))

            @block.vector
            def _(dve):
                base = state["base"]
                n = [0]

                def then(ins):
                    n[0] += 1
                    ins.then_inc(chain, 1)
                    dve.wait_ge(chain, n[0])

                dve.memset(zero[:, :], 0.0).then_inc(zeroed, 1)
                dve.wait_ge(load, 48)
                b = base[:, :]
                pr = prow[:, :]
                then(dve.tensor_tensor(tailf[:, :, :], bass.AP(b.tensor, b.offset, [b.ap[0], [1, NE], [0, 2]]),
                                       bass.AP(pr.tensor, pr.offset, [pr.ap[0], [0, NE], [1, 2]]), ALU.add))
                then(dve.tensor_copy(tail[:, :, :], tailf[:, :, :]))
                then(dve.tensor_scalar(cneg[:, :], c["rev"][:, :], float(CAP), float(TILE - 1 - NE * CAP), ALU.mult, ALU.add))
                then(dve.tensor_tensor(ti[:, :], base[:, :], cneg[:, :], ALU.add))
                then(dve.tensor_scalar(tj[:, :], ti[:, :], TILE.bit_length() - 1, None, ALU.logical_shift_right))
                then(dve.tensor_copy(tf[:, :], tj[:, :]))
                t = tf[:, :]
                then(dve.tensor_tensor(cm[:, :, :], le[:, :, :], bass.AP(t.tensor, t.offset, [t.ap[0], [0, NE], [1, NE]]), ALU.mult))
                then(dve.tensor_reduce(cum[:, :], cm[:, :, :], AX.X, ALU.add))
                t0 = tf[0:1, :]
                u, v = iota[:, :], cum[0:1, :]
                then(dve.tensor_tensor(ge[:, :, :], bass.AP(u.tensor, u.offset, [u.ap[0], [1, TILES], [0, NE]]),
                                       bass.AP(v.tensor, v.offset, [v.ap[0], [0, TILES], [1, NE]]), ALU.is_ge))
                then(dve.tensor_reduce(ei[:, :], ge[:, :, :], AX.X, ALU.add))
                then(dve.tensor_tensor(go[:, :, :], ge[:, :, :], bass.AP(t.tensor, t.offset, [t0.ap[0], [0, TILES], [1, NE]]), ALU.mult))
                then(dve.tensor_reduce(off[:, :], go[:, :, :], AX.X, ALU.add))
                then(dve.tensor_tensor(off[:, :], iota[:, :], off[:, :], ALU.subtract))
                then(dve.scalar_tensor_tensor(out=table[:, 0, :], in0=ei[:, :], scalar=float(TPE), in1=off[:, :],
                                              op0=ALU.mult, op1=ALU.add))
                then(dve.tensor_scalar(shift[:, :], tf[:, :], float(TILE), -float(CAP), ALU.mult, ALU.add))
                posf = state["posf"]
                p = posf[:, :, :].rearrange("t k p -> t (k p)")
                mv = moved[:, :, :].rearrange("t k p -> t (k p)")
                pc = posf2[:, :, :].rearrange("t k p -> t (k p)")
                then(dve.tensor_copy(pc, p))
                for e in range(1, NE):
                    then(dve.tensor_scalar(mv, p, float(e * CAP), shift[:, e - 1:e], ALU.is_ge, ALU.mult))
                    then(dve.tensor_tensor(pc, pc, mv, ALU.add))
                then(dve.tensor_copy(state["pos"][:, :, :], posf2[:, :, :]))
                then(dve.tensor_scalar(table[:, 1, :], ei[:, :], float(NE - 1), None, ALU.min))
                dve.sem_inc(y_ready.sem, y_ready.per)
                if swiglu:
                    dve.sem_inc(h_ready.sem, h_ready.per)

            @block.gpsimd
            def _(pool):
                pool.wait_ge(chain, 2)
                pool.wait_ge(zeroed, 1)
                for e in range(NE):
                    for r in range(2):
                        pool.indirect_dma_start(out=rows_in, out_offset=bass.IndirectOffsetOnAxis(ap=tail[:, e, r:r + 1], axis=0),
                                                in_=zero[:, :], in_offset=None).then_inc(tsem, 16)
                pool.wait_ge(tsem, 16 * 2 * NE)

            @block.scalar
            def _(act):
                open_signals(act, [xT_ready, act_done])

            @block.tensor
            def _(pe):
                open_signals(pe, [pe_x, pe_up, pe_down])

        bT, bY = banks[0], banks[7]
        NB = 3 if swiglu else 2
        up_banks = [banks[1:1 + NB], banks[4:4 + NB]]
        TURNS = TILES // UN

        with nc.Block() as block:
            @block.sync
            def _(sp):
                def read(g, j):
                    at = sp.value_load(table[0:1, 0, bass.ds(g * UN + j, 1)], min_val=0, max_val=(NE + 1) * TPE - 1)
                    ex = sp.value_load(table[0:1, 1, bass.ds(g * UN + j, 1)], min_val=0, max_val=NE - 1)
                    sp.wait_ge(*pe_down.now(g, j - UN))
                    sp.dma_start(w[j][:, :], wall[bass.ds(ex, 1), :, :].rearrange("a p n -> p (a n)")).then_inc(loaded[j], 16)
                    sp.dma_start(xg[j][:, :, :], list_tiles[bass.ds(at, 1), :, :, :].rearrange("a p t c -> p (a t) c")).then_inc(loaded[j], 16)

                def write(g, j):
                    sp.wait_ge(*y_ready.now(g, j))
                    sp.dma_start(y_tiles[bass.ds(g * UN + j, 1), :, :, :].rearrange("a p t c -> p (a t) c"), yb[j][:, :, :])\
                        .then_inc(stored[j], 16)

                for j in range(UN):
                    read(0, j)

                def body(g):
                    for j in range(UN):
                        write(g - 1, j)
                        read(g, j)
                turns(sp, 1, TURNS, body)
                for j in range(UN):
                    write(TURNS - 1, j)
                for j in range(UN):
                    sp.wait_ge(stored[j], 16 * TURNS)

            @block.tensor
            def _(pe):
                def x_T(g, j):
                    jj = j % UN
                    gg = g + 1 if j == UN else g
                    pe.wait_ge(loaded[jj], (gg + 1) * 32)
                    pe.wait_ge(*xT_ready.now(g, j - 1))
                    for t in range(2):
                        i = pe.transpose(bT[:, 128 * t:128 * t + 128], xg[jj][:, t, :], ident[:, :])
                    i.then_inc(pe_x.sem, 1)

                def up(g, j):
                    pe.wait_ge(*xT_ready.now(g, j))
                    pe.wait_ge(*h_ready.now(g, NK * (j - 2) + NK - 1))
                    for k, (c0, cn) in enumerate(chunks):
                        if swiglu:
                            bank = up_banks[j % 2][k]
                            for m in range(2):
                                i = pe.matmul(bank[0:cn, TILE * m:TILE * m + TILE], w[j][:, HID * m + c0:HID * m + c0 + cn],
                                              xT[j % 2][:, :], start=(m == 0), stop=True, skip_group_check=True)
                            i.then_inc(pe_up.sem, 1)
                        else:
                            bank = up_banks[j % 2][k // 2]
                            i = pe.matmul(bank[0:cn, TILE * (k % 2):TILE * (k % 2) + TILE], w[j][:, c0:c0 + cn],
                                          xT[j % 2][:, :], start=(k % 2 == 0), stop=True, skip_group_check=True)
                            i.then_inc(pe_up.sem, 1)

                def down(g, j):
                    jj = j % UN
                    pe.wait_ge(*h_ready.now(g, NK * j + NK - 1))
                    pe.wait_ge(*y_ready.now(g, j - 1))
                    for t in range(2):
                        for k, (c0, cn) in enumerate(chunks):
                            i = pe.matmul(bY[:, 128 * t:128 * t + 128], hT[jj % 2][0:cn, k, 128 * t:128 * t + 128],
                                          w[jj][0:cn, W2 + 128 * k:W2 + 128 * k + 128], start=(k == 0), stop=(k == NK - 1),
                                          skip_group_check=True)
                    i.then_inc(pe_down.sem, 1)

                def body(g, first=False, last=False):
                    for j in range(UN):
                        up(g, j)
                        if not (last and j == UN - 1):
                            x_T(g, j + 1)
                        if not (first and j == 0):
                            down(g, j - 1)
                x_T(0, 0)
                body(0, first=True)
                turns(pe, 1, TURNS - 1, body)
                body(TURNS - 1, last=True)
                down(TURNS - 1, UN - 1)

            @block.scalar
            def _(act):
                def x_T(g, j):
                    act.wait_ge(*pe_x.now(g, j))
                    act.wait_ge(*pe_up.now(g, NK * (j - 2) + NK - 1))
                    act.activation(xT[j % 2][:, :], bT[:, 0:TILE], ACT.Copy).then_inc(xT_ready.sem, 1)

                def body(g, last=False):
                    for j in range(UN):
                        for k, (c0, cn) in enumerate(chunks):
                            if swiglu:
                                act.wait_ge(*pe_up.now(g, NK * j + k))
                                act.wait_ge(*h_ready.now(g, NK * (j - 2) + k))
                                act.activation(sg[j % 2][0:cn, k, :], up_banks[j % 2][k][0:cn, 0:TILE], ACT.Silu)\
                                   .then_inc(act_done.sem, 1)
                            else:
                                act.wait_ge(*pe_up.now(g, NK * j + k // 2 * 2 + 1))
                                act.wait_ge(*pe_down.now(g, j - 2))
                                bank = up_banks[j % 2][k // 2]
                                b1 = W2 + NK * C + k
                                act.activation(sg[j % 2][0:cn, k, :], bank[0:cn, TILE * (k % 2):TILE * (k % 2) + TILE], ACT.Gelu,
                                               bias=w[j][:, b1:b1 + 1]).then_inc(act_done.sem, 1)
                        if not (last and j == UN - 1):
                            x_T(g, j + 1)
                x_T(0, 0)
                turns(act, 0, TURNS - 1, body)
                body(TURNS - 1, last=True)

            @block.vector
            def _(dve):
                def out(g, j):
                    jj = j % UN
                    dve.wait_ge(*pe_down.now(g, j))
                    src = bY[:, 0:2 * C].rearrange("r (t c) -> r t c", t=2)
                    if swiglu:
                        dve.tensor_copy(yb[jj][:, :, :], src).then_inc(y_ready.sem, 1)
                    else:
                        b = w[jj][:, W2 + NK * C + NK:W2 + NK * C + NK + C]
                        dve.tensor_tensor(yb[jj][:, :, :], src, bass.AP(b.tensor, b.offset, [b.ap[0], [0, 2], [1, C]]), ALU.add)\
                           .then_inc(y_ready.sem, 1)

                def body(g, first=False):
                    for j in range(UN):
                        if swiglu:
                            for k, (c0, cn) in enumerate(chunks):
                                dve.wait_ge(*act_done.now(g, NK * j + k))
                                dve.wait_ge(*pe_down.now(g, j - 2))
                                dve.tensor_tensor(hT[j % 2][0:cn, k, :], up_banks[j % 2][k][0:cn, TILE:2 * TILE],
                                                  sg[j % 2][0:cn, k, :], ALU.mult).then_inc(h_ready.sem, 1)
                        if not (first and j == 0):
                            out_wait(g, j - 1)
                            out(g, j - 1)

                def out_wait(g, j):
                    gg = g - 1 if j < 0 else g
                    if isinstance(gg, int):
                        if gg > 0:
                            dve.wait_ge(stored[j % UN], 16 * gg)
                    else:
                        dve.wait_ge(stored[j % UN], gg * 16)
                body(0, first=True)
                body(1)
                turns(dve, 2, TURNS, body)
                out_wait(TURNS - 1, UN - 1)
                out(TURNS - 1, UN - 1)
        clear_taken(nc)


class Combine:

    def __init__(self, ctx, nc, name, state, rows):
        def sig(n, per=1):
            return Signal(take_semaphore(ctx, nc, f"{name}_{n}"), per)

        self.state, self.rows = state, rows
        self.pos = ctx.enter_context(nc.sbuf_tensor(f"{name}_pos", [128, 2, PG], I32))
        self.y = ctx.enter_context(nc.sbuf_tensor(f"{name}_y", [128, 2, PG, C], F32))
        self.landed = take_semaphore(ctx, nc, f"{name}_landed")
        self.pos_ready = sig("pos_ready")
        self.gate = sig("gate")
        self.mixed = sig("mixed", 2 * PG)
        self.pool_signals = [self.pos_ready]
        self.dve_signals = [self.mixed]

    def fetch(self, pool, g):
        pos = self.state["pos"]
        if not (isinstance(g, int) and g == 0):
            pool.wait_ge(*self.mixed.now(g - 1, 2 * PG - 1))
            pool.wait_ge(self.landed, g * (16 * 2 * PG))
        pool.tensor_copy(self.pos[:, :, :], pos[:, :, bass.ds(g * PG, PG)]).then_inc(self.pos_ready.sem, 1)
        pool.wait_ge(*self.pos_ready.now(g))
        pool.sem_inc(self.gate.sem, 1)
        for k in range(2):
            for p in range(PG):
                pool.indirect_dma_start(out=self.y[:, k, p, :], out_offset=None, in_=self.rows,
                                        in_offset=bass.IndirectOffsetOnAxis(ap=self.pos[:, k, p:p + 1], axis=0))\
                    .then_inc(self.landed, 16)

    def vector_mix(self, dve, g, x):
        w = self.state["w"]
        dve.wait_ge(self.landed, (g + 1) * (16 * 2 * PG))
        for k in range(2):
            if k:
                dve.wait_ge(*self.mixed.now(g, PG - 1))
            for p in range(PG):
                xt = x[:, bass.ds(g * PG + p, 1), :].rearrange("p a c -> p (a c)")
                dve.scalar_tensor_tensor(out=xt, in0=self.y[:, k, p, :], scalar=w[:, k, bass.ds(g * PG + p, 1)], in1=xt,
                                         op0=ALU.mult, op1=ALU.add).then_inc(self.mixed.sem, 1)


def phase_gnn1(nc, A, x, banks, c, state1, rows1, state2, dest):
    ident, half, adj = c["ident"], c["half"], c["adj"]
    with ExitStack() as ctx:
        def sb(name, shape, dt=F32):
            return ctx.enter_context(nc.sbuf_tensor("g1_" + name, shape, dt))

        def sig(name, per=1):
            return Signal(take_semaphore(ctx, nc, "g1_" + name), per)

        w1, w2, w3 = sb("w1", [128, C]), sb("w2", [128, C]), sb("w3", [128, C])
        wg = sb("wg", [128, NE])
        bg = sb("bg", [128, NE])
        mask = sb("mask", [128, NODES])
        st = sb("st", [128, 2, PG, 11]); mean = sb("mean", [128, 2, PG]); ve = sb("ve", [128, 2, PG]); rs = sb("rs", [128, 2, PG])
        xn = sb("xn", [128, PG, C])
        xT = sb("xT", [128, GT])
        h1, h2 = sb("h1", [128, GT]), sb("h2", [128, GT])
        h3 = sb("h3", [128, PG, C + 1])
        e1 = sb("e1", [128, PG, NODES])
        e2 = sb("e2", [128, PG, NODES])
        mx = sb("mx", [128, PG])
        s = sb("s", [128, PG, NODES])
        pr = sb("pr", [128, PG, 2, NODES])
        pt = sb("pt", [128, PG, 128])
        rc = sb("rc", [128, PG])
        o = sb("o", [128, PG, C])
        flat = sb("flat", [128, PG, C])
        fT = sb("fT", [128, GT])
        load = take_semaphore(ctx, nc, "g1_load")
        setup = take_semaphore(ctx, nc, "g1_setup")
        R = Routing(ctx, nc, "g1r", c, dict(state2, bias=bg))
        M = Combine(ctx, nc, "g1c", state1, rows1)

        bn, part, vs = [sig("bn0", PG), sig("bn1", PG)], [sig("part0", 6), sig("part1", 6)], [sig("vs0"), sig("vs1")]
        xn_ready, h3_ready = sig("xn_ready", PG), sig("h3_ready")
        e_steps = sig("e_steps", 5)
        rc_ready, o_ready, x3_ready = sig("rc_ready", 2), sig("o_ready", PG), sig("x3_ready")
        flat_ready = sig("flat_ready", PG)
        gate = sig("gate")
        dve_signals = bn + part + vs + [xn_ready, h3_ready, e_steps, rc_ready, o_ready, x3_ready, flat_ready]\
            + R.dve_signals + M.dve_signals
        xT_ready, h12_ready, p_ready, pt_ready, fT_ready = sig("xT_ready"), sig("h12_ready", 2), sig("p_ready", 2), sig("pt_ready"), sig("fT_ready")
        act_signals = [xT_ready, h12_ready, p_ready, pt_ready, fT_ready] + R.act_signals
        rs_ready = [sig("rs0_ready"), sig("rs1_ready")]
        pool_signals = rs_ready + R.pool_signals + M.pool_signals
        pe_xT, pe_h, pe_e, pe_pt, pe_o, pe_fT = sig("pe_xT"), sig("pe_h", 3), sig("pe_e"), sig("pe_pt"), sig("pe_o", 2), sig("pe_fT")
        pe_signals = [pe_xT, pe_h, pe_e, pe_pt, pe_o, pe_fT] + R.pe_signals
        bT, bH1, bH2, bH3, bE, bO0, bO1, bR = banks

        with nc.Block() as block:
            @block.sync
            def _(sp):
                sp.dma_start(w1[:, :], A["L1_gnn_W1"]).then_inc(load, 16)
                sp.dma_start(w2[:, :], A["L1_gnn_W2"]).then_inc(load, 16)
                sp.dma_start(w3[:, :], A["L1_gnn_W3"]).then_inc(load, 16)
                sp.dma_start(wg[:, :], A["L1_ffn_Wg"]).then_inc(load, 16)
                sp.dma_start(bg[:, :], row_bcast(A["L1_ffn_bg"])).then_inc(load, 16)
                sp.wait_ge(load, 16 * 5)

            @block.gpsimd
            def _(pool):
                pool.memset(pr[:, :, :, :], 0.0).then_inc(setup, 1)
                pool.memset(h3[:, :, C:C + 1], 1.0).then_inc(setup, 1)
                open_signals(pool, pool_signals)

            @block.vector
            def _(dve):
                dve.tensor_scalar(mask[:, :], adj[:, :], 0.0, -1e12, ALU.is_le, ALU.mult)
                b = state2["base"]
                dve.tensor_scalar(b[:, :], c["rev"][:, :], -float(CAP), float(NE * CAP), ALU.mult, ALU.add)
                open_signals(dve, dve_signals)

            @block.scalar
            def _(act):
                open_signals(act, act_signals)

            @block.tensor
            def _(pe):
                open_signals(pe, pe_signals)

        def xt(g, p):
            return x[:, bass.ds(g * PG + p, 1), :].rearrange("p a c -> p (a c)")

        with nc.Block() as block:
            @block.tensor
            def _(pe):
                def body(g):
                    pe.wait_ge(*xn_ready.now(g, PG - 1))
                    pe.wait_ge(*fT_ready.before(g))
                    for p in range(PG):
                        i = pe.transpose(bT[:, 128 * p:128 * p + 128], xn[:, p, :], ident[:, :])
                    i.then_inc(pe_xT.sem, 1)
                    pe.wait_ge(*xT_ready.now(g))
                    pe.wait_ge(*h12_ready.before(g))
                    pe.matmul(bH1[:, :], w1[:, :], xT[:, :], start=True, stop=True).then_inc(pe_h.sem, 1)
                    pe.wait_ge(*pt_ready.before(g))
                    pe.matmul(bH2[:, :], w2[:, :], xT[:, :], start=True, stop=True).then_inc(pe_h.sem, 1)
                    pe.wait_ge(*h3_ready.before(g))
                    for p in range(PG):
                        i = pe.matmul(bH3[:, 128 * p:128 * p + 128], xT[:, 128 * p:128 * p + 128], w3[:, :],
                                      start=(p == 0), stop=True, skip_group_check=True)
                    i.then_inc(pe_h.sem, 1)
                    pe.wait_ge(*h12_ready.now(g, 1))
                    pe.wait_ge(*e_steps.before(g, 1))
                    for fr in range(2 * PG):
                        f, p = fr % 2, fr // 2
                        t = slice(64 * fr, 64 * fr + 64)
                        i = pe.matmul(bE[64 * f:64 * f + 64, 64 * p:64 * p + 64], h1[:, t], h2[:, t],
                                      start=(p == 0), stop=True, skip_group_check=True)
                    i.then_inc(pe_e.sem, 1)
                    pe.wait_ge(*p_ready.now(g, 1))
                    for p in range(PG):
                        i = pe.transpose(bH2[:, 128 * p:128 * p + 128], pr[:, p, :, :].rearrange("n f m -> n (f m)"), ident[:, :])
                    i.then_inc(pe_pt.sem, 1)
                    pe.wait_ge(*pt_ready.now(g))
                    pe.wait_ge(*h3_ready.now(g))
                    pe.wait_ge(*o_ready.before(g))
                    for u, bank in enumerate([bO0, bO1]):
                        for q in range(2):
                            p = 2 * u + q
                            i = pe.matmul(bank[:, (C + 1) * q:(C + 1) * q + C + 1], pt[:, p, :], h3[:, p, :],
                                          start=(q == 0), stop=True, skip_group_check=True)
                        i.then_inc(pe_o.sem, 1)
                    pe.wait_ge(*flat_ready.now(g, PG - 1))
                    for p in range(PG):
                        i = pe.transpose(bT[:, 128 * p:128 * p + 128], flat[:, p, :], ident[:, :])
                    i.then_inc(pe_fT.sem, 1)
                    pe.wait_ge(*fT_ready.now(g))
                    pe.wait_ge(*R.pstep.before(g, 0))
                    R.tensor_logits(pe, g, bR, fT, wg)
                    R.tensor_rank(pe, g, bR)
                turns(pe, 0, GROUPS, body)

            @block.scalar
            def _(act):
                def body(g):
                    act.wait_ge(*pe_xT.now(g))
                    act.activation(xT[:, :], bT[:, :], ACT.Copy).then_inc(xT_ready.sem, 1)
                    for n, (bank, h) in enumerate([(bH1, h1), (bH2, h2)]):
                        act.wait_ge(*pe_h.now(g, n))
                        act.wait_ge(*pe_e.before(g))
                        act.activation(h[:, :], bank[:, :], ACT.Copy).then_inc(h12_ready.sem, 1)
                    act.wait_ge(*e_steps.now(g, 4))
                    act.wait_ge(*pe_pt.before(g))
                    for f in range(2):
                        r = slice(64 * f, 64 * f + 64)
                        act.activation(pr[r, :, f, :], s[r, :, :], ACT.Exp).then_inc(p_ready.sem, 1)
                    act.wait_ge(*pe_pt.now(g))
                    act.wait_ge(*pe_o.before(g))
                    act.activation(pt[:, :, :].rearrange("m p n -> m (p n)"), bH2[:, :], ACT.Copy).then_inc(pt_ready.sem, 1)
                    act.wait_ge(*pe_fT.now(g))
                    act.wait_ge(*R.pe_logits.before(g))
                    act.activation(fT[:, :], bT[:, :], ACT.Copy).then_inc(fT_ready.sem, 1)
                    R.scalar_exp(act, g, False)
                turns(act, 0, GROUPS, body)

            @block.vector
            def _(dve):
                def body(g):
                    M.vector_mix(dve, g, x)
                    norm_stats(dve, lambda p: xt(g, p), st[:, 0, :, :], mean[:, 0, :], ve[:, 0, :], bn[0], part[0], vs[0], g,
                               EPS_LN, [M.mixed.now(g, 2 * PG - 1), rs_ready[0].before(g), xn_ready.before(g)], gate)
                    dve.wait_ge(*rs_ready[0].now(g))
                    dve.wait_ge(*pe_xT.before(g))
                    for p in range(PG):
                        dve.tensor_scalar(xn[:, p, :], xt(g, p), mean[:, 0, p:p + 1], rs[:, 0, p:p + 1],
                                          ALU.subtract, ALU.mult).then_inc(xn_ready.sem, 1)
                    dve.wait_ge(*pe_h.now(g, 2))
                    dve.wait_ge(*pe_o.before(g))
                    dve.tensor_copy(h3[:, :, 0:C], bH3[:, :].rearrange("m (p c) -> m p c", p=PG)).then_inc(h3_ready.sem, 1)
                    ev = bE[:, 0:PG * NODES].rearrange("n (p m) -> n p m", p=PG)
                    dve.wait_ge(*pe_e.now(g))
                    dve.wait_ge(*e_steps.before(g))
                    dve.tensor_scalar(e1[:, :, :], ev, 0.2, None, ALU.mult).then_inc(e_steps.sem, 1)
                    dve.wait_ge(*e_steps.now(g, 0))
                    dve.tensor_tensor(e1[:, :, :], ev, e1[:, :, :], ALU.max).then_inc(e_steps.sem, 1)
                    dve.wait_ge(*e_steps.now(g, 1))
                    mk = mask[:, :]
                    dve.tensor_tensor(e2[:, :, :], e1[:, :, :], bass.AP(mk.tensor, mk.offset, [mk.ap[0], [0, PG], [1, NODES]]), ALU.add)\
                       .then_inc(e_steps.sem, 1)
                    dve.wait_ge(*e_steps.now(g, 2))
                    dve.tensor_reduce(mx[:, :], e2[:, :, :], AX.X, ALU.max).then_inc(e_steps.sem, 1)
                    dve.wait_ge(*e_steps.now(g, 3))
                    dve.wait_ge(*p_ready.before(g))
                    m = mx[:, :]
                    dve.tensor_tensor(s[:, :, :], e2[:, :, :], bass.AP(m.tensor, m.offset, [m.ap[0], [1, PG], [0, NODES]]), ALU.subtract)\
                       .then_inc(e_steps.sem, 1)
                    for u, bank in enumerate([bO0, bO1]):
                        dve.wait_ge(*pe_o.now(g, u))
                        ov = bank[:, 0:2 * (C + 1)].rearrange("n (p c) -> n p c", p=2)
                        dve.wait_ge(*o_ready.before(g))
                        dve.reciprocal(rc[:, 2 * u:2 * u + 2], ov[:, :, C]).then_inc(rc_ready.sem, 1)
                        dve.wait_ge(*rc_ready.now(g, u))
                        if u == 0:
                            dve.wait_ge(*x3_ready.before(g))
                        for q in range(2):
                            p = 2 * u + q
                            dve.tensor_scalar(o[:, p, :], ov[:, q, 0:C], rc[:, p:p + 1], 0.0, ALU.mult, ALU.max).then_inc(o_ready.sem, 1)
                    dve.wait_ge(*o_ready.now(g, PG - 1))
                    xg = x[:, bass.ds(g * PG, PG), :]
                    dve.tensor_tensor(xg, xg, o[:, :, :], ALU.add).then_inc(x3_ready.sem, 1)
                    norm_stats(dve, lambda p: xt(g, p), st[:, 1, :, :], mean[:, 1, :], ve[:, 1, :], bn[1], part[1], vs[1], g,
                               EPS_LN, [x3_ready.now(g), rs_ready[1].before(g), flat_ready.before(g)], gate)
                    dve.wait_ge(*rs_ready[1].now(g))
                    dve.wait_ge(*pe_fT.before(g))
                    dve.wait_ge(*R.scattered.before(g))
                    for p in range(PG):
                        dve.tensor_scalar(flat[:, p, :], xt(g, p), mean[:, 1, p:p + 1], rs[:, 1, p:p + 1],
                                          ALU.subtract, ALU.mult).then_inc(flat_ready.sem, 1)
                    R.vector_choose(dve, g, bR, False)
                    R.vector_rows(dve, g, bR)
                    R.vector_weights(dve, g, False)
                turns(dve, 0, GROUPS, body)

            @block.gpsimd
            def _(pool):
                def body(g, last=False):
                    pool.wait_ge(*vs[0].now(g))
                    pool.wait_ge(*xn_ready.before(g))
                    pool.tensor_tensor(rs[:, 0, :], ve[:, 0, :], half[:, 0:PG], ALU.pow).then_inc(rs_ready[0].sem, 1)
                    if not last:
                        M.fetch(pool, g + 1)
                    pool.wait_ge(*vs[1].now(g))
                    pool.wait_ge(*flat_ready.before(g))
                    pool.tensor_tensor(rs[:, 1, :], ve[:, 1, :], half[:, 0:PG], ALU.pow).then_inc(rs_ready[1].sem, 1)
                    pool.wait_ge(*flat_ready.now(g, PG - 1))
                    R.pool_scatter(pool, g, flat, dest)
                M.fetch(pool, 0)
                turns(pool, 0, GROUPS - 1, body)
                body(GROUPS - 1, last=True)
        clear_taken(nc)


def phase_finish(nc, x, c, state, rows, out_dram):
    with ExitStack() as ctx:
        M = Combine(ctx, nc, "fin", state, rows)
        stored = take_semaphore(ctx, nc, "fin_stored")
        with nc.Block() as block:
            @block.gpsimd
            def _(pool):
                open_signals(pool, M.pool_signals)

            @block.vector
            def _(dve):
                open_signals(dve, M.dve_signals)

        with nc.Block() as block:
            @block.gpsimd
            def _(pool):
                M.fetch(pool, 0)
                turns(pool, 1, GROUPS, lambda g: M.fetch(pool, g))

            @block.vector
            def _(dve):
                turns(dve, 0, GROUPS, lambda g: M.vector_mix(dve, g, x))

            @block.sync
            def _(sp):
                def body(g):
                    sp.wait_ge(*M.mixed.now(g, 2 * PG - 1))
                    sp.dma_start(out_dram[:, bass.ds(g * PG, PG), :], x[:, bass.ds(g * PG, PG), :]).then_inc(stored, 16)
                turns(sp, 0, GROUPS, body)
                sp.wait_ge(stored, 16 * GROUPS)


_INS = ['x', 'adj', 'L0_gnn_w_qkv', 'L0_gnn_ln1_g', 'L0_gnn_ln1_b', 'L0_gnn_ln2_g', 'L0_gnn_ln2_b', 'L0_gnn_w1',
        'L0_gnn_b1', 'L0_gnn_w2', 'L0_gnn_b2', 'L0_ffn_ln1_w', 'L0_ffn_ln2_w', 'L1_gnn_W1', 'L1_gnn_W2', 'L1_gnn_W3',
        'L1_ffn_Wg', 'L1_ffn_bg']


def laid_out(inputs):
    import numpy as np

    def T(w):
        return np.ascontiguousarray(np.asarray(w).T)

    eye = np.eye(128, dtype=np.float32)
    a = {"c_ident": eye}
    a["c_rev"] = np.ascontiguousarray(np.broadcast_to(NE - np.arange(NE, dtype=np.float32), (128, NE)))
    a["c_tri"] = np.triu(np.ones((128, 128), np.float32), 1)
    inv_freq = 1.0 / 10000.0 ** (np.arange(0, D1, 2, dtype=np.float32) / D1)
    ang = np.outer(np.arange(NODES, dtype=np.float32), inv_freq)
    cos, sin = np.cos(ang).T, np.sin(ang).T
    a["c_rope"] = np.ascontiguousarray(np.stack([np.tile(np.concatenate([cos, cos]), (H1, 1)),
                                                 np.tile(np.concatenate([-sin, sin]), (H1, 1))], axis=1), dtype=np.float32)
    n, m = np.arange(128)[:, None] % NODES, np.arange(NODES)[None, :]
    a["c_causal"] = np.where(m > n, np.float32(-1e30 * D1 ** 0.5), np.float32(0))
    swap = np.arange(D1) ^ (D1 // 2)
    wq = T(inputs["L0_ffn_wq"]).reshape(C, H1, D1)
    wk = np.repeat(T(inputs["L0_ffn_wk"]).reshape(C, KV1, D1), H1 // KV1, axis=1)
    for name, w in [("c_wq", wq), ("c_wk", wk)]:
        a[name] = np.ascontiguousarray(w.reshape(C, 128))
        a[name + "_x"] = np.ascontiguousarray(w[:, :, swap].reshape(C, 128))
    a["c_wv"] = T(inputs["L0_ffn_wv"])
    a["c_wo"] = T(inputs["L0_ffn_wo"])
    a["c_wr"] = T(inputs["L0_ffn_router_w"])
    e = np.arange(NE)
    a["c_le"] = np.ascontiguousarray(np.broadcast_to(e[None, :] <= e[:, None], (128, NE, NE)), dtype=np.float32)
    a["c_iota"] = np.arange(TILES, dtype=np.float32)[None]
    a["c_prow"] = (np.arange(128)[:, None] + 128 * np.arange(2)[None]).astype(np.float32)

    def by_chunk(w):
        chunks = -(-w.shape[1] // 128)
        full = np.zeros((NE, chunks * 128, C), np.float32)
        full[:, :w.shape[1]] = w
        return full.reshape(NE, chunks, 128, C).transpose(0, 2, 1, 3).reshape(NE, 128, chunks * C)

    w1, w2, w3 = (np.asarray(inputs[f"L0_ffn_w{i}"]).transpose(0, 2, 1) for i in (1, 2, 3))
    a["c_wall1"] = np.ascontiguousarray(np.concatenate([w1, w3, by_chunk(w2)], axis=2))
    w1, w2, b1, b2 = (np.asarray(inputs["L1_ffn_" + n]) for n in ("W1", "W2", "b1", "b2"))
    a["c_wall2"] = np.ascontiguousarray(np.concatenate(
        [w1, by_chunk(w2), b1.reshape(NE, len(CH2), 128).transpose(0, 2, 1), np.broadcast_to(b2[:, None], (NE, 128, C))], axis=2))
    return a


def kernel(**inputs):
    import numpy as np
    import concourse.bacc as bacc
    from concourse import mybir as mb
    from concourse.bass_utils import run_bass_kernel_spmd as run

    nc = bacc.Bacc("TRN2", target_bir_lowering=False, num_devices=1)
    arrays = {n: np.ascontiguousarray(inputs[n]) for n in _INS}
    arrays.update(laid_out(inputs))
    A = {}
    for n, a in arrays.items():
        A[n] = nc.dram_tensor(f"in_{n}", a.shape, mb.dt.from_np(a.dtype), kind="ExternalInput").ap()
    out = nc.dram_tensor("out_0", (FRAMES, NODES, C), mb.dt.float32, kind="ExternalOutput").ap()
    build(nc, A, out)
    r = run(nc, [{f"in_{n}": a for n, a in arrays.items()}], core_ids=[0])
    return r.results[0]["out_0"]
```

```python
from contextlib import ExitStack

import concourse.bass as bass
from concourse import mybir

F32 = mybir.dt.float32
BF16 = mybir.dt.bfloat16
I32 = mybir.dt.int32
U32 = mybir.dt.uint32
ALU = mybir.AluOpType
ACT = mybir.ActivationFunctionType
AX = mybir.AxisListType

FRAMES, NODES, C = 128, 64, 128
PAIRS = FRAMES // 2
PG = 4
GROUPS = PAIRS // PG
GT = PG * 128
EPS_LN = 1e-5
EPS_RMS = 1e-6
H0, D0 = 8, 16
H1, KV1, D1 = 4, 2, 32
NE = 8
HID1 = 341
HID2 = 512
TILE = 256
CAP = PAIRS * 128 + TILE
TILES = 2 * PAIRS * 128 // TILE + NE
UN = 4
TOKENS = FRAMES * NODES
ROW = C + 2
TRASH = 2 * NE * 128 + (TILES - 2 * TOKENS // TILE) * TILE
CH1 = [(0, 128), (128, 128), (256, 85)]
CH2 = [(128 * i, 128) for i in range(4)]


TAKEN = []


class Signal:

    def __init__(self, sem, per):
        self.sem, self.per = sem, per

    def now(self, g, j=0):
        return self.sem, (g + 2) * self.per + (j + 1)

    def before(self, g, j=None, turns=1):
        return self.sem, (g + 2 - turns) * self.per + (self.per if j is None else j + 1)


def take_semaphore(ctx, nc, name):
    sem = ctx.enter_context(nc.semaphore(name))
    TAKEN.append(sem)
    return sem


def clear_taken(nc):
    with nc.Block() as block:
        @block.gpsimd
        def _(pool):
            nums = sorted(s.num for s in TAKEN)
            while nums:
                n = 1
                while n < len(nums) and nums[n] == nums[0] + n:
                    n += 1
                pool.sem_clear(range(nums[0], nums[0] + n))
                del nums[:n]
    TAKEN.clear()


def open_signals(eng, signals):
    for s in signals:
        eng.sem_inc(s.sem, 2 * s.per)


def turns(eng, first, last, body):
    with eng.Fori(first, last) as g:
        body(g)


def runs(i):
    return not isinstance(i, int) or 0 <= i < GROUPS


def skewed(eng, step, first=2):
    for g in range(-1, first):
        step(g, g % 2)
    with eng.Fori(first // 2, GROUPS // 2 - 1) as turn:
        for b in range(2):
            step(turn * 2 + b, b)
    for g in range(GROUPS - 2, GROUPS + 2):
        step(g, g % 2)


def row_bcast(vec, rows=128):
    n = vec.shape[-1]
    return bass.AP(vec.tensor, vec.offset, [[0, rows], [1, n]])


def build(nc, A, out):
    TAKEN.clear()
    with ExitStack() as ctx:
        def sb(name, shape, dt=F32):
            return ctx.enter_context(nc.sbuf_tensor(name, shape, dt))

        x = sb("x", [128, PAIRS, C])
        ident = sb("ident", [128, 128])
        identb = sb("identb", [128, 128], BF16)
        half = sb("half", [128, 8])
        rev = sb("rev", [128, NE])
        tri = sb("tri", [128, 128], BF16)
        ids = sb("ids", [128, PAIRS])
        tri32 = sb("tri32", [128, 128])
        ones = sb("ones", [128, 128], BF16)
        maskb = sb("maskb", [128, NODES], BF16)
        adj = sb("adj_sb", [128, NODES], I32)
        load_sem = ctx.enter_context(nc.semaphore("load_sem"))
        setup_sem = ctx.enter_context(nc.semaphore("setup_sem"))
        banks = [ctx.enter_context(nc.psum_tensor(f"bank{i}", [128, 512], F32)) for i in range(8)]
        x_dram = A["x"].rearrange("(t f) n c -> (f n) t c", f=2)
        out_dram = out.rearrange("(t f) n c -> (f n) t c", f=2)

        with nc.Block() as block:
            @block.sync
            def _(sp):
                sp.dma_start(ident[:, :], A["c_ident"]).then_inc(load_sem, 16)
                sp.dma_start(rev[:, :], A["c_rev"]).then_inc(load_sem, 16)
                sp.dma_start(ids[:, :], A["c_ids"]).then_inc(load_sem, 16)
                sp.dma_start(tri32[:, :], A["c_tri"]).then_inc(load_sem, 16)
                for f in range(2):
                    sp.dma_start(adj[64 * f:64 * f + 64, :], A["adj"]).then_inc(load_sem, 16)
                for i in range(4):
                    n = PAIRS // 4
                    sp.dma_start(x[:, n * i:n * i + n, :], x_dram[:, n * i:n * i + n, :]).then_inc(load_sem, 16)
                sp.wait_ge(load_sem, 16 * 10)

            @block.vector
            def _(dve):
                dve.wait_ge(load_sem, 16 * 10)
                dve.tensor_copy(identb[:, :], ident[:, :])
                dve.tensor_copy(tri[:, :], tri32[:, :])

            @block.gpsimd
            def _(pool):
                pool.memset(half[:, :], -0.5).then_inc(setup_sem, 1)
                pool.memset(ones[:, :], 1.0).then_inc(setup_sem, 1)

        common = dict(x=x, ident=ident, identb=identb, half=half, maskb=maskb, adj=adj, banks=banks)
        phase_gnn0(nc, A, **common)
        list1 = nc.dram_tensor("dispatch1", ((NE + 1) * CAP, ROW), F32, kind="Internal").ap()
        c = dict(ident=ident, identb=identb, half=half, rev=rev, tri=tri, ones=ones, adj=adj, ids=ids)
        state = dict(base=sb("base1", [128, NE]), w=sb("w1", [128, 2, PAIRS]))
        phase_attn1(nc, A, x, banks, c, state, list1)
        rows1 = nc.dram_tensor("rows1", (2 * TOKENS + TRASH, C), F32, kind="Internal").ap()
        phase_experts(nc, A, banks, c, state, list1, rows1, A["c_wall1"], True, "m1")
        list2 = nc.dram_tensor("dispatch2", ((NE + 1) * CAP, ROW), F32, kind="Internal").ap()
        state2 = dict(base=sb("base2", [128, NE]), w=sb("w2", [128, 2, PAIRS]))
        phase_gnn1(nc, A, x, banks, c, state, rows1, state2, list2)
        rows2 = nc.dram_tensor("rows2", (2 * TOKENS + TRASH, C), F32, kind="Internal").ap()
        phase_experts(nc, A, banks, c, state2, list2, rows2, A["c_wall2"], False, "m2")
        phase_finish(nc, x, c, state2, rows2, out_dram)


def norm_stats(dve, src, st, mean, ve, bn, part, vs, g, eps, waits=(), gate=None):
    for w in waits:
        dve.wait_ge(*w)
    if gate is not None:
        dve.sem_inc(gate.sem, 1)
    for p in range(PG):
        dve.bn_stats(st[:, p, 0:6], src(p)).then_inc(bn.sem, 1)
    dve.wait_ge(*bn.now(g, PG - 1))
    dve.tensor_tensor(st[:, :, 6], st[:, :, 1], st[:, :, 4], ALU.add).then_inc(part.sem, 1)
    dve.tensor_tensor(st[:, :, 7], st[:, :, 1], st[:, :, 4], ALU.subtract).then_inc(part.sem, 1)
    dve.tensor_tensor(st[:, :, 8], st[:, :, 2], st[:, :, 5], ALU.add).then_inc(part.sem, 1)
    dve.wait_ge(*part.now(g, 1))
    dve.tensor_scalar(mean[:, :], st[:, :, 6], 0.5, None, ALU.mult).then_inc(part.sem, 1)
    dve.scalar_tensor_tensor(out=st[:, :, 9], in0=st[:, :, 7], scalar=0.25, in1=st[:, :, 7],
                             op0=ALU.mult, op1=ALU.mult).then_inc(part.sem, 1)
    dve.wait_ge(*part.now(g, 2))
    dve.tensor_scalar(st[:, :, 10], st[:, :, 8], 1.0 / C, eps, ALU.mult, ALU.add).then_inc(part.sem, 1)
    dve.wait_ge(*part.now(g, 5))
    dve.tensor_tensor(ve[:, :], st[:, :, 9], st[:, :, 10], ALU.add).then_inc(vs.sem, 1)


def phase_gnn0(nc, A, x, ident, identb, half, maskb, adj, banks):
    with ExitStack() as ctx:
        def sb(name, shape, dt=F32):
            return ctx.enter_context(nc.sbuf_tensor("g0_" + name, shape, dt))

        def sig(name, per=1):
            return Signal(take_semaphore(ctx, nc, "g0_" + name), per)

        wqkv = sb("wqkv", [128, 3 * C])
        wq = sb("wq", [128, 2, 2, 128])
        wk = sb("wk", [128, 2, 2, 128])
        w1 = sb("w1", [128, C])
        w2 = sb("w2", [128, C])
        vecs = sb("vecs", [128, 5, C])
        b1 = sb("b1", [128, 1])
        xn = [sb(f"xn{i}", [128, PG, C]) for i in range(2)]
        mv = sb("mv", [128, PG]); st6 = sb("st6", [128, PG, 11]); ve = sb("ve", [128, PG]); rs = sb("rs", [128, PG])
        mv1 = sb("mv1", [128, PG]); st61 = sb("st61", [128, PG, 11]); ve1 = sb("ve1", [128, PG]); rs1 = sb("rs1", [128, PG])
        mv2 = sb("mv2", [128, PG]); st62 = sb("st62", [128, PG, 11]); ve2 = sb("ve2", [128, PG]); rs2 = sb("rs2", [128, PG])
        xT = sb("xT", [128, GT])
        qs = [sb(f"q{i}", [128, 2, PG, 2, NODES]) for i in range(2)]
        ks = [sb(f"k{i}", [128, 2, PG, 4, NODES]) for i in range(2)]
        vs = [sb(f"v{i}", [128, 2 * PG, 4, 2, D0 + 1]) for i in range(2)]
        s = sb("s", [128, 2, H0, NODES])
        mx = sb("mx", [128, 2, H0])
        pt = sb("pt", [128, 2, 4, 128])
        rc = sb("rc", [128, 2, H0])
        ts = [sb(f"t{i}", [128, PG, C]) for i in range(2)]
        y1 = sb("y1", [128, PG, C])
        y1b = sb("y1b", [128, PG, C])
        y1T = sb("y1T", [128, GT])
        hT = sb("hT", [128, GT])
        u = sb("u", [128, PG, C])

        load = take_semaphore(ctx, nc, "g0_load")
        setup = take_semaphore(ctx, nc, "g0_setup")
        gate = sig("gate")
        bn0, ag0, ve0 = sig("bn0", PG), sig("ag0", 6), sig("ve0")
        bn1, ag1, vs1 = sig("bn1", PG), sig("ag1", 6), sig("vs1")
        bn2, ag2, vs2 = sig("bn2", PG), sig("ag2", 6), sig("vs2")
        xn_ready = sig("xn_ready", PG)
        kd_ready = sig("kd_ready", 2)
        v_ready = sig("v_ready", 2)
        mx_ready = sig("mx_ready", PG)
        s_ready = sig("s_ready", PG)
        rc_ready = sig("rc_ready", PG)
        o_ready = sig("o_ready", PG)
        t_ready = sig("t_ready")
        n1_ready = sig("n1_ready", PG)
        u_ready = sig("u_ready")
        n2_ready = sig("n2_ready", PG)
        dve_signals = [bn0, ag0, ve0, bn1, ag1, vs1, bn2, ag2, vs2, xn_ready, kd_ready, v_ready, mx_ready,
                       s_ready, rc_ready, o_ready, t_ready, n1_ready, u_ready, n2_ready]
        xT_ready, q_ready, ka_ready = sig("xT_ready"), sig("q_ready", 2), sig("ka_ready", 2)
        e_ready, pt_ready = sig("e_ready", PG), sig("pt_ready", PG)
        y1T_ready, hT_ready = sig("y1T_ready"), sig("hT_ready")
        act_signals = [xT_ready, q_ready, ka_ready, e_ready, pt_ready, y1T_ready, hT_ready]
        rs0_ready, rs1_ready, rs2_ready = sig("rs0_ready"), sig("rs1_ready"), sig("rs2_ready")
        y1m, y1_ready, y1b_ready = sig("y1m"), sig("y1_ready"), sig("y1b_ready")
        fin = sig("fin", 3)
        pool_signals = [rs0_ready, rs1_ready, rs2_ready, y1m, y1_ready, y1b_ready, fin]
        pe_xT, pe_q, pe_k, pe_v = sig("pe_xT"), sig("pe_q", 2), sig("pe_k"), sig("pe_v")
        pe_s, pe_pt, pe_o = sig("pe_s", PG), sig("pe_pt", PG), sig("pe_o", PG)
        pe_y1T, pe_h, pe_f = sig("pe_y1T"), sig("pe_h"), sig("pe_f")
        pe_signals = [pe_xT, pe_q, pe_k, pe_v, pe_s, pe_pt, pe_o, pe_y1T, pe_h, pe_f]

        bT, bQ0, bQ1, bF, bS0, bS1, bPT, bO = banks

        with nc.Block() as block:
            @block.sync
            def _(sp):
                sp.dma_start(wqkv[:, :], A["L0_gnn_w_qkv"]).then_inc(load, 16)
                sp.dma_start(w1[:, :], A["L0_gnn_w1"]).then_inc(load, 16)
                sp.dma_start(w2[:, :], A["L0_gnn_w2"]).then_inc(load, 16)
                for i, name in enumerate(["ln1_g", "ln1_b", "ln2_g", "ln2_b", "b2"]):
                    sp.dma_start(vecs[:, i, :], row_bcast(A["L0_gnn_" + name])).then_inc(load, 16)
                sp.dma_start(b1[:, :], A["L0_gnn_b1"].rearrange("(c a) -> c a", a=1)).then_inc(load, 16)
                sp.wait_ge(load, 16 * 9)

            @block.gpsimd
            def _(pool):
                for i, z in enumerate([wq, wk]):
                    pool.memset(z[:, :, :, :], 0.0).then_inc(setup, 1)
                for i in range(2):
                    pool.memset(ks[i][:, :, :, :, :], 0.0).then_inc(setup, 1)
                    pool.memset(vs[i][:, :, :, :, :], 0.0).then_inc(setup, 1)
                pool.wait_ge(setup, 6)
                for h2 in range(2):
                    for i in range(2):
                        pool.memset(vs[i][64 * h2:64 * h2 + 64, :, :, h2, D0:D0 + 1], 1.0).then_inc(setup, 1)
                    pool.wait_ge(setup, 8 + 2 * h2)
                pool.wait_ge(load, 16 * 9)
                for n, w in enumerate([wq, wk]):
                    for j in range(2):
                        for f in range(2):
                            dst = w[:, j, f, :].rearrange("c (h f d) -> c h f d", h=4, f=2)[:, :, f, :]
                            src = wqkv[:, n * C + 64 * j:n * C + 64 * j + 64].rearrange("c (h d) -> c h d", h=4)
                            pool.tensor_copy(dst, src).then_inc(setup, 1)
                open_signals(pool, pool_signals)

            @block.vector
            def _(dve):
                dve.tensor_scalar(maskb[:, :], adj[:, :], 0.0, -4e9, ALU.is_le, ALU.mult)
                open_signals(dve, dve_signals)

            @block.scalar
            def _(act):
                open_signals(act, act_signals)

            @block.tensor
            def _(pe):
                open_signals(pe, pe_signals)

        def xg(i):
            return x[:, bass.ds(i * PG, PG), :]

        def xp(i, p):
            return x[:, bass.ds(i * PG + p, 1), :].rearrange("p a c -> p (a c)")

        with nc.Block() as block:
            @block.tensor
            def _(pe):
                xTv = xT[:, :].rearrange("c (p f n) -> c p f n", p=PG, f=2)

                def head_T(i, b):
                    if not runs(i):
                        return
                    pe.wait_ge(*xn_ready.now(i, PG - 1))
                    pe.wait_ge(*y1T_ready.before(i, turns=2))
                    for p in range(PG):
                        ins = pe.transpose(bT[:, 128 * p:128 * p + 128], xn[b][:, p, :], ident[:, :])
                    ins.then_inc(pe_xT.sem, 1)

                def head_q(i):
                    if not runs(i):
                        return
                    pe.wait_ge(*xT_ready.now(i))
                    pe.wait_ge(*ka_ready.before(i))
                    pe.wait_ge(*kd_ready.before(i))
                    pe.wait_ge(*v_ready.before(i))
                    for j, bank in enumerate([bQ0, bQ1]):
                        bv = bank[:, :].rearrange("c (p f n) -> c p f n", p=PG, f=2)
                        for f in range(2):
                            ins = pe.matmul(bv[:, :, f, :], wq[:, j, f, :], xTv[:, :, f, :], start=(f == 0), stop=True,
                                            skip_group_check=True)
                        ins.then_inc(pe_q.sem, 1)

                def head_k(i):
                    if not runs(i):
                        return
                    pe.wait_ge(*q_ready.now(i, 0))
                    kv = bQ0[:, :].rearrange("c (j p n) -> c j p n", j=2, p=PG)
                    for j in range(2):
                        for f in range(2):
                            ins = pe.matmul(kv[:, j, :, :], wk[:, j, f, :], xTv[:, :, f, :], start=(f == 0), stop=(f == 1),
                                            skip_group_check=True)
                    ins.then_inc(pe_k.sem, 1)

                def head_v(i):
                    if not runs(i):
                        return
                    pe.wait_ge(*q_ready.now(i, 1))
                    wv = wqkv[:, 2 * C:3 * C].rearrange("c (hp h2 d) -> c hp h2 d", hp=4, h2=2)
                    for fr in range(2 * PG):
                        for h2 in range(2):
                            ins = pe.matmul(bQ1[64 * h2:64 * h2 + 64, 64 * fr:64 * fr + 64], xT[:, 64 * fr:64 * fr + 64],
                                            wv[:, :, h2, :], start=(fr == 0), stop=True, skip_group_check=True)
                    ins.then_inc(pe_v.sem, 1)

                def scores(i, p, b):
                    if not runs(i):
                        return
                    bank = [bS0, bS1][p % 2]
                    pe.wait_ge(*kd_ready.now(i, 1))
                    pe.wait_ge(*ka_ready.now(i, 1))
                    pe.wait_ge(*s_ready.now(i, p - 2))
                    mk = bass.AP(maskb, 0, [maskb[:, :].ap[0], [0, H0], [1, NODES]])
                    pe.matmul(bank[:, :], identb[:, :], mk, start=True, stop=False, skip_group_check=True)
                    for j in range(2):
                        ins = pe.matmul(bank[:, 256 * j:256 * j + 256], qs[b][:, j, p, :, :].rearrange("c f n -> c (f n)"),
                                        ks[b][:, j, p, :, :].rearrange("c h m -> c (h m)"), start=False, stop=True,
                                        skip_group_check=True)
                    ins.then_inc(pe_s.sem, 1)

                def probs_T(i, p):
                    if not runs(i):
                        return
                    pe.wait_ge(*e_ready.now(i, p))
                    pe.wait_ge(*pt_ready.now(i, p - 1))
                    for hp in range(4):
                        ins = pe.transpose(bPT[:, 128 * hp:128 * hp + 128],
                                           s[:, p % 2, 2 * hp:2 * hp + 2, :].rearrange("p h m -> p (h m)"), ident[:, :])
                    ins.then_inc(pe_pt.sem, 1)

                def mix(i, p, b):
                    if not runs(i):
                        return
                    pe.wait_ge(*pt_ready.now(i, p))
                    pe.wait_ge(*v_ready.now(i, 1))
                    pe.wait_ge(*o_ready.now(i, p - 1))
                    w = 2 * (D0 + 1)
                    for f in range(2):
                        for hp in range(4):
                            ins = pe.matmul(bO[64 * f:64 * f + 64, w * hp:w * hp + w],
                                            pt[:, p % 2, hp, 64 * f:64 * f + 64],
                                            vs[b][:, 2 * p + f, hp, :, :].rearrange("m h d -> m (h d)"),
                                            start=(hp == 0), stop=True, skip_group_check=True)
                    ins.then_inc(pe_o.sem, 1)

                def ffn_T(i):
                    if not runs(i):
                        return
                    pe.wait_ge(*y1_ready.now(i))
                    if runs(i + 1):
                        pe.wait_ge(*xT_ready.now(i + 1))
                    for p in range(PG):
                        ins = pe.transpose(bT[:, 128 * p:128 * p + 128], y1[:, p, :], ident[:, :])
                    ins.then_inc(pe_y1T.sem, 1)

                def ffn_1(i):
                    if not runs(i):
                        return
                    pe.wait_ge(*y1T_ready.now(i))
                    pe.wait_ge(*u_ready.before(i))
                    pe.matmul(bF[:, :], w1[:, :], y1T[:, :], start=True, stop=True).then_inc(pe_h.sem, 1)

                def ffn_2(i):
                    if not runs(i):
                        return
                    pe.wait_ge(*hT_ready.now(i))
                    for p in range(PG):
                        ins = pe.matmul(bF[:, 128 * p:128 * p + 128], hT[:, 128 * p:128 * p + 128], w2[:, :],
                                        start=(p == 0), stop=True, skip_group_check=True)
                    ins.then_inc(pe_f.sem, 1)

                def step(g, b):
                    scores(g, 0, b)
                    scores(g, 1, b)
                    probs_T(g, 0)
                    mix(g, 0, b)
                    scores(g, 2, b)
                    probs_T(g, 1)
                    mix(g, 1, b)
                    scores(g, 3, b)
                    ffn_T(g - 1)
                    probs_T(g, 2)
                    mix(g, 2, b)
                    head_T(g + 1, 1 - b)
                    ffn_1(g - 1)
                    probs_T(g, 3)
                    head_q(g + 1)
                    mix(g, 3, b)
                    head_k(g + 1)
                    ffn_2(g - 1)
                    head_v(g + 1)
                skewed(pe, step)

            @block.scalar
            def _(act):
                def head_xT(i):
                    if not runs(i):
                        return
                    act.wait_ge(*pe_xT.now(i))
                    act.wait_ge(*pe_v.before(i))
                    act.activation(xT[:, :], bT[:, :], ACT.Copy).then_inc(xT_ready.sem, 1)

                def head_q(i, b):
                    if not runs(i):
                        return
                    for j, bank in enumerate([bQ0, bQ1]):
                        act.wait_ge(*pe_q.now(i, j))
                        act.wait_ge(*pe_s.before(i, turns=2))
                        act.activation(qs[b][:, j, :, :, :].rearrange("c p f n -> c (p f n)"), bank[:, :], ACT.Copy)\
                           .then_inc(q_ready.sem, 1)

                def head_k(i, b):
                    if not runs(i):
                        return
                    kv = bQ0[:, :].rearrange("c (j p n) -> c j p n", j=2, p=PG)
                    act.wait_ge(*kd_ready.now(i, 1))
                    for h4 in (2, 3):
                        r = slice(32 * h4, 32 * h4 + 32)
                        act.activation(ks[b][r, :, :, h4, :], kv[r, :, :, :], ACT.Copy).then_inc(ka_ready.sem, 1)

                def exp(i, p):
                    if not runs(i):
                        return
                    act.wait_ge(*s_ready.now(i, p))
                    act.activation(s[:, p % 2, :, :], s[:, p % 2, :, :], ACT.Exp, scale=0.25).then_inc(e_ready.sem, 1)

                def probs_T(i, p):
                    if not runs(i):
                        return
                    act.wait_ge(*pe_pt.now(i, p))
                    act.wait_ge(*pe_o.now(i, p - 2))
                    act.activation(pt[:, p % 2, :, :].rearrange("m h n -> m (h n)"), bPT[:, :], ACT.Copy)\
                       .then_inc(pt_ready.sem, 1)

                def ffn_T(i):
                    if not runs(i):
                        return
                    act.wait_ge(*pe_y1T.now(i))
                    act.wait_ge(*pe_h.before(i))
                    act.activation(y1T[:, :], bT[:, :], ACT.Copy).then_inc(y1T_ready.sem, 1)

                def ffn_h(i):
                    if not runs(i):
                        return
                    act.wait_ge(*pe_h.now(i))
                    act.wait_ge(*pe_f.before(i))
                    act.activation(hT[:, :], bF[:, :], ACT.Relu, bias=b1[:, 0:1]).then_inc(hT_ready.sem, 1)

                def step(g, b):
                    exp(g, 0)
                    probs_T(g, 0)
                    exp(g, 1)
                    probs_T(g, 1)
                    exp(g, 2)
                    ffn_T(g - 1)
                    exp(g, 3)
                    probs_T(g, 2)
                    head_xT(g + 1)
                    ffn_h(g - 1)
                    probs_T(g, 3)
                    head_q(g + 1, 1 - b)
                    head_k(g + 1, 1 - b)
                skewed(act, step)

            @block.vector
            def _(dve):
                def head_stats(i):
                    if runs(i):
                        norm_stats(dve, lambda p: xp(i, p), st6, mv, ve, bn0, ag0, ve0, i, EPS_LN, [rs0_ready.before(i)], gate)

                def head_xn(i, b):
                    if not runs(i):
                        return
                    dve.wait_ge(*rs0_ready.now(i))
                    dve.wait_ge(*pe_xT.before(i, turns=2))
                    dve.wait_ge(*t_ready.before(i, turns=2))
                    for p in range(PG):
                        dve.tensor_scalar(xn[b][:, p, :], xp(i, p), mv[:, p:p + 1], rs[:, p:p + 1],
                                          ALU.subtract, ALU.mult).then_inc(xn_ready.sem, 1)

                def head_kv(i, b):
                    if not runs(i):
                        return
                    kv = bQ0[:, :].rearrange("c (j p n) -> c j p n", j=2, p=PG)
                    dve.wait_ge(*pe_k.now(i))
                    dve.wait_ge(*pe_s.before(i, turns=2))
                    for h4 in (0, 1):
                        r = slice(32 * h4, 32 * h4 + 32)
                        dve.tensor_copy(ks[b][r, :, :, h4, :], kv[r, :, :, :]).then_inc(kd_ready.sem, 1)
                    dve.wait_ge(*pe_o.before(i, turns=2))
                    dve.wait_ge(*pe_v.now(i))
                    bv = bQ1[:, :].rearrange("m (f hp d) -> m f hp d", f=2 * PG, hp=4)
                    for h2 in range(2):
                        r = slice(64 * h2, 64 * h2 + 64)
                        dve.tensor_copy(vs[b][r, :, :, h2, 0:D0], bv[r, :, :, :]).then_inc(v_ready.sem, 1)

                def soft(i, p):
                    if not runs(i):
                        return
                    bank = [bS0, bS1][p % 2]
                    bv = bank[:, :].rearrange("p (h m) -> p h m", h=H0)
                    dve.wait_ge(*pe_s.now(i, p))
                    dve.wait_ge(*s_ready.now(i, p - 2))
                    dve.tensor_reduce(mx[:, p % 2, :], bv, AX.X, ALU.max).then_inc(mx_ready.sem, 1)
                    dve.wait_ge(*mx_ready.now(i, p))
                    dve.wait_ge(*pe_pt.now(i, p - 2))
                    m = mx[:, p % 2, :]
                    dve.tensor_tensor(s[:, p % 2, :, :], bv, bass.AP(m.tensor, m.offset, [m.ap[0], [1, H0], [0, NODES]]),
                                      ALU.subtract).then_inc(s_ready.sem, 1)

                def norm(i, p, b):
                    if not runs(i):
                        return
                    bv = bO[:, 0:H0 * (D0 + 1)].rearrange("n (h d) -> n h d", h=H0)
                    dve.wait_ge(*pe_o.now(i, p))
                    dve.wait_ge(*o_ready.now(i, p - 2))
                    dve.reciprocal(rc[:, p % 2, :], bv[:, :, D0]).then_inc(rc_ready.sem, 1)
                    dve.wait_ge(*rc_ready.now(i, p))
                    if p == 0:
                        dve.wait_ge(*y1m.before(i, turns=2))
                    m = rc[:, p % 2, :]
                    dve.tensor_tensor(ts[b][:, p, :].rearrange("n (h d) -> n h d", h=H0), bv[:, :, 0:D0],
                                      bass.AP(m.tensor, m.offset, [m.ap[0], [1, H0], [0, D0]]), ALU.mult)\
                       .then_inc(o_ready.sem, 1)

                def ffn_stats(i, b):
                    if not runs(i):
                        return
                    dve.wait_ge(*o_ready.now(i, PG - 1))
                    dve.tensor_tensor(ts[b][:, :, :], ts[b][:, :, :], xn[b][:, :, :], ALU.add).then_inc(t_ready.sem, 1)
                    norm_stats(dve, lambda p: ts[b][:, p, :], st61, mv1, ve1, bn1, ag1, vs1, i, EPS_LN,
                               [t_ready.now(i), rs1_ready.before(i)])

                def ffn_norm(i, b):
                    if not runs(i):
                        return
                    dve.wait_ge(*rs1_ready.now(i))
                    for p in range(PG):
                        dve.tensor_scalar(ts[b][:, p, :], ts[b][:, p, :], mv1[:, p:p + 1], rs1[:, p:p + 1],
                                          ALU.subtract, ALU.mult).then_inc(n1_ready.sem, 1)

                def last_stats(i):
                    if not runs(i):
                        return
                    dve.wait_ge(*pe_f.now(i))
                    dve.wait_ge(*y1b_ready.now(i))
                    dve.wait_ge(*fin.before(i))
                    dve.tensor_tensor(u[:, :, :], bF[:, :].rearrange("p (t c) -> p t c", t=PG), y1b[:, :, :], ALU.add)\
                       .then_inc(u_ready.sem, 1)
                    norm_stats(dve, lambda p: u[:, p, :], st62, mv2, ve2, bn2, ag2, vs2, i, EPS_LN,
                               [u_ready.now(i), rs2_ready.before(i)])

                def last_norm(i):
                    if not runs(i):
                        return
                    dve.wait_ge(*rs2_ready.now(i))
                    for p in range(PG):
                        dve.tensor_scalar(u[:, p, :], u[:, p, :], mv2[:, p:p + 1], rs2[:, p:p + 1],
                                          ALU.subtract, ALU.mult).then_inc(n2_ready.sem, 1)

                def step(g, b):
                    soft(g, 0)
                    last_stats(g - 2)
                    soft(g, 1)
                    ffn_stats(g - 1, 1 - b)
                    norm(g, 0, b)
                    soft(g, 2)
                    ffn_norm(g - 1, 1 - b)
                    head_stats(g + 1)
                    norm(g, 1, b)
                    soft(g, 3)
                    head_xn(g + 1, 1 - b)
                    norm(g, 2, b)
                    last_norm(g - 2)
                    norm(g, 3, b)
                    head_kv(g + 1, 1 - b)
                skewed(dve, step)

            @block.gpsimd
            def _(pool):
                def vec(i):
                    w = vecs[:, i, :]
                    return bass.AP(w.tensor, w.offset, [w.ap[0], [0, PG], [1, C]])

                def head_rs(i):
                    if not runs(i):
                        return
                    pool.wait_ge(*ve0.now(i))
                    pool.wait_ge(*xn_ready.before(i))
                    pool.tensor_tensor(rs[:, :], ve[:, :], half[:, 0:PG], ALU.pow).then_inc(rs0_ready.sem, 1)

                def ffn_rs(i):
                    if not runs(i):
                        return
                    pool.wait_ge(*vs1.now(i))
                    pool.wait_ge(*n1_ready.before(i))
                    pool.tensor_tensor(rs1[:, :], ve1[:, :], half[:, 0:PG], ALU.pow).then_inc(rs1_ready.sem, 1)

                def ffn_y1(i, b):
                    if not runs(i):
                        return
                    pool.wait_ge(*n1_ready.now(i, PG - 1))
                    pool.wait_ge(*pe_y1T.before(i))
                    pool.wait_ge(*y1b_ready.before(i))
                    pool.tensor_tensor(y1[:, :, :], ts[b][:, :, :], vec(0), ALU.mult).then_inc(y1m.sem, 1)
                    pool.wait_ge(*y1m.now(i))
                    pool.tensor_tensor(y1[:, :, :], y1[:, :, :], vec(1), ALU.add).then_inc(y1_ready.sem, 1)

                def ffn_y1b(i):
                    if not runs(i):
                        return
                    pool.wait_ge(*y1_ready.now(i))
                    pool.wait_ge(*u_ready.before(i))
                    pool.tensor_tensor(y1b[:, :, :], y1[:, :, :], vec(4), ALU.add).then_inc(y1b_ready.sem, 1)

                def last_rs(i):
                    if not runs(i):
                        return
                    pool.wait_ge(*vs2.now(i))
                    pool.wait_ge(*n2_ready.before(i))
                    pool.tensor_tensor(rs2[:, :], ve2[:, :], half[:, 0:PG], ALU.pow).then_inc(rs2_ready.sem, 1)

                def last_x(i):
                    if not runs(i):
                        return
                    pool.wait_ge(*n2_ready.now(i, PG - 1))
                    pool.tensor_tensor(u[:, :, :], u[:, :, :], vec(2), ALU.mult).then_inc(fin.sem, 1)
                    pool.wait_ge(*fin.now(i, 0))
                    pool.tensor_tensor(u[:, :, :], u[:, :, :], vec(3), ALU.add).then_inc(fin.sem, 1)
                    pool.wait_ge(*fin.now(i, 1))
                    pool.tensor_tensor(xg(i), xg(i), u[:, :, :], ALU.add).then_inc(fin.sem, 1)

                def step(g, b):
                    last_rs(g - 2)
                    ffn_rs(g - 1)
                    ffn_y1(g - 1, 1 - b)
                    head_rs(g + 1)
                    ffn_y1b(g - 1)
                    last_x(g - 2)
                skewed(pool, step)
        clear_taken(nc)


class Routing:

    def __init__(self, ctx, nc, name, consts, state):
        def sb(n, shape, dt=F32):
            return ctx.enter_context(nc.sbuf_tensor(f"{name}_{n}", shape, dt))

        def sig(n, per=1):
            return Signal(take_semaphore(ctx, nc, f"{name}_{n}"), per)

        self.c, self.state = consts, state
        self.lg = sb("lg", [128, PG, NE])
        self.eq = sb("eq", [128, PG, NE])
        self.m = sb("m", [128, 2, PG])
        self.key = sb("key", [128, 2, PG])
        self.oh = sb("oh", [128, 2, PG, NE])
        self.both = sb("both", [128, PG, NE], BF16)
        self.d = sb("d", [128, PG, NE + 1])
        self.e = sb("e", [128, PG, NE + 1])
        self.z = sb("z", [128, PG])
        self.den = sb("den", [128, PG])
        self.rows = sb("rows", [128, PG + 1, NE])
        self.pick = sb("pick", [128, 2, PG, NE])
        self.posf = sb("posf", [128, 2, PG])
        self.pos = sb("pos", [128, 2, PG], I32)
        self.step = sig("step", 12)
        self.both_ready = sig("both_ready")
        self.d_ready = sig("d_ready", 2)
        self.e_ready = sig("e_ready")
        self.wstep = sig("wstep", 6)
        self.pstep = sig("pstep", 6)
        self.pe_logits = sig("pe_logits")
        self.pe_rank = sig("pe_rank")
        self.gate = sig("gate")
        self.landed = take_semaphore(ctx, nc, f"{name}_landed")
        self.dve_signals = [self.step, self.both_ready, self.d_ready, self.wstep, self.pstep]
        self.act_signals = [self.e_ready]
        self.pe_signals = [self.pe_logits, self.pe_rank]
        self.tagged = sig("tagged", 2)
        self.pool_signals = [self.tagged]

    def tensor_logits(self, pe, g, bank, flatT, wr):
        for p in range(PG):
            i = pe.matmul(bank[:, NE * p:NE * p + NE], flatT[:, 128 * p:128 * p + 128], wr[:, :],
                          start=(p == 0), stop=True, skip_group_check=True)
        i.then_inc(self.pe_logits.sem, 1)

    def tensor_rank(self, pe, g, bank):
        pe.wait_ge(*self.both_ready.now(g))
        pe.wait_ge(*self.step.now(g, 0))
        r = bank[:, 64:64 + NE * (PG + 1)]
        pe.matmul(r[:, 0:NE * PG], self.c["tri"][:, :], self.both[:, :, :].rearrange("t p e -> t (p e)"),
                  start=True, stop=False, skip_group_check=True)
        for q in range(PG):
            m = self.both[:, q, :]
            i = pe.matmul(r[:, NE * (q + 1):NE * (PG + 1)], self.c["ones"][:, :],
                          bass.AP(m.tensor, m.offset, [m.ap[0], [0, PG - q], [1, NE]]),
                          start=False, stop=(q == PG - 1), skip_group_check=True)
        i.then_inc(self.pe_rank.sem, 1)

    def vector_choose(self, dve, g, bank, with_z):
        c = self.c

        def over_e(ap):
            return bass.AP(ap.tensor, ap.offset, [ap.ap[0], [1, PG], [0, NE]])

        rev = bass.AP(c["rev"], 0, [c["rev"][:, :].ap[0], [0, PG], [1, NE]])
        s = self.step
        dve.wait_ge(*self.pe_logits.now(g))
        dve.wait_ge(*self.wstep.before(g))
        bv = bank[:, 0:NE * PG].rearrange("t (p e) -> t p e", p=PG)
        if self.state.get("bias") is not None:
            b = self.state["bias"]
            dve.tensor_tensor(self.lg[:, :, :], bv, bass.AP(b, 0, [b[:, :].ap[0], [0, PG], [1, NE]]), ALU.add)\
               .then_inc(s.sem, 1)
        else:
            dve.tensor_copy(self.lg[:, :, :], bv).then_inc(s.sem, 1)
        src = self.lg[:, :, :]
        n = 1
        for k in range(2):
            dve.wait_ge(*s.now(g, n - 1))
            if k == 0:
                dve.wait_ge(*self.tagged.before(g))
            dve.tensor_reduce(self.m[:, k, :], src, AX.X, ALU.max).then_inc(s.sem, 1)
            dve.wait_ge(*s.now(g, n))
            dve.tensor_tensor(self.eq[:, :, :], src, over_e(self.m[:, k, :]), ALU.is_equal).then_inc(s.sem, 1)
            dve.wait_ge(*s.now(g, n + 1))
            dve.tensor_tensor(self.eq[:, :, :], self.eq[:, :, :], rev, ALU.mult).then_inc(s.sem, 1)
            dve.wait_ge(*s.now(g, n + 2))
            dve.tensor_reduce(self.key[:, k, :], self.eq[:, :, :], AX.X, ALU.max).then_inc(s.sem, 1)
            dve.wait_ge(*s.now(g, n + 3))
            if k == 0:
                dve.wait_ge(*self.pstep.before(g))
            dve.tensor_tensor(self.oh[:, k, :, :], rev, over_e(self.key[:, k, :]), ALU.is_equal).then_inc(s.sem, 1)
            n += 5
            if k == 0:
                dve.wait_ge(*s.now(g, n - 1))
                dve.scalar_tensor_tensor(out=self.eq[:, :, :].rearrange("t p e -> t (p e)"),
                                         in0=self.oh[:, 0, :, :].rearrange("t p e -> t (p e)"), scalar=-1e30,
                                         in1=self.lg[:, :, :].rearrange("t p e -> t (p e)"),
                                         op0=ALU.mult, op1=ALU.add).then_inc(s.sem, 1)
                n += 1
                src = self.eq[:, :, :]
        dve.wait_ge(*s.now(g, n - 1))
        dve.wait_ge(*self.pe_rank.before(g))
        dve.tensor_tensor(self.both[:, :, :], self.oh[:, 0, :, :], self.oh[:, 1, :, :], ALU.add)\
           .then_inc(self.both_ready.sem, 1)
        dve.wait_ge(*self.e_ready.before(g))
        dve.tensor_tensor(self.d[:, :, NE], self.m[:, 1, :], self.m[:, 0, :], ALU.subtract).then_inc(self.d_ready.sem, 1)
        if with_z:
            dve.tensor_tensor(self.d[:, :, 0:NE], self.lg[:, :, :], over_e(self.m[:, 0, :]), ALU.subtract)\
               .then_inc(self.d_ready.sem, 1)
        else:
            dve.tensor_copy(self.d[:, :, 0:NE], self.lg[:, :, :]).then_inc(self.d_ready.sem, 1)

    def scalar_exp(self, act, g, with_z):
        act.wait_ge(*self.d_ready.now(g, 1))
        act.wait_ge(*self.wstep.before(g))
        lo = 0 if with_z else NE
        act.activation(self.e[:, :, lo:NE + 1], self.d[:, :, lo:NE + 1], ACT.Exp).then_inc(self.e_ready.sem, 1)

    def vector_weights(self, dve, g, with_z):
        w = self.state["w"]
        s = self.wstep
        dve.wait_ge(*self.e_ready.now(g))
        e2 = self.e[:, :, NE]
        if with_z:
            dve.tensor_reduce(self.z[:, :], self.e[:, :, 0:NE], AX.X, ALU.add).then_inc(s.sem, 1)
            dve.wait_ge(*s.now(g, 0))
            dve.scalar_tensor_tensor(out=self.den[:, :], in0=self.z[:, :], scalar=1e-9, in1=e2,
                                     op0=ALU.mult, op1=ALU.add).then_inc(s.sem, 1)
        else:
            dve.tensor_copy(self.z[:, :], e2).then_inc(s.sem, 1)
            dve.wait_ge(*s.now(g, 0))
            dve.tensor_copy(self.den[:, :], self.z[:, :]).then_inc(s.sem, 1)
        dve.wait_ge(*s.now(g, 1))
        dve.tensor_scalar(self.den[:, :], self.den[:, :], 1.0, None, ALU.add).then_inc(s.sem, 1)
        dve.wait_ge(*s.now(g, 2))
        dve.reciprocal(self.z[:, :], self.den[:, :]).then_inc(s.sem, 1)
        dve.wait_ge(*s.now(g, 3))
        dve.tensor_copy(w[:, 0, bass.ds(g * PG, PG)], self.z[:, :]).then_inc(s.sem, 1)
        dve.tensor_tensor(w[:, 1, bass.ds(g * PG, PG)], self.z[:, :], e2, ALU.mult).then_inc(s.sem, 1)

    def vector_rows(self, dve, g, bank):
        base = self.state["base"]
        s = self.pstep
        dve.wait_ge(*self.pe_rank.now(g))
        dve.wait_ge(*s.before(g))
        b = base[:, :]
        dve.tensor_tensor(self.rows[:, :, :], bank[:, 64:64 + NE * (PG + 1)].rearrange("t (p e) -> t p e", e=NE),
                          bass.AP(b.tensor, b.offset, [b.ap[0], [0, PG + 1], [1, NE]]), ALU.add).then_inc(s.sem, 1)
        dve.wait_ge(*s.now(g, 0))
        dve.tensor_copy(base[:, :], self.rows[:, PG, :]).then_inc(s.sem, 1)
        for k in range(2):
            dve.tensor_tensor(self.pick[:, k, :, :], self.oh[:, k, :, :], self.rows[:, 0:PG, :], ALU.mult).then_inc(s.sem, 1)
        dve.wait_ge(*s.now(g, 3))
        dve.tensor_reduce(self.posf[:, :, :], self.pick[:, :, :, :], AX.X, ALU.add).then_inc(s.sem, 1)
        dve.wait_ge(*s.now(g, 4))
        self.wait_landed(dve, g - 1)
        dve.tensor_copy(self.pos[:, :, :], self.posf[:, :, :]).then_inc(s.sem, 1)

    def wait_landed(self, eng, i):
        if not isinstance(i, int) or i >= 0:
            eng.wait_ge(self.landed, (i + 1) * (16 * 2 * PG))

    def pool_scatter(self, pool, g, flat, dest):
        pool.wait_ge(*self.tagged.before(g, turns=2))
        pool.wait_ge(*self.step.now(g, 4))
        pool.sem_inc(self.gate.sem, 1)
        pool.tensor_copy(flat[:, :, C], self.c["ids"][:, bass.ds(g * PG, PG)]).then_inc(self.tagged.sem, 1)
        pool.tensor_copy(flat[:, :, C + 1], self.key[:, 0, :]).then_inc(self.tagged.sem, 1)
        pool.wait_ge(*self.pstep.now(g, 5))
        pool.wait_ge(*self.tagged.now(g, 1))
        pool.sem_inc(self.gate.sem, 1)
        for p in range(PG):
            for k in range(2):
                pool.indirect_dma_start(out=dest, out_offset=bass.IndirectOffsetOnAxis(ap=self.pos[:, k, p:p + 1], axis=0),
                                        in_=flat[:, p, :], in_offset=None).then_inc(self.landed, 16)


def phase_attn1(nc, A, x, banks, c, state, dest):
    ident, identb, half = c["ident"], c["identb"], c["half"]
    with ExitStack() as ctx:
        def sb(name, shape, dt=F32):
            return ctx.enter_context(nc.sbuf_tensor("a1_" + name, shape, dt))

        def sig(name, per=1):
            return Signal(take_semaphore(ctx, nc, "a1_" + name), per)

        FR = 2 * PG
        wq = sb("wq", [128, 2, 128])
        wk = sb("wk", [128, 2, 128])
        wv = sb("wv", [128, 64])
        wo = sb("wo", [128, 128])
        wr = sb("wr", [128, NE])
        lnw = sb("lnw", [128, 1])
        ln2w = sb("ln2w", [128, C])
        rope = sb("rope", [128, 2, NODES])
        causal = sb("causal", [128, NODES], BF16)
        causal32 = sb("causal32", [128, NODES])
        st = sb("st", [128, PG, 11]); mean = sb("mean", [128, PG]); ve = sb("ve", [128, PG]); rs = sb("rs", [128, PG])
        rr = sb("rr", [128, 4, PG])
        ms = sb("ms", [128, 3, PG])
        vn = [sb(f"vn{i}", [128, PG, C]) for i in range(2)]
        h = sb("h", [128, PG, C])
        hT = sb("hT", [128, GT])
        q1, q2, q = sb("q1", [128, FR, NODES]), sb("q2", [128, FR, NODES]), sb("q", [128, FR, NODES])
        k1, k2 = sb("k1", [128, FR, NODES]), sb("k2", [128, FR, NODES])
        k = sb("k", [128, FR, H1, NODES])
        v = sb("v", [128, FR, KV1, 2, D1 + 1])
        s = sb("s", [128, 2, 2, H1, NODES])
        mx = sb("mx", [128, 2, 2, H1])
        pt = sb("pt", [128, 2, 2, KV1, 128])
        rc = sb("rc", [128, 2, 2, H1])
        y = sb("y", [128, PG, C])
        yT = sb("yT", [128, GT])
        x2 = sb("x2", [128, PG, C])
        sq = sb("sq", [128, PG, C])
        flat = [sb(f"flat{i}", [128, PG, ROW]) for i in range(2)]
        fT = sb("fT", [128, GT])
        gate = sig("gate")
        load = take_semaphore(ctx, nc, "a1_load")
        setup = take_semaphore(ctx, nc, "a1_setup")
        R = Routing(ctx, nc, "a1r", c, state)

        bn, part, vs = sig("bn", PG), sig("part", 6), sig("vs")
        vn_ready, h_ready = sig("vn_ready", PG), sig("h_ready", PG)
        rms_in = sig("rms_in", 3)
        rope_q, rope_k = sig("rope_q", 2), sig("rope_k", 2)
        q_ready, kd_ready = sig("q_ready"), sig("kd_ready", 2)
        mx_ready, s_ready = sig("mx_ready", 2), sig("s_ready", 2)
        rc_ready, y_ready = sig("rc_ready", 2), sig("y_ready", 2)
        x2_ready, ms_ready = sig("x2_ready"), sig("ms_ready", 2)
        f0_ready, flat_ready = sig("f0_ready", PG), sig("flat_ready")
        dve_signals = [bn, part, vs, vn_ready, h_ready, rms_in, rope_q, rope_k, q_ready, kd_ready, mx_ready, s_ready,
                       rc_ready, y_ready, x2_ready, ms_ready, f0_ready, flat_ready] + R.dve_signals
        hT_ready, v_ready, e_ready, pt_ready = sig("hT_ready"), sig("v_ready", 2), sig("e_ready", 2), sig("pt_ready", 2)
        yT_ready, fT_ready = sig("yT_ready"), sig("fT_ready")
        act_signals = [hT_ready, v_ready, e_ready, pt_ready, yT_ready, fT_ready] + R.act_signals
        rs_ready, r2_ready, rh_ready = sig("rs_ready"), sig("r2_ready"), sig("rh_ready")
        kp_ready, sq_ready, rms2_ready, fin = sig("kp_ready", 2), sig("sq_ready"), sig("rms2_ready"), sig("fin")
        pool_signals = [rs_ready, r2_ready, rh_ready, kp_ready, sq_ready, rms2_ready, fin]
        pe_hT, pe_q, pe_k, pe_v = sig("pe_hT"), sig("pe_q"), sig("pe_k"), sig("pe_v")
        pe_s, pe_pt, pe_o = sig("pe_s", 2), sig("pe_pt", 2), sig("pe_o", 2)
        pe_yT, pe_x, pe_fT = sig("pe_yT"), sig("pe_x"), sig("pe_fT")
        pe_signals = [pe_hT, pe_q, pe_k, pe_v, pe_s, pe_pt, pe_o, pe_yT, pe_x, pe_fT] + R.pe_signals
        bT, bQ, bQr, bK, bKr, bV, bR, bPT = banks
        S_BANKS = [bQ, bQr]
        PT_BANKS = [bPT, bQr]
        bO = bQ

        with nc.Block() as block:
            @block.sync
            def _(sp):
                n = 0
                for i, t in enumerate(["c_wq", "c_wq_x"]):
                    sp.dma_start(wq[:, i, :], A[t]).then_inc(load, 16)
                for i, t in enumerate(["c_wk", "c_wk_x"]):
                    sp.dma_start(wk[:, i, :], A[t]).then_inc(load, 16)
                sp.dma_start(wv[:, :], A["c_wv"]).then_inc(load, 16)
                sp.dma_start(wo[:, :], A["c_wo"]).then_inc(load, 16)
                sp.dma_start(wr[:, :], A["c_wr"]).then_inc(load, 16)
                sp.dma_start(lnw[:, :], A["L0_ffn_ln1_w"].rearrange("(c a) -> c a", a=1)).then_inc(load, 16)
                sp.dma_start(ln2w[:, :], row_bcast(A["L0_ffn_ln2_w"])).then_inc(load, 16)
                sp.dma_start(rope[:, :, :], A["c_rope"]).then_inc(load, 16)
                sp.dma_start(causal32[:, :], A["c_causal"]).then_inc(load, 16)
                sp.wait_ge(load, 16 * 11)

            @block.gpsimd
            def _(pool):
                pool.memset(k[:, :, :, :], 0.0).then_inc(setup, 1)
                pool.memset(v[:, :, :, :, :], 0.0).then_inc(setup, 1)
                pool.wait_ge(setup, 2)
                for h2 in range(2):
                    pool.memset(v[64 * h2:64 * h2 + 64, :, :, h2, D1:D1 + 1], 1.0).then_inc(setup, 1)
                    pool.wait_ge(setup, 3 + h2)
                open_signals(pool, pool_signals)
                open_signals(pool, R.pool_signals)

            @block.vector
            def _(dve):
                dve.wait_ge(load, 16 * 11)
                dve.tensor_copy(causal[:, :], causal32[:, :])
                dve.wait_ge(load, 16 * 11)
                for w in [wq[:, :, :], wk[:, :, :], wv[:, :]]:
                    dve.tensor_scalar(w, w, lnw[:, 0:1], None, ALU.mult)
                dve.tensor_scalar(state["base"][:, :], c["rev"][:, :], -float(CAP), float(NE * CAP), ALU.mult, ALU.add)
                open_signals(dve, dve_signals)

            @block.scalar
            def _(act):
                open_signals(act, act_signals)

            @block.tensor
            def _(pe):
                open_signals(pe, pe_signals)

        def xt(i, p):
            return x[:, bass.ds(i * PG + p, 1), :].rearrange("p a c -> p (a c)")

        with nc.Block() as block:
            @block.tensor
            def _(pe):
                def head_T(i):
                    if not runs(i):
                        return
                    pe.wait_ge(*h_ready.now(i, PG - 1))
                    pe.wait_ge(*yT_ready.before(i, turns=2))
                    for p in range(PG):
                        ins = pe.transpose(bT[:, 128 * p:128 * p + 128], h[:, p, :], ident[:, :])
                    ins.then_inc(pe_hT.sem, 1)

                def head_k(i):
                    if not runs(i):
                        return
                    pe.wait_ge(*hT_ready.now(i))
                    pe.wait_ge(*rope_k.before(i))
                    for n, bank in enumerate([bK, bKr]):
                        ins = pe.matmul(bank[:, :], wk[:, n, :], hT[:, :], start=True, stop=True)
                    ins.then_inc(pe_k.sem, 1)

                def head_v(i):
                    if not runs(i):
                        return
                    pe.wait_ge(*x2_ready.before(i, turns=2))
                    for fr in range(FR):
                        for h2 in range(2):
                            ins = pe.matmul(bV[64 * h2:64 * h2 + 64, 64 * fr:64 * fr + 64], hT[:, 64 * fr:64 * fr + 64],
                                            wv[:, :], start=(fr == 0), stop=True, skip_group_check=True)
                    ins.then_inc(pe_v.sem, 1)

                def head_q(i):
                    if not runs(i):
                        return
                    pe.wait_ge(*s_ready.before(i))
                    pe.wait_ge(*pt_ready.before(i))
                    pe.wait_ge(*y_ready.before(i))
                    for n, bank in enumerate([bQ, bQr]):
                        ins = pe.matmul(bank[:, :], wq[:, n, :], hT[:, :], start=True, stop=True)
                    ins.then_inc(pe_q.sem, 1)

                def scores(i):
                    if not runs(i):
                        return
                    pe.wait_ge(*kd_ready.now(i, 1))
                    pe.wait_ge(*kp_ready.now(i, 1))
                    pe.wait_ge(*q_ready.now(i))
                    for u in range(2):
                        mk = bass.AP(causal, 0, [causal[:, :].ap[0], [0, 2 * H1], [1, NODES]])
                        pe.matmul(S_BANKS[u][:, :], identb[:, :], mk, start=True, stop=False, skip_group_check=True)
                        for fr in range(4):
                            f, pr = fr % 2, fr // 2
                            ins = pe.matmul(S_BANKS[u][64 * f:64 * f + 64, 256 * pr:256 * pr + 256], q[:, 4 * u + fr, :],
                                            k[:, 4 * u + fr, :, :].rearrange("c h m -> c (h m)"), start=False, stop=True,
                                            skip_group_check=True)
                        ins.then_inc(pe_s.sem, 1)

                def probs_T(i, u):
                    if not runs(i):
                        return
                    pe.wait_ge(*e_ready.now(i, u))
                    pe.wait_ge(*(pt_ready.before(i, 0) if u == 0 else s_ready.now(i, 1)))
                    for pr in range(2):
                        for kv in range(KV1):
                            n = 2 * pr + kv
                            ins = pe.transpose(PT_BANKS[u][:, 128 * n:128 * n + 128],
                                               s[:, u, pr, 2 * kv:2 * kv + 2, :].rearrange("n h m -> n (h m)"), ident[:, :])
                    ins.then_inc(pe_pt.sem, 1)

                def mix(i, u):
                    if not runs(i):
                        return
                    pe.wait_ge(*v_ready.now(i, 1))
                    pe.wait_ge(*pt_ready.now(i, u))
                    pe.wait_ge(*(s_ready.now(i, 0) if u == 0 else y_ready.now(i, 0)))
                    w = 2 * (D1 + 1)
                    for pr in range(2):
                        for kv in range(KV1):
                            for f in range(2):
                                o = w * (KV1 * pr + kv)
                                ins = pe.matmul(bO[64 * f:64 * f + 64, o:o + w], pt[:, u, pr, kv, 64 * f:64 * f + 64],
                                                v[:, 4 * u + 2 * pr + f, kv, :, :].rearrange("m h d -> m (h d)"),
                                                start=(pr == 0 and kv == 0), stop=True, skip_group_check=True)
                    ins.then_inc(pe_o.sem, 1)

                def out_T(i):
                    if not runs(i):
                        return
                    pe.wait_ge(*y_ready.now(i, 1))
                    pe.wait_ge(*fT_ready.before(i))
                    for p in range(PG):
                        ins = pe.transpose(bT[:, 128 * p:128 * p + 128], y[:, p, :], ident[:, :])
                    ins.then_inc(pe_yT.sem, 1)

                def out_product(i):
                    if not runs(i):
                        return
                    pe.wait_ge(*yT_ready.now(i))
                    if runs(i + 1):
                        pe.wait_ge(*v_ready.now(i + 1, 1))
                    for p in range(PG):
                        ins = pe.matmul(bV[:, 128 * p:128 * p + 128], yT[:, 128 * p:128 * p + 128], wo[:, :],
                                        start=(p == 0), stop=True, skip_group_check=True)
                    ins.then_inc(pe_x.sem, 1)

                def flat_T(i, b):
                    if not runs(i):
                        return
                    pe.wait_ge(*flat_ready.now(i))
                    if runs(i + 2):
                        pe.wait_ge(*hT_ready.now(i + 2))
                    for p in range(PG):
                        ins = pe.transpose(bT[:, 128 * p:128 * p + 128], flat[b][:, p, 0:C], ident[:, :])
                    ins.then_inc(pe_fT.sem, 1)

                def logits(i):
                    if not runs(i):
                        return
                    pe.wait_ge(*fT_ready.now(i))
                    pe.wait_ge(*R.pstep.before(i, 0))
                    R.tensor_logits(pe, i, bR, fT, wr)

                def step(g, b):
                    scores(g)
                    out_T(g - 1)
                    out_product(g - 1)
                    probs_T(g, 0)
                    probs_T(g, 1)
                    head_T(g + 1)
                    mix(g, 0)
                    head_k(g + 1)
                    if runs(g - 2):
                        R.tensor_rank(pe, g - 2, bR)
                    head_v(g + 1)
                    mix(g, 1)
                    flat_T(g - 1, 1 - b)
                    head_q(g + 1)
                    logits(g - 1)
                skewed(pe, step)

            @block.scalar
            def _(act):
                def head_T(i):
                    if not runs(i):
                        return
                    act.wait_ge(*pe_hT.now(i))
                    act.wait_ge(*pe_q.before(i))
                    act.activation(hT[:, :], bT[:, :], ACT.Copy).then_inc(hT_ready.sem, 1)

                def head_v(i):
                    if not runs(i):
                        return
                    act.wait_ge(*pe_v.now(i))
                    act.wait_ge(*pe_o.before(i))
                    bv = bV[:, :].rearrange("m (f kv d) -> m f kv d", f=FR, kv=KV1)
                    for h2 in range(2):
                        r = slice(64 * h2, 64 * h2 + 64)
                        act.activation(v[r, :, :, h2, 0:D1], bv[r, :, :, :], ACT.Copy).then_inc(v_ready.sem, 1)

                def exp(i, u):
                    if not runs(i):
                        return
                    act.wait_ge(*s_ready.now(i, u))
                    su = s[:, u, :, :, :].rearrange("n p h m -> n (p h m)")
                    act.activation(su, su, ACT.Exp, scale=float(D1) ** -0.5).then_inc(e_ready.sem, 1)

                def probs_T(i, u):
                    if not runs(i):
                        return
                    act.wait_ge(*pe_pt.now(i, u))
                    act.wait_ge(*pe_o.before(i, u))
                    act.activation(pt[:, u, :, :, :].rearrange("m p k n -> m (p k n)"), PT_BANKS[u][:, :], ACT.Copy)\
                       .then_inc(pt_ready.sem, 1)

                def out_T(i):
                    if not runs(i):
                        return
                    act.wait_ge(*pe_yT.now(i))
                    act.wait_ge(*pe_x.before(i))
                    act.activation(yT[:, :], bT[:, :], ACT.Copy).then_inc(yT_ready.sem, 1)

                def flat_T(i):
                    if not runs(i):
                        return
                    act.wait_ge(*pe_fT.now(i))
                    act.wait_ge(*R.pe_logits.before(i))
                    act.activation(fT[:, :], bT[:, :], ACT.Copy).then_inc(fT_ready.sem, 1)

                def step(g, b):
                    out_T(g - 1)
                    exp(g, 0)
                    exp(g, 1)
                    probs_T(g, 0)
                    probs_T(g, 1)
                    head_T(g + 1)
                    if runs(g - 2):
                        R.scalar_exp(act, g - 2, True)
                    head_v(g + 1)
                    flat_T(g - 1)
                skewed(act, step)

            @block.vector
            def _(dve):
                def table(i, rows=slice(0, 128), n=FR):
                    t = rope[rows, i, :]
                    return bass.AP(t.tensor, t.offset, [t.ap[0], [0, n], [1, NODES]])

                def fview(bank):
                    return bank[:, :].rearrange("c (f n) -> c f n", f=FR)

                def head_stats(i):
                    if not runs(i):
                        return
                    norm_stats(dve, lambda p: xt(i, p), st, mean, ve, bn, part, vs, i, EPS_LN,
                               [rs_ready.before(i), rms_in.before(i)], gate)

                def head_vn(i, b):
                    if not runs(i):
                        return
                    dve.wait_ge(*rs_ready.now(i))
                    dve.wait_ge(*x2_ready.before(i, turns=2))
                    for p in range(PG):
                        dve.tensor_scalar(vn[b][:, p, :], xt(i, p), mean[:, p:p + 1], rs[:, p:p + 1],
                                          ALU.subtract, ALU.mult).then_inc(vn_ready.sem, 1)
                    dve.wait_ge(*vs.now(i))
                    dve.tensor_tensor(rr[:, 0, :], rs[:, :], rs[:, :], ALU.mult).then_inc(rms_in.sem, 1)
                    dve.wait_ge(*rms_in.now(i, 0))
                    dve.scalar_tensor_tensor(out=rr[:, 1, :], in0=ve[:, :], scalar=-EPS_LN, in1=rr[:, 0, :],
                                             op0=ALU.add, op1=ALU.mult).then_inc(rms_in.sem, 1)
                    dve.wait_ge(*rms_in.now(i, 1))
                    dve.wait_ge(*rh_ready.before(i))
                    dve.tensor_scalar(rr[:, 2, :], rr[:, 1, :], EPS_RMS, None, ALU.add).then_inc(rms_in.sem, 1)

                def head_h(i, b):
                    if not runs(i):
                        return
                    dve.wait_ge(*rh_ready.now(i))
                    dve.wait_ge(*vn_ready.now(i, PG - 1))
                    dve.wait_ge(*pe_hT.before(i))
                    for p in range(PG):
                        dve.tensor_scalar(h[:, p, :], vn[b][:, p, :], rr[:, 3, p:p + 1], None, ALU.mult).then_inc(h_ready.sem, 1)

                def rotate_k(i):
                    if not runs(i):
                        return
                    dve.wait_ge(*pe_k.now(i))
                    dve.wait_ge(*kd_ready.before(i))
                    dve.wait_ge(*kp_ready.before(i))
                    dve.tensor_tensor(k1[:, :, :], fview(bK), table(0), ALU.mult).then_inc(rope_k.sem, 1)
                    dve.tensor_tensor(k2[:, :, :], fview(bKr), table(1), ALU.mult).then_inc(rope_k.sem, 1)
                    dve.wait_ge(*rope_k.now(i, 1))
                    dve.wait_ge(*pe_s.before(i))
                    for h4 in (0, 1):
                        r = slice(32 * h4, 32 * h4 + 32)
                        dve.tensor_tensor(k[r, :, h4, :], k1[r, :, :], k2[r, :, :], ALU.add).then_inc(kd_ready.sem, 1)

                def rotate_q(i):
                    if not runs(i):
                        return
                    dve.wait_ge(*pe_q.now(i))
                    dve.wait_ge(*q_ready.before(i))
                    dve.tensor_tensor(q1[:, :, :], fview(bQ), table(0), ALU.mult).then_inc(rope_q.sem, 1)
                    dve.tensor_tensor(q2[:, :, :], fview(bQr), table(1), ALU.mult).then_inc(rope_q.sem, 1)
                    dve.wait_ge(*rope_q.now(i, 1))
                    dve.wait_ge(*pe_s.before(i))
                    dve.tensor_tensor(q[:, :, :], q1[:, :, :], q2[:, :, :], ALU.add).then_inc(q_ready.sem, 1)

                def soft(i, u):
                    if not runs(i):
                        return
                    sv = S_BANKS[u][:, :].rearrange("n (h m) -> n h m", m=NODES)
                    m = mx[:, u, :, :].rearrange("n p h -> n (p h)")
                    dve.wait_ge(*pe_s.now(i, u))
                    dve.wait_ge(*s_ready.before(i, u))
                    dve.tensor_reduce(m, sv, AX.X, ALU.max).then_inc(mx_ready.sem, 1)
                    dve.wait_ge(*mx_ready.now(i, u))
                    dve.wait_ge(*pe_pt.before(i, u))
                    dve.tensor_tensor(s[:, u, :, :, :].rearrange("n p h m -> n (p h) m"), sv,
                                      bass.AP(m.tensor, m.offset, [m.ap[0], [1, 2 * H1], [0, NODES]]), ALU.subtract)\
                       .then_inc(s_ready.sem, 1)

                def norm(i, u):
                    if not runs(i):
                        return
                    ov = bO[:, 0:2 * H1 * (D1 + 1)].rearrange("n (h d) -> n h d", d=D1 + 1)
                    m = rc[:, u, :, :].rearrange("n p h -> n (p h)")
                    dve.wait_ge(*pe_o.now(i, u))
                    dve.wait_ge(*y_ready.before(i, u))
                    dve.reciprocal(m, ov[:, :, D1]).then_inc(rc_ready.sem, 1)
                    dve.wait_ge(*rc_ready.now(i, u))
                    dve.wait_ge(*pe_yT.before(i))
                    dve.tensor_tensor(y[:, 2 * u:2 * u + 2, :].rearrange("n p (h d) -> n (p h) d", h=H1), ov[:, :, 0:D1],
                                      bass.AP(m.tensor, m.offset, [m.ap[0], [1, 2 * H1], [0, D1]]), ALU.mult)\
                       .then_inc(y_ready.sem, 1)

                def out_x2(i, b):
                    if not runs(i):
                        return
                    dve.wait_ge(*pe_x.now(i))
                    dve.wait_ge(*fin.before(i))
                    dve.wait_ge(*f0_ready.before(i))
                    dve.tensor_tensor(x2[:, :, :], bV[:, :].rearrange("n (p c) -> n p c", p=PG), vn[b][:, :, :], ALU.add)\
                       .then_inc(x2_ready.sem, 1)

                def out_ms(i):
                    if not runs(i):
                        return
                    dve.wait_ge(*sq_ready.now(i))
                    dve.wait_ge(*rms2_ready.before(i))
                    dve.tensor_reduce(ms[:, 0, :], sq[:, :, :], AX.X, ALU.add).then_inc(ms_ready.sem, 1)
                    dve.wait_ge(*ms_ready.now(i, 0))
                    dve.tensor_scalar(ms[:, 1, :], ms[:, 0, :], 1.0 / C, EPS_RMS, ALU.mult, ALU.add).then_inc(ms_ready.sem, 1)

                def out_flat(i, b):
                    if not runs(i):
                        return
                    dve.wait_ge(*rms2_ready.now(i))
                    dve.wait_ge(*pe_fT.before(i))
                    R.wait_landed(dve, i - 2)
                    w = ln2w[:, :]
                    for p in range(PG):
                        dve.scalar_tensor_tensor(out=flat[b][:, p, 0:C], in0=x2[:, p, :], scalar=ms[:, 2, p:p + 1], in1=w,
                                                 op0=ALU.mult, op1=ALU.mult).then_inc(f0_ready.sem, 1)
                    dve.wait_ge(*f0_ready.now(i, PG - 1))
                    dve.tensor_copy(ms[:, 1, 0:1], ms[:, 0, 0:1]).then_inc(flat_ready.sem, 1)

                def step(g, b):
                    head_stats(g + 1)
                    soft(g, 0)
                    soft(g, 1)
                    out_x2(g - 1, 1 - b)
                    head_vn(g + 1, 1 - b)
                    head_h(g + 1, 1 - b)
                    if runs(g - 2):
                        R.vector_choose(dve, g - 2, bR, True)
                    norm(g, 0)
                    out_ms(g - 1)
                    if runs(g - 2):
                        R.vector_rows(dve, g - 2, bR)
                    rotate_k(g + 1)
                    norm(g, 1)
                    out_flat(g - 1, 1 - b)
                    if runs(g - 2):
                        R.vector_weights(dve, g - 2, True)
                    rotate_q(g + 1)
                skewed(dve, step, first=4)

            @block.gpsimd
            def _(pool):
                def head_rs(i):
                    if not runs(i):
                        return
                    pool.wait_ge(*vs.now(i))
                    pool.wait_ge(*vn_ready.before(i))
                    pool.wait_ge(*rms_in.before(i, 0))
                    pool.tensor_tensor(rs[:, :], ve[:, :], half[:, 0:PG], ALU.pow).then_inc(rs_ready.sem, 1)

                def head_rh(i):
                    if not runs(i):
                        return
                    pool.wait_ge(*rms_in.now(i, 2))
                    pool.wait_ge(*h_ready.before(i))
                    pool.tensor_tensor(rr[:, 3, :], rr[:, 2, :], half[:, 0:PG], ALU.pow).then_inc(rh_ready.sem, 1)

                def rotate_k(i):
                    if not runs(i):
                        return
                    pool.wait_ge(*rope_k.now(i, 1))
                    pool.wait_ge(*pe_s.before(i))
                    pool.wait_ge(*rh_ready.now(i))
                    if runs(i - 2):
                        pool.wait_ge(*rms2_ready.now(i - 2))
                    for n, h4 in enumerate((2, 3)):
                        r = slice(32 * h4, 32 * h4 + 32)
                        if n:
                            pool.wait_ge(*kp_ready.now(i, n - 1))
                        pool.tensor_tensor(k[r, :, h4, :], k1[r, :, :], k2[r, :, :], ALU.add).then_inc(kp_ready.sem, 1)
                    pool.wait_ge(*kp_ready.now(i, 1))

                def out_sq(i):
                    if not runs(i):
                        return
                    pool.wait_ge(*x2_ready.now(i))
                    pool.wait_ge(*ms_ready.before(i, 0))
                    pool.tensor_tensor(sq[:, :, :], x2[:, :, :], x2[:, :, :], ALU.mult).then_inc(sq_ready.sem, 1)

                def out_rms(i):
                    if not runs(i):
                        return
                    pool.wait_ge(*ms_ready.now(i, 1))
                    pool.wait_ge(*f0_ready.before(i))
                    pool.tensor_tensor(ms[:, 2, :], ms[:, 1, :], half[:, 0:PG], ALU.pow).then_inc(rms2_ready.sem, 1)

                def out_x(i):
                    if not runs(i):
                        return
                    xg = x[:, bass.ds(i * PG, PG), :]
                    pool.wait_ge(*x2_ready.now(i))
                    pool.tensor_tensor(xg, xg, x2[:, :, :], ALU.add).then_inc(fin.sem, 1)

                def step(g, b):
                    head_rs(g + 1)
                    head_rh(g + 1)
                    out_sq(g - 1)
                    out_rms(g - 1)
                    rotate_k(g + 1)
                    out_x(g - 1)
                    if runs(g - 2):
                        R.pool_scatter(pool, g - 2, flat[b], dest)
                skewed(pool, step)
                R.wait_landed(pool, GROUPS - 1)
        clear_taken(nc)


def phase_experts(nc, A, banks, c, state, rows_in, rows_out, wall, swiglu, name):
    chunks = CH1 if swiglu else CH2
    HID = HID1 if swiglu else HID2
    NK = len(chunks)
    NW = wall.shape[-1]
    W2 = 2 * HID if swiglu else HID
    ident = c["ident"]
    with ExitStack() as ctx:
        def sb(n, shape, dt=F32):
            return ctx.enter_context(nc.sbuf_tensor(f"{name}_{n}", shape, dt))

        def sig(n, per=UN):
            return Signal(take_semaphore(ctx, nc, f"{name}_{n}"), per)

        def raw(n):
            return take_semaphore(ctx, nc, f"{name}_{n}")

        w = [sb(f"w{i}", [128, NW]) for i in range(UN)]
        xg = [sb(f"xg{i}", [128, 2, ROW]) for i in range(UN)]
        yb = [sb(f"yb{i}", [128, 2, C]) for i in range(UN)]
        xT = [sb(f"xT{i}", [128, TILE]) for i in range(2)]
        sg = [sb(f"sg{i}", [128, NK, TILE]) for i in range(2)]
        hT = [sb(f"hT{i}", [128, NK, TILE]) for i in range(2)] if swiglu else sg
        dst = [sb(f"dst{i}", [128, 2]) for i in range(UN)]
        dsti = [sb(f"dsti{i}", [128, 2], I32) for i in range(UN)]
        zero = sb("zero", [128, TRASH // 128, ROW])
        trash = sb("trash", [128, TRASH // 128])
        tail = sb("tail", [128, NE, 2], I32)
        tailf = sb("tailf", [128, NE, 2])
        le = sb("le", [128, NE, NE])
        iota = sb("iota", [128, TILES])
        cneg = sb("cneg", [128, NE])
        ti, tj = sb("ti", [128, NE], I32), sb("tj", [128, NE], I32)
        tf = sb("tf", [128, NE])
        cm, cum = sb("cm", [128, NE, NE]), sb("cum", [128, NE])
        ge, go = sb("ge", [128, TILES, NE]), sb("go", [128, TILES, NE])
        ei, off = sb("ei", [128, TILES]), sb("off", [128, TILES])
        rv = sb("rv", [128, TILES])
        table = sb("table", [128, 2, TILES], I32)
        prow = sb("prow", [128, 2])
        load, chain, zeroed, zlist, tsem = raw("load"), raw("chain"), raw("zeroed"), raw("zlist"), raw("tails")
        loaded = [raw(f"loaded{i}") for i in range(UN)]
        stored = [raw(f"stored{i}") for i in range(UN)]
        pe_x, pe_up, pe_down = sig("pe_x"), sig("pe_up", UN * NK), sig("pe_down")
        xT_ready, act_done = sig("xT_ready"), sig("act_done", UN * NK)
        h_ready = sig("h_ready", UN * NK) if swiglu else act_done
        y_ready = sig("y_ready")
        dst_ready = sig("dst_ready", 3 * UN)
        gate, read_gate = raw("gate"), raw("read_gate")
        list_tiles = rows_in.rearrange("(a t p) c -> a p t c", t=2, p=128)
        TPE = CAP // TILE

        with nc.Block() as block:
            @block.sync
            def _(sp):
                sp.dma_start(le[:, :, :], A["c_le"]).then_inc(load, 16)
                sp.dma_start(iota[:, :], row_bcast(A["c_iota"])).then_inc(load, 16)
                sp.dma_start(trash[:, :], A["c_trash"]).then_inc(load, 16)
                sp.dma_start(prow[:, :], A["c_prow"]).then_inc(load, 16)
                sp.wait_ge(zeroed, 1)
                spare = TILES - 2 * TOKENS // TILE
                for i in range(spare):
                    sp.dma_start(list_tiles[NE * TPE + i], zero[:, 2 * NE + 2 * i:2 * NE + 2 * i + 2, :]).then_inc(zlist, 16)
                sp.wait_ge(zlist, 16 * spare)

            @block.vector
            def _(dve):
                base = state["base"]
                n = [0]

                def then(ins):
                    n[0] += 1
                    ins.then_inc(chain, 1)
                    dve.wait_ge(chain, n[0])

                then(dve.memset(zero[:, :, :], 0.0))
                dve.wait_ge(load, 64)
                dve.tensor_copy(zero[:, :, C], trash[:, :]).then_inc(zeroed, 1)
                b = base[:, :]
                pr = prow[:, :]
                then(dve.tensor_tensor(tailf[:, :, :], bass.AP(b.tensor, b.offset, [b.ap[0], [1, NE], [0, 2]]),
                                       bass.AP(pr.tensor, pr.offset, [pr.ap[0], [0, NE], [1, 2]]), ALU.add))
                then(dve.tensor_copy(tail[:, :, :], tailf[:, :, :]))
                then(dve.tensor_scalar(cneg[:, :], c["rev"][:, :], float(CAP), float(TILE - 1 - NE * CAP), ALU.mult, ALU.add))
                then(dve.tensor_tensor(ti[:, :], base[:, :], cneg[:, :], ALU.add))
                then(dve.tensor_scalar(tj[:, :], ti[:, :], TILE.bit_length() - 1, None, ALU.logical_shift_right))
                then(dve.tensor_copy(tf[:, :], tj[:, :]))
                t = tf[:, :]
                then(dve.tensor_tensor(cm[:, :, :], le[:, :, :], bass.AP(t.tensor, t.offset, [t.ap[0], [0, NE], [1, NE]]), ALU.mult))
                then(dve.tensor_reduce(cum[:, :], cm[:, :, :], AX.X, ALU.add))
                u, v = iota[:, :], cum[:, :]
                then(dve.tensor_tensor(ge[:, :, :], bass.AP(u.tensor, u.offset, [u.ap[0], [1, TILES], [0, NE]]),
                                       bass.AP(v.tensor, v.offset, [v.ap[0], [0, TILES], [1, NE]]), ALU.is_ge))
                then(dve.tensor_reduce(ei[:, :], ge[:, :, :], AX.X, ALU.add))
                then(dve.tensor_tensor(go[:, :, :], ge[:, :, :], bass.AP(t.tensor, t.offset, [t.ap[0], [0, TILES], [1, NE]]), ALU.mult))
                then(dve.tensor_reduce(off[:, :], go[:, :, :], AX.X, ALU.add))
                then(dve.tensor_tensor(off[:, :], iota[:, :], off[:, :], ALU.subtract))
                then(dve.scalar_tensor_tensor(out=table[:, 0, :], in0=ei[:, :], scalar=float(TPE), in1=off[:, :],
                                              op0=ALU.mult, op1=ALU.add))
                then(dve.tensor_scalar(off[:, :], ei[:, :], float(NE - 1), None, ALU.min))
                then(dve.tensor_copy(table[:, 1, :], off[:, :]))
                then(dve.tensor_scalar(rv[:, :], off[:, :], -1.0, float(NE), ALU.mult, ALU.add))
                open_signals(dve, [y_ready, dst_ready])
                if swiglu:
                    open_signals(dve, [h_ready])

            @block.gpsimd
            def _(pool):
                pool.wait_ge(chain, 3)
                pool.wait_ge(zeroed, 1)
                for e in range(NE):
                    for r in range(2):
                        pool.indirect_dma_start(out=rows_in, out_offset=bass.IndirectOffsetOnAxis(ap=tail[:, e, r:r + 1], axis=0),
                                                in_=zero[:, 2 * e + r, :], in_offset=None).then_inc(tsem, 16)
                pool.wait_ge(tsem, 16 * 2 * NE)

            @block.scalar
            def _(act):
                open_signals(act, [xT_ready, act_done])

            @block.tensor
            def _(pe):
                open_signals(pe, [pe_x, pe_up, pe_down])

        bT, bY = banks[0], banks[7]
        NB = 3 if swiglu else 2
        up_banks = [banks[1:1 + NB], banks[4:4 + NB]]
        TURNS = TILES // UN

        with nc.Block() as block:
            @block.sync
            def _(sp):
                def read(g, j):
                    at = sp.value_load(table[0:1, 0, bass.ds(g * UN + j, 1)], min_val=0, max_val=(NE + 1) * TPE - 1)
                    ex = sp.value_load(table[0:1, 1, bass.ds(g * UN + j, 1)], min_val=0, max_val=NE - 1)
                    sp.wait_ge(*y_ready.now(g, j - UN))
                    sp.sem_inc(read_gate, 1)
                    sp.dma_start(w[j][:, :], wall[bass.ds(ex, 1), :, :].rearrange("a p n -> p (a n)")).then_inc(loaded[j], 16)
                    sp.dma_start(xg[j][:, :, :], list_tiles[bass.ds(at, 1), :, :, :].rearrange("a p t c -> p (a t) c")).then_inc(loaded[j], 16)

                turns(sp, 0, TURNS, lambda g: [read(g, j) for j in range(UN)])

            @block.gpsimd
            def _(pool):
                def body(g):
                    for j in range(UN):
                        pool.wait_ge(*y_ready.now(g, j))
                        pool.wait_ge(*dst_ready.now(g, 3 * j + 2))
                        pool.sem_inc(gate, 1)
                        for t in range(2):
                            pool.indirect_dma_start(
                                out=rows_out, out_offset=bass.IndirectOffsetOnAxis(ap=dsti[j][:, t:t + 1], axis=0),
                                in_=yb[j][:, t, :], in_offset=None).then_inc(stored[j], 16)
                turns(pool, 0, TURNS, body)
                for j in range(UN):
                    pool.wait_ge(stored[j], 32 * TURNS)

            @block.tensor
            def _(pe):
                def x_T(g, j):
                    jj = j % UN
                    gg = g + 1 if j == UN else g
                    pe.wait_ge(loaded[jj], (gg + 1) * 32)
                    pe.wait_ge(*xT_ready.now(g, j - 1))
                    for t in range(2):
                        i = pe.transpose(bT[:, 128 * t:128 * t + 128], xg[jj][:, t, 0:C], ident[:, :])
                    i.then_inc(pe_x.sem, 1)

                def up(g, j):
                    pe.wait_ge(*xT_ready.now(g, j))
                    pe.wait_ge(*h_ready.now(g, NK * (j - 2) + NK - 1))
                    for k, (c0, cn) in enumerate(chunks):
                        if swiglu:
                            bank = up_banks[j % 2][k]
                            for m in range(2):
                                i = pe.matmul(bank[0:cn, TILE * m:TILE * m + TILE], w[j][:, HID * m + c0:HID * m + c0 + cn],
                                              xT[j % 2][:, :], start=(m == 0), stop=True, skip_group_check=True)
                            i.then_inc(pe_up.sem, 1)
                        else:
                            bank = up_banks[j % 2][k // 2]
                            i = pe.matmul(bank[0:cn, TILE * (k % 2):TILE * (k % 2) + TILE], w[j][:, c0:c0 + cn],
                                          xT[j % 2][:, :], start=(k % 2 == 0), stop=True, skip_group_check=True)
                            i.then_inc(pe_up.sem, 1)

                def down(g, j):
                    jj = j % UN
                    pe.wait_ge(*h_ready.now(g, NK * j + NK - 1))
                    pe.wait_ge(*y_ready.now(g, j - 1))
                    for t in range(2):
                        for k, (c0, cn) in enumerate(chunks):
                            i = pe.matmul(bY[:, 128 * t:128 * t + 128], hT[jj % 2][0:cn, k, 128 * t:128 * t + 128],
                                          w[jj][0:cn, W2 + 128 * k:W2 + 128 * k + 128], start=(k == 0), stop=(k == NK - 1),
                                          skip_group_check=True)
                    i.then_inc(pe_down.sem, 1)

                def body(g, first=False, last=False):
                    for j in range(UN):
                        up(g, j)
                        if not (last and j == UN - 1):
                            x_T(g, j + 1)
                        if not (first and j == 0):
                            down(g, j - 1)
                x_T(0, 0)
                body(0, first=True)
                turns(pe, 1, TURNS - 1, body)
                body(TURNS - 1, last=True)
                down(TURNS - 1, UN - 1)

            @block.scalar
            def _(act):
                def x_T(g, j):
                    act.wait_ge(*pe_x.now(g, j))
                    act.wait_ge(*pe_up.now(g, NK * (j - 2) + NK - 1))
                    act.activation(xT[j % 2][:, :], bT[:, 0:TILE], ACT.Copy).then_inc(xT_ready.sem, 1)

                def body(g, last=False):
                    for j in range(UN):
                        for k, (c0, cn) in enumerate(chunks):
                            if swiglu:
                                act.wait_ge(*pe_up.now(g, NK * j + k))
                                act.wait_ge(*h_ready.now(g, NK * (j - 2) + k))
                                act.activation(sg[j % 2][0:cn, k, :], up_banks[j % 2][k][0:cn, 0:TILE], ACT.Silu)\
                                   .then_inc(act_done.sem, 1)
                            else:
                                act.wait_ge(*pe_up.now(g, NK * j + k // 2 * 2 + 1))
                                act.wait_ge(*pe_down.now(g, j - 2))
                                bank = up_banks[j % 2][k // 2]
                                b1 = W2 + NK * C + k
                                act.activation(sg[j % 2][0:cn, k, :], bank[0:cn, TILE * (k % 2):TILE * (k % 2) + TILE], ACT.Gelu,
                                               bias=w[j][:, b1:b1 + 1]).then_inc(act_done.sem, 1)
                        if not (last and j == UN - 1):
                            x_T(g, j + 1)
                x_T(0, 0)
                turns(act, 0, TURNS - 1, body)
                body(TURNS - 1, last=True)

            @block.vector
            def _(dve):
                def out(g, j):
                    jj = j % UN
                    dve.wait_ge(*pe_down.now(g, j))
                    src = bY[:, 0:2 * C].rearrange("r (t c) -> r t c", t=2)
                    if swiglu:
                        dve.tensor_copy(yb[jj][:, :, :], src).then_inc(y_ready.sem, 1)
                    else:
                        b = w[jj][:, W2 + NK * C + NK:W2 + NK * C + NK + C]
                        dve.tensor_tensor(yb[jj][:, :, :], src, bass.AP(b.tensor, b.offset, [b.ap[0], [0, 2], [1, C]]), ALU.add)\
                           .then_inc(y_ready.sem, 1)

                def body(g, first=False):
                    for j in range(UN):
                        if swiglu:
                            for k, (c0, cn) in enumerate(chunks):
                                dve.wait_ge(*act_done.now(g, NK * j + k))
                                dve.wait_ge(*pe_down.now(g, j - 2))
                                dve.tensor_tensor(hT[j % 2][0:cn, k, :], up_banks[j % 2][k][0:cn, TILE:2 * TILE],
                                                  sg[j % 2][0:cn, k, :], ALU.mult).then_inc(h_ready.sem, 1)
                        if not (first and j == 0):
                            out_wait(g, j - 1)
                            out(g, j - 1)
                        where(g, j)

                def where(g, j):
                    dve.wait_ge(loaded[j], (g + 1) * 32)
                    if not isinstance(g, int) or g > 0:
                        dve.wait_ge(stored[j], g * 32)
                    dve.tensor_scalar(dst[j][:, :], xg[j][:, :, C + 1], rv[:, bass.ds(g * UN + j, 1)], float(TOKENS),
                                      ALU.not_equal, ALU.mult).then_inc(dst_ready.sem, 1)
                    dve.wait_ge(*dst_ready.now(g, 3 * j))
                    dve.tensor_tensor(dst[j][:, :], dst[j][:, :], xg[j][:, :, C], ALU.add).then_inc(dst_ready.sem, 1)
                    dve.wait_ge(*dst_ready.now(g, 3 * j + 1))
                    dve.tensor_copy(dsti[j][:, :], dst[j][:, :]).then_inc(dst_ready.sem, 1)

                def out_wait(g, j):
                    gg = g - 1 if j < 0 else g
                    if isinstance(gg, int):
                        if gg > 0:
                            dve.wait_ge(stored[j % UN], 32 * gg)
                    else:
                        dve.wait_ge(stored[j % UN], gg * 32)
                body(0, first=True)
                body(1)
                turns(dve, 2, TURNS, body)
                out_wait(TURNS - 1, UN - 1)
                out(TURNS - 1, UN - 1)
        clear_taken(nc)


class Combine:

    def __init__(self, ctx, nc, name, state, rows):
        self.state = state
        self.rows = rows[0:2 * TOKENS, :].rearrange("(k t p) c -> p k t c", k=2, p=128)
        self.y = ctx.enter_context(nc.sbuf_tensor(f"{name}_y", [128, 2, PG, C], F32))
        self.landed = take_semaphore(ctx, nc, f"{name}_landed")
        self.mixed = Signal(take_semaphore(ctx, nc, f"{name}_mixed"), 2 * PG)
        self.gate = take_semaphore(ctx, nc, f"{name}_gate")
        self.dve_signals = [self.mixed]

    def fetch(self, sp, g):
        sp.wait_ge(*self.mixed.before(g))
        sp.sem_inc(self.gate, 1)
        for k in range(2):
            sp.dma_start(self.y[:, k, :, :], self.rows[:, k, bass.ds(g * PG, PG), :]).then_inc(self.landed, 16)

    def vector_mix(self, dve, g, x):
        w = self.state["w"]
        dve.wait_ge(self.landed, (g + 1) * 32)
        for k in range(2):
            if k:
                dve.wait_ge(*self.mixed.now(g, PG - 1))
            for p in range(PG):
                xt = x[:, bass.ds(g * PG + p, 1), :].rearrange("p a c -> p (a c)")
                dve.scalar_tensor_tensor(out=xt, in0=self.y[:, k, p, :], scalar=w[:, k, bass.ds(g * PG + p, 1)], in1=xt,
                                         op0=ALU.mult, op1=ALU.add).then_inc(self.mixed.sem, 1)


def phase_gnn1(nc, A, x, banks, c, state1, rows1, state2, dest):
    ident, half, adj = c["ident"], c["half"], c["adj"]
    with ExitStack() as ctx:
        def sb(name, shape, dt=F32):
            return ctx.enter_context(nc.sbuf_tensor("g1_" + name, shape, dt))

        def sig(name, per=1):
            return Signal(take_semaphore(ctx, nc, "g1_" + name), per)

        w1, w2, w3 = sb("w1", [128, C]), sb("w2", [128, C]), sb("w3", [128, C])
        wg = sb("wg", [128, NE])
        bg = sb("bg", [128, NE])
        mask = sb("mask", [128, NODES])
        st = sb("st", [128, 2, PG, 11]); mean = sb("mean", [128, 2, PG]); ve = sb("ve", [128, 2, PG]); rs = sb("rs", [128, 2, PG])
        xn = sb("xn", [128, PG, C])
        xT = sb("xT", [128, GT])
        h1, h2 = sb("h1", [128, GT]), sb("h2", [128, GT])
        h3 = sb("h3", [128, PG, C + 1])
        e1 = sb("e1", [128, PG, NODES])
        e2 = sb("e2", [128, PG, NODES])
        mx = sb("mx", [128, PG])
        s = sb("s", [128, PG, NODES])
        pr = sb("pr", [128, PG, 2, NODES])
        pt = sb("pt", [128, PG, 128])
        rc = sb("rc", [128, PG])
        o = sb("o", [128, PG, C])
        flat = [sb(f"flat{i}", [128, PG, ROW]) for i in range(2)]
        fT = sb("fT", [128, GT])
        load = take_semaphore(ctx, nc, "g1_load")
        setup = take_semaphore(ctx, nc, "g1_setup")
        R = Routing(ctx, nc, "g1r", c, dict(state2, bias=bg))
        M = Combine(ctx, nc, "g1c", state1, rows1)

        bn, part, vs = [sig("bn0", PG), sig("bn1", PG)], [sig("part0", 6), sig("part1", 6)], [sig("vs0"), sig("vs1")]
        xn_ready, h3_ready = sig("xn_ready", PG), sig("h3_ready")
        e_steps = sig("e_steps", 5)
        rc_ready, o_ready, x3_ready = sig("rc_ready", 2), sig("o_ready", PG), sig("x3_ready")
        flat_ready = sig("flat_ready", PG)
        gate = sig("gate")
        dve_signals = bn + part + vs + [xn_ready, h3_ready, e_steps, rc_ready, o_ready, x3_ready, flat_ready]\
            + R.dve_signals + M.dve_signals
        xT_ready, h12_ready, p_ready, pt_ready, fT_ready = sig("xT_ready"), sig("h12_ready", 2), sig("p_ready", 2), sig("pt_ready"), sig("fT_ready")
        act_signals = [xT_ready, h12_ready, p_ready, pt_ready, fT_ready] + R.act_signals
        rs_ready = [sig("rs0_ready"), sig("rs1_ready")]
        pool_signals = rs_ready + R.pool_signals
        pe_xT, pe_h, pe_e, pe_pt, pe_o, pe_fT = sig("pe_xT"), sig("pe_h", 3), sig("pe_e"), sig("pe_pt"), sig("pe_o", 2), sig("pe_fT")
        pe_signals = [pe_xT, pe_h, pe_e, pe_pt, pe_o, pe_fT] + R.pe_signals
        bT, bH1, bH2, bH3, bE, bO0, bO1, bR = banks

        with nc.Block() as block:
            @block.sync
            def _(sp):
                sp.dma_start(w1[:, :], A["L1_gnn_W1"]).then_inc(load, 16)
                sp.dma_start(w2[:, :], A["L1_gnn_W2"]).then_inc(load, 16)
                sp.dma_start(w3[:, :], A["L1_gnn_W3"]).then_inc(load, 16)
                sp.dma_start(wg[:, :], A["L1_ffn_Wg"]).then_inc(load, 16)
                sp.dma_start(bg[:, :], row_bcast(A["L1_ffn_bg"])).then_inc(load, 16)
                sp.wait_ge(load, 16 * 5)

            @block.gpsimd
            def _(pool):
                pool.memset(pr[:, :, :, :], 0.0).then_inc(setup, 1)
                pool.memset(h3[:, :, C:C + 1], 1.0).then_inc(setup, 1)
                open_signals(pool, pool_signals)

            @block.vector
            def _(dve):
                dve.tensor_scalar(mask[:, :], adj[:, :], 0.0, -1e12, ALU.is_le, ALU.mult)
                b = state2["base"]
                dve.tensor_scalar(b[:, :], c["rev"][:, :], -float(CAP), float(NE * CAP), ALU.mult, ALU.add)
                open_signals(dve, dve_signals)

            @block.scalar
            def _(act):
                open_signals(act, act_signals)

            @block.tensor
            def _(pe):
                open_signals(pe, pe_signals)

        def xt(i, p):
            return x[:, bass.ds(i * PG + p, 1), :].rearrange("p a c -> p (a c)")

        with nc.Block() as block:
            @block.tensor
            def _(pe):
                def head_T(i):
                    if not runs(i):
                        return
                    pe.wait_ge(*xn_ready.now(i, PG - 1))
                    pe.wait_ge(*fT_ready.before(i, turns=2))
                    for p in range(PG):
                        ins = pe.transpose(bT[:, 128 * p:128 * p + 128], xn[:, p, :], ident[:, :])
                    ins.then_inc(pe_xT.sem, 1)

                def head_h(i):
                    if not runs(i):
                        return
                    pe.wait_ge(*xT_ready.now(i))
                    pe.wait_ge(*h12_ready.before(i))
                    pe.matmul(bH1[:, :], w1[:, :], xT[:, :], start=True, stop=True).then_inc(pe_h.sem, 1)
                    pe.wait_ge(*pt_ready.before(i))
                    pe.matmul(bH2[:, :], w2[:, :], xT[:, :], start=True, stop=True).then_inc(pe_h.sem, 1)
                    pe.wait_ge(*h3_ready.before(i))
                    for p in range(PG):
                        ins = pe.matmul(bH3[:, 128 * p:128 * p + 128], xT[:, 128 * p:128 * p + 128], w3[:, :],
                                        start=(p == 0), stop=True, skip_group_check=True)
                    ins.then_inc(pe_h.sem, 1)

                def scores(i):
                    if not runs(i):
                        return
                    pe.wait_ge(*h12_ready.now(i, 1))
                    pe.wait_ge(*e_steps.before(i, 1))
                    for fr in range(2 * PG):
                        f, p = fr % 2, fr // 2
                        t = slice(64 * fr, 64 * fr + 64)
                        ins = pe.matmul(bE[64 * f:64 * f + 64, 64 * p:64 * p + 64], h1[:, t], h2[:, t],
                                        start=(p == 0), stop=True, skip_group_check=True)
                    ins.then_inc(pe_e.sem, 1)

                def probs_T(i):
                    if not runs(i):
                        return
                    pe.wait_ge(*p_ready.now(i, 1))
                    for p in range(PG):
                        ins = pe.transpose(bH2[:, 128 * p:128 * p + 128], pr[:, p, :, :].rearrange("n f m -> n (f m)"), ident[:, :])
                    ins.then_inc(pe_pt.sem, 1)

                def mix(i):
                    if not runs(i):
                        return
                    pe.wait_ge(*pt_ready.now(i))
                    pe.wait_ge(*h3_ready.now(i))
                    pe.wait_ge(*o_ready.before(i))
                    for u, bank in enumerate([bO0, bO1]):
                        for n in range(2):
                            p = 2 * u + n
                            ins = pe.matmul(bank[:, (C + 1) * n:(C + 1) * n + C + 1], pt[:, p, :], h3[:, p, :],
                                            start=(n == 0), stop=True, skip_group_check=True)
                        ins.then_inc(pe_o.sem, 1)

                def flat_T(i, b):
                    if not runs(i):
                        return
                    pe.wait_ge(*flat_ready.now(i, PG - 1))
                    if runs(i + 1):
                        pe.wait_ge(*xT_ready.now(i + 1))
                    for p in range(PG):
                        ins = pe.transpose(bT[:, 128 * p:128 * p + 128], flat[b][:, p, 0:C], ident[:, :])
                    ins.then_inc(pe_fT.sem, 1)

                def logits(i):
                    if not runs(i):
                        return
                    pe.wait_ge(*fT_ready.now(i))
                    pe.wait_ge(*R.pstep.before(i, 0))
                    R.tensor_logits(pe, i, bR, fT, wg)

                def step(g, b):
                    scores(g)
                    flat_T(g - 1, 1 - b)
                    probs_T(g)
                    if runs(g - 2):
                        R.tensor_rank(pe, g - 2, bR)
                    mix(g)
                    head_T(g + 1)
                    head_h(g + 1)
                    logits(g - 1)
                skewed(pe, step)

            @block.scalar
            def _(act):
                def head(i):
                    if not runs(i):
                        return
                    act.wait_ge(*pe_xT.now(i))
                    act.wait_ge(*pe_h.before(i))
                    act.activation(xT[:, :], bT[:, :], ACT.Copy).then_inc(xT_ready.sem, 1)
                    for n, (bank, h) in enumerate([(bH1, h1), (bH2, h2)]):
                        act.wait_ge(*pe_h.now(i, n))
                        act.wait_ge(*pe_e.before(i))
                        act.activation(h[:, :], bank[:, :], ACT.Copy).then_inc(h12_ready.sem, 1)

                def exp(i):
                    if not runs(i):
                        return
                    act.wait_ge(*e_steps.now(i, 4))
                    act.wait_ge(*pe_pt.before(i))
                    for f in range(2):
                        r = slice(64 * f, 64 * f + 64)
                        act.activation(pr[r, :, f, :], s[r, :, :], ACT.Exp).then_inc(p_ready.sem, 1)

                def probs_T(i):
                    if not runs(i):
                        return
                    act.wait_ge(*pe_pt.now(i))
                    act.wait_ge(*pe_o.before(i))
                    act.activation(pt[:, :, :].rearrange("m p n -> m (p n)"), bH2[:, :], ACT.Copy).then_inc(pt_ready.sem, 1)

                def flat_T(i):
                    if not runs(i):
                        return
                    act.wait_ge(*pe_fT.now(i))
                    act.wait_ge(*R.pe_logits.before(i))
                    act.activation(fT[:, :], bT[:, :], ACT.Copy).then_inc(fT_ready.sem, 1)

                def step(g, b):
                    exp(g)
                    flat_T(g - 1)
                    probs_T(g)
                    if runs(g - 2):
                        R.scalar_exp(act, g - 2, False)
                    head(g + 1)
                skewed(act, step)

            @block.vector
            def _(dve):
                def head_stats(i):
                    if not runs(i):
                        return
                    M.vector_mix(dve, i, x)
                    norm_stats(dve, lambda p: xt(i, p), st[:, 0, :, :], mean[:, 0, :], ve[:, 0, :], bn[0], part[0], vs[0], i,
                               EPS_LN, [M.mixed.now(i, 2 * PG - 1), rs_ready[0].before(i)], gate)

                def head_xn(i):
                    if not runs(i):
                        return
                    dve.wait_ge(*rs_ready[0].now(i))
                    dve.wait_ge(*pe_xT.before(i))
                    for p in range(PG):
                        dve.tensor_scalar(xn[:, p, :], xt(i, p), mean[:, 0, p:p + 1], rs[:, 0, p:p + 1],
                                          ALU.subtract, ALU.mult).then_inc(xn_ready.sem, 1)

                def head_h3(i):
                    if not runs(i):
                        return
                    dve.wait_ge(*pe_h.now(i, 2))
                    dve.wait_ge(*pe_o.before(i))
                    dve.tensor_copy(h3[:, :, 0:C], bH3[:, :].rearrange("m (p c) -> m p c", p=PG)).then_inc(h3_ready.sem, 1)

                def soft(i):
                    if not runs(i):
                        return
                    ev = bE[:, 0:PG * NODES].rearrange("n (p m) -> n p m", p=PG)
                    dve.wait_ge(*pe_e.now(i))
                    dve.wait_ge(*e_steps.before(i))
                    dve.tensor_scalar(e1[:, :, :], ev, 0.2, None, ALU.mult).then_inc(e_steps.sem, 1)
                    dve.wait_ge(*e_steps.now(i, 0))
                    dve.tensor_tensor(e1[:, :, :], ev, e1[:, :, :], ALU.max).then_inc(e_steps.sem, 1)
                    dve.wait_ge(*e_steps.now(i, 1))
                    mk = mask[:, :]
                    dve.tensor_tensor(e2[:, :, :], e1[:, :, :], bass.AP(mk.tensor, mk.offset, [mk.ap[0], [0, PG], [1, NODES]]), ALU.add)\
                       .then_inc(e_steps.sem, 1)
                    dve.wait_ge(*e_steps.now(i, 2))
                    dve.tensor_reduce(mx[:, :], e2[:, :, :], AX.X, ALU.max).then_inc(e_steps.sem, 1)
                    dve.wait_ge(*e_steps.now(i, 3))
                    dve.wait_ge(*p_ready.before(i))
                    m = mx[:, :]
                    dve.tensor_tensor(s[:, :, :], e2[:, :, :], bass.AP(m.tensor, m.offset, [m.ap[0], [1, PG], [0, NODES]]), ALU.subtract)\
                       .then_inc(e_steps.sem, 1)

                def norm(i):
                    if not runs(i):
                        return
                    for u, bank in enumerate([bO0, bO1]):
                        dve.wait_ge(*pe_o.now(i, u))
                        ov = bank[:, 0:2 * (C + 1)].rearrange("n (p c) -> n p c", p=2)
                        dve.wait_ge(*o_ready.before(i))
                        dve.reciprocal(rc[:, 2 * u:2 * u + 2], ov[:, :, C]).then_inc(rc_ready.sem, 1)
                        dve.wait_ge(*rc_ready.now(i, u))
                        if u == 0:
                            dve.wait_ge(*x3_ready.before(i))
                        for n in range(2):
                            p = 2 * u + n
                            dve.tensor_scalar(o[:, p, :], ov[:, n, 0:C], rc[:, p:p + 1], 0.0, ALU.mult, ALU.max).then_inc(o_ready.sem, 1)
                    dve.wait_ge(*o_ready.now(i, PG - 1))
                    xg = x[:, bass.ds(i * PG, PG), :]
                    dve.tensor_tensor(xg, xg, o[:, :, :], ALU.add).then_inc(x3_ready.sem, 1)

                def flat_stats(i):
                    if not runs(i):
                        return
                    norm_stats(dve, lambda p: xt(i, p), st[:, 1, :, :], mean[:, 1, :], ve[:, 1, :], bn[1], part[1], vs[1], i,
                               EPS_LN, [x3_ready.now(i), rs_ready[1].before(i)], gate)

                def flat_norm(i, b):
                    if not runs(i):
                        return
                    dve.wait_ge(*rs_ready[1].now(i))
                    dve.wait_ge(*pe_fT.before(i))
                    R.wait_landed(dve, i - 2)
                    for p in range(PG):
                        dve.tensor_scalar(flat[b][:, p, 0:C], xt(i, p), mean[:, 1, p:p + 1], rs[:, 1, p:p + 1],
                                          ALU.subtract, ALU.mult).then_inc(flat_ready.sem, 1)

                def step(g, b):
                    flat_stats(g - 1)
                    soft(g)
                    flat_norm(g - 1, 1 - b)
                    head_stats(g + 1)
                    if runs(g - 2):
                        R.vector_choose(dve, g - 2, bR, False)
                    head_xn(g + 1)
                    norm(g)
                    if runs(g - 2):
                        R.vector_rows(dve, g - 2, bR)
                        R.vector_weights(dve, g - 2, False)
                    head_h3(g + 1)
                skewed(dve, step, first=4)

            @block.gpsimd
            def _(pool):
                def head_rs(i):
                    if not runs(i):
                        return
                    pool.wait_ge(*vs[0].now(i))
                    pool.wait_ge(*xn_ready.before(i))
                    pool.tensor_tensor(rs[:, 0, :], ve[:, 0, :], half[:, 0:PG], ALU.pow).then_inc(rs_ready[0].sem, 1)

                def flat_rs(i):
                    if not runs(i):
                        return
                    pool.wait_ge(*vs[1].now(i))
                    pool.wait_ge(*flat_ready.before(i))
                    pool.tensor_tensor(rs[:, 1, :], ve[:, 1, :], half[:, 0:PG], ALU.pow).then_inc(rs_ready[1].sem, 1)

                def step(g, b):
                    flat_rs(g - 1)
                    head_rs(g + 1)
                    if runs(g - 2):
                        R.pool_scatter(pool, g - 2, flat[b], dest)
                skewed(pool, step)
                R.wait_landed(pool, GROUPS - 1)

            @block.sync
            def _(sp):
                turns(sp, 0, GROUPS, lambda g: M.fetch(sp, g))
        clear_taken(nc)


def phase_finish(nc, x, c, state, rows, out_dram):
    with ExitStack() as ctx:
        M = Combine(ctx, nc, "fin", state, rows)
        stored = take_semaphore(ctx, nc, "fin_stored")
        with nc.Block() as block:
            @block.vector
            def _(dve):
                open_signals(dve, M.dve_signals)

        with nc.Block() as block:
            @block.scalar
            def _(act):
                turns(act, 0, GROUPS, lambda g: M.fetch(act, g))

            @block.vector
            def _(dve):
                turns(dve, 0, GROUPS, lambda g: M.vector_mix(dve, g, x))

            @block.sync
            def _(sp):
                def body(g):
                    sp.wait_ge(*M.mixed.now(g, 2 * PG - 1))
                    sp.dma_start(out_dram[:, bass.ds(g * PG, PG), :], x[:, bass.ds(g * PG, PG), :]).then_inc(stored, 16)
                turns(sp, 0, GROUPS, body)
                sp.wait_ge(stored, 16 * GROUPS)


_INS = ['x', 'adj', 'L0_gnn_w_qkv', 'L0_gnn_ln1_g', 'L0_gnn_ln1_b', 'L0_gnn_ln2_g', 'L0_gnn_ln2_b', 'L0_gnn_w1',
        'L0_gnn_b1', 'L0_gnn_w2', 'L0_gnn_b2', 'L0_ffn_ln1_w', 'L0_ffn_ln2_w', 'L1_gnn_W1', 'L1_gnn_W2', 'L1_gnn_W3',
        'L1_ffn_Wg', 'L1_ffn_bg']


def laid_out(inputs):
    import numpy as np

    def T(w):
        return np.ascontiguousarray(np.asarray(w).T)

    eye = np.eye(128, dtype=np.float32)
    a = {"c_ident": eye}
    a["c_rev"] = np.ascontiguousarray(np.broadcast_to(NE - np.arange(NE, dtype=np.float32), (128, NE)))
    a["c_ids"] = (np.arange(128)[:, None] + 128 * np.arange(PAIRS)[None]).astype(np.float32)
    a["c_trash"] = (TOKENS + np.arange(128)[:, None] + 128 * np.arange(TRASH // 128)[None]).astype(np.float32)
    a["c_tri"] = np.triu(np.ones((128, 128), np.float32), 1)
    inv_freq = 1.0 / 10000.0 ** (np.arange(0, D1, 2, dtype=np.float32) / D1)
    ang = np.outer(np.arange(NODES, dtype=np.float32), inv_freq)
    cos, sin = np.cos(ang).T, np.sin(ang).T
    a["c_rope"] = np.ascontiguousarray(np.stack([np.tile(np.concatenate([cos, cos]), (H1, 1)),
                                                 np.tile(np.concatenate([-sin, sin]), (H1, 1))], axis=1), dtype=np.float32)
    n, m = np.arange(128)[:, None] % NODES, np.arange(NODES)[None, :]
    a["c_causal"] = np.where(m > n, np.float32(-1e30 * D1 ** 0.5), np.float32(0))
    swap = np.arange(D1) ^ (D1 // 2)
    wq = T(inputs["L0_ffn_wq"]).reshape(C, H1, D1)
    wk = np.repeat(T(inputs["L0_ffn_wk"]).reshape(C, KV1, D1), H1 // KV1, axis=1)
    for name, w in [("c_wq", wq), ("c_wk", wk)]:
        a[name] = np.ascontiguousarray(w.reshape(C, 128))
        a[name + "_x"] = np.ascontiguousarray(w[:, :, swap].reshape(C, 128))
    a["c_wv"] = T(inputs["L0_ffn_wv"])
    a["c_wo"] = T(inputs["L0_ffn_wo"])
    a["c_wr"] = T(inputs["L0_ffn_router_w"])
    e = np.arange(NE)
    a["c_le"] = np.ascontiguousarray(np.broadcast_to(e[None, :] <= e[:, None], (128, NE, NE)), dtype=np.float32)
    a["c_iota"] = np.arange(TILES, dtype=np.float32)
    a["c_prow"] = (np.arange(128)[:, None] + 128 * np.arange(2)[None]).astype(np.float32)

    def by_chunk(w):
        chunks = -(-w.shape[1] // 128)
        full = np.zeros((NE, chunks * 128, C), np.float32)
        full[:, :w.shape[1]] = w
        return full.reshape(NE, chunks, 128, C).transpose(0, 2, 1, 3).reshape(NE, 128, chunks * C)

    w1, w2, w3 = (np.asarray(inputs[f"L0_ffn_w{i}"]).transpose(0, 2, 1) for i in (1, 2, 3))
    a["c_wall1"] = np.ascontiguousarray(np.concatenate([w1, w3, by_chunk(w2)], axis=2))
    w1, w2, b1, b2 = (np.asarray(inputs["L1_ffn_" + n]) for n in ("W1", "W2", "b1", "b2"))
    a["c_wall2"] = np.ascontiguousarray(np.concatenate(
        [w1, by_chunk(w2), b1.reshape(NE, len(CH2), 128).transpose(0, 2, 1), np.broadcast_to(b2[:, None], (NE, 128, C))], axis=2))
    return a


def kernel(**inputs):
    import numpy as np
    import concourse.bacc as bacc
    from concourse import mybir as mb
    from concourse.bass_utils import run_bass_kernel_spmd as run

    nc = bacc.Bacc("TRN2", target_bir_lowering=False, num_devices=1)
    arrays = {n: np.ascontiguousarray(inputs[n]) for n in _INS}
    arrays.update(laid_out(inputs))
    A = {}
    for n, a in arrays.items():
        A[n] = nc.dram_tensor(f"in_{n}", a.shape, mb.dt.from_np(a.dtype), kind="ExternalInput").ap()
    out = nc.dram_tensor("out_0", (FRAMES, NODES, C), mb.dt.float32, kind="ExternalOutput").ap()
    build(nc, A, out)
    r = run(nc, [{f"in_{n}": a for n, a in arrays.items()}], core_ids=[0])
    return r.results[0]["out_0"]
```

```python
from contextlib import ExitStack

import concourse.bass as bass
from concourse import mybir

F32 = mybir.dt.float32
BF16 = mybir.dt.bfloat16
I32 = mybir.dt.int32
ALU = mybir.AluOpType
ACT = mybir.ActivationFunctionType
AX = mybir.AxisListType

FRAMES, NODES, C = 128, 64, 128
PAIRS = FRAMES // 2
PG = 4
GROUPS = PAIRS // PG
GT = PG * 128
EPS_LN = 1e-5
EPS_RMS = 1e-6
H0, D0 = 8, 16
H1, KV1, D1 = 4, 2, 32
NE = 8
HID1 = 341
HID2 = 512
TILE = 256
CAP = PAIRS * 128 + TILE
TILES = 2 * PAIRS * 128 // TILE + NE
UN = 4
TOKENS = FRAMES * NODES
ROW = C + 2
SPARE = TILES - 2 * TOKENS // TILE
TRASH = (NE + SPARE) * TILE
CH1 = [(0, 128), (128, 128), (256, 85)]
CH2 = [(128 * i, 128) for i in range(4)]


TAKEN = []


class Signal:

    def __init__(self, sem, per):
        self.sem, self.per = sem, per

    def now(self, g, j=0):
        return self.sem, (g + 3) * self.per + (j + 1)

    def before(self, g, j=None, turns=1):
        return self.sem, (g + 3 - turns) * self.per + (self.per if j is None else j + 1)


def take_semaphore(ctx, nc, name):
    sem = ctx.enter_context(nc.semaphore(name))
    TAKEN.append(sem)
    return sem


def clear_taken(nc):
    with nc.Block() as block:
        @block.gpsimd
        def _(pool):
            nums = sorted(s.num for s in TAKEN)
            while nums:
                n = 1
                while n < len(nums) and nums[n] == nums[0] + n:
                    n += 1
                pool.sem_clear(range(nums[0], nums[0] + n))
                del nums[:n]
    TAKEN.clear()


def open_signals(eng, signals):
    for s in signals:
        eng.sem_inc(s.sem, 3 * s.per)


def turns(eng, first, last, body):
    with eng.Fori(first, last) as g:
        body(g)


def runs(i):
    return not isinstance(i, int) or 0 <= i < GROUPS


def skewed(eng, step, first=2, ahead=2):
    for g in range(-3, first):
        step(g, g % 2)
    end = (GROUPS - ahead) // 2
    with eng.Fori(first // 2, end) as turn:
        for b in range(2):
            step(turn * 2 + b, b)
    for g in range(2 * end, GROUPS + 3):
        step(g, g % 2)


def row_bcast(vec, rows=128):
    n = vec.shape[-1]
    return bass.AP(vec.tensor, vec.offset, [[0, rows], [1, n]])


def build(nc, A, out):
    TAKEN.clear()
    with ExitStack() as ctx:
        def sb(name, shape, dt=F32):
            return ctx.enter_context(nc.sbuf_tensor(name, shape, dt))

        x = sb("x", [128, PAIRS, C])
        ident = sb("ident", [128, 128])
        identb = sb("identb", [128, 128], BF16)
        half = sb("half", [128, 8])
        rev = sb("rev", [128, NE])
        tri = sb("tri", [128, 128], BF16)
        ids = sb("ids", [128, PAIRS])
        tri32 = sb("tri32", [128, 128])
        ones = sb("ones", [128, 128], BF16)
        maskb = sb("maskb", [128, NODES], BF16)
        adj = sb("adj_sb", [128, NODES], I32)
        nobody = sb("nobody", [128, TRASH // 128, ROW])
        trash = sb("trash", [128, TRASH // 128])
        le = sb("le", [128, NE, NE])
        iota = sb("iota", [128, TILES])
        load_sem = ctx.enter_context(nc.semaphore("load_sem"))
        x_sem = ctx.enter_context(nc.semaphore("x_sem"))
        fill_sem = ctx.enter_context(nc.semaphore("fill_sem"))
        later_sem = ctx.enter_context(nc.semaphore("later_sem"))
        setup_sem = ctx.enter_context(nc.semaphore("setup_sem"))
        banks = [ctx.enter_context(nc.psum_tensor(f"bank{i}", [128, 512], F32)) for i in range(8)]
        x_dram = A["x"].rearrange("(t f) n c -> (f n) t c", f=2)
        out_dram = out.rearrange("(t f) n c -> (f n) t c", f=2)

        with nc.Block() as block:
            @block.sync
            def _(sp):
                sp.dma_start(ident[:, :], A["c_ident"]).then_inc(load_sem, 16)
                sp.dma_start(rev[:, :], A["c_rev"]).then_inc(load_sem, 16)
                sp.dma_start(ids[:, :], A["c_ids"]).then_inc(load_sem, 16)
                sp.dma_start(tri32[:, :], A["c_tri"]).then_inc(load_sem, 16)
                sp.dma_start(trash[:, :], A["c_trash"]).then_inc(load_sem, 16)
                for f in range(2):
                    sp.dma_start(adj[64 * f:64 * f + 64, :], A["adj"]).then_inc(load_sem, 16)
                sp.dma_start(le[:, :, :], A["c_le"]).then_inc(load_sem, 16)
                sp.dma_start(iota[:, :], row_bcast(A["c_iota"])).then_inc(load_sem, 16)
                sp.dma_start(x[:, 0:PAIRS // 4, :], x_dram[:, 0:PAIRS // 4, :]).then_inc(x_sem, 16)
                sp.wait_ge(load_sem, 16 * 9)
                sp.wait_ge(x_sem, 16)

            @block.vector
            def _(dve):
                dve.wait_ge(load_sem, 16 * 9)
                dve.wait_ge(setup_sem, 3)
                dve.tensor_copy(nobody[:, :, C], trash[:, :])
                dve.tensor_copy(identb[:, :], ident[:, :])
                dve.tensor_copy(tri[:, :], tri32[:, :])

            @block.gpsimd
            def _(pool):
                pool.memset(half[:, :], -0.5).then_inc(setup_sem, 1)
                pool.memset(ones[:, :], 1.0).then_inc(setup_sem, 1)
                pool.memset(nobody[:, :, :], 0.0).then_inc(setup_sem, 1)

        list1, list2 = [nc.dram_tensor(f"dispatch{i}", ((NE + 1) * CAP, ROW), F32, kind="Internal").ap() for i in (1, 2)]

        shapes = dict(wq=[128, 2, 128],
                      wk=[128, 2, 128],
                      wv=[128, 64], wo=[128, 128], wr=[128, NE], lnw=[128, 1], ln2w=[128, C], rope=[128, 2, NODES],
                      causal32=[128, NODES], w1=[128, C], w2=[128, C], w3=[128, C], wg=[128, NE], bg=[128, NE])
        W = {n: sb("W_" + n, shape) for n, shape in shapes.items()}

        def behind(sp):
            for i in range(1, 4):
                n = PAIRS // 4
                sp.dma_start(x[:, n * i:n * i + n, :], x_dram[:, n * i:n * i + n, :]).then_inc(x_sem, 16)
            for rows in (list1, list2):
                tiles = rows.rearrange("(a t p) c -> a p t c", t=2, p=128)
                for i in range(SPARE):
                    n = 2 * (NE + i)
                    sp.dma_start(tiles[NE * CAP // TILE + i], nobody[:, n:n + 2, :]).then_inc(fill_sem, 16)
            sp.wait_ge(fill_sem, 16 * 2 * SPARE)
            loads = [(W["wq"][:, 0, :], A["c_wq"]), (W["wq"][:, 1, :], A["c_wq_x"]), (W["wk"][:, 0, :], A["c_wk"]),
                     (W["wk"][:, 1, :], A["c_wk_x"]), (W["wv"][:, :], A["c_wv"]), (W["wo"][:, :], A["c_wo"]),
                     (W["wr"][:, :], A["c_wr"]), (W["lnw"][:, :], A["L0_ffn_ln1_w"].rearrange("(c a) -> c a", a=1)),
                     (W["ln2w"][:, :], row_bcast(A["L0_ffn_ln2_w"])), (W["rope"][:, :, :], A["c_rope"]),
                     (W["causal32"][:, :], A["c_causal"]), (W["w1"][:, :], A["L1_gnn_W1"]), (W["w2"][:, :], A["L1_gnn_W2"]),
                     (W["w3"][:, :], A["L1_gnn_W3"]), (W["wg"][:, :], A["L1_ffn_Wg"]), (W["bg"][:, :], row_bcast(A["L1_ffn_bg"]))]
            for tile, src in loads:
                sp.dma_start(tile, src).then_inc(later_sem, 16)
            sp.wait_ge(later_sem, 16 * len(loads))

        phase_gnn0(nc, A, x, ident, identb, half, maskb, adj, banks, behind, x_sem)
        c = dict(ident=ident, identb=identb, half=half, rev=rev, tri=tri, ones=ones, adj=adj, ids=ids, nobody=nobody,
                 le=le, iota=iota)
        state = dict(base=sb("base1", [128, NE]), w=sb("w1", [128, 2, PAIRS]))
        phase_attn1(nc, W, x, banks, c, state, list1)
        rows1 = nc.dram_tensor("rows1", (2 * TOKENS + TRASH, C), F32, kind="Internal").ap()
        phase_experts(nc, banks, c, state, list1, rows1, A["c_wall1"], True, "m1")
        state2 = dict(base=sb("base2", [128, NE]), w=sb("w2", [128, 2, PAIRS]))
        phase_gnn1(nc, W, x, banks, c, state, rows1, state2, list2)
        rows2 = nc.dram_tensor("rows2", (2 * TOKENS + TRASH, C), F32, kind="Internal").ap()
        phase_experts(nc, banks, c, state2, list2, rows2, A["c_wall2"], False, "m2")
        phase_finish(nc, x, state2, rows2, out_dram)


def norm_stats(dve, src, st, mv, ve, bn, agg, vs, g, eps, gate, waits=()):
    for w in waits:
        dve.wait_ge(*w)
    dve.sem_inc(gate.sem, 1)
    for p in range(PG):
        dve.bn_stats(st[:, p, :], src(p)).then_inc(bn.sem, 1)
    dve.wait_ge(*bn.now(g, PG - 1))
    dve.sem_inc(gate.sem, 1)
    for p in range(PG):
        dve.bn_aggr(mv[:, p, :], st[:, p, :]).then_inc(agg.sem, 1)
    dve.wait_ge(*agg.now(g, PG - 1))
    dve.tensor_scalar(ve[:, :], mv[:, :, 1], eps, None, ALU.add).then_inc(vs.sem, 1)


def phase_gnn0(nc, A, x, ident, identb, half, maskb, adj, banks, behind, x_sem):
    with ExitStack() as ctx:
        def sb(name, shape, dt=F32):
            return ctx.enter_context(nc.sbuf_tensor("g0_" + name, shape, dt))

        def sig(name, per=1):
            return Signal(take_semaphore(ctx, nc, "g0_" + name), per)

        wqkv = sb("wqkv", [128, 3 * C])
        wq = sb("wq", [128, 2, 2, 128])
        wk = sb("wk", [128, 2, 2, 128])
        w1 = sb("w1", [128, C])
        w2 = sb("w2", [128, C])
        vecs = sb("vecs", [128, 5, C])
        b1 = sb("b1", [128, 1])
        xn = [sb(f"xn{i}", [128, PG, C]) for i in range(2)]
        st0, st1, st2 = [sb(f"st{i}", [128, PG, 6]) for i in range(3)]
        mv0, mv1, mv2 = [sb(f"mv{i}", [128, PG, 2]) for i in range(3)]
        ve0, ve1, ve2 = [sb(f"ve{i}", [128, PG]) for i in range(3)]
        rs0, rs1, rs2 = [sb(f"rs{i}", [128, PG]) for i in range(3)]
        xT = sb("xT", [128, GT])
        qs = [sb(f"q{i}", [128, 2, PG, 2, NODES]) for i in range(2)]
        ks = [sb(f"k{i}", [128, 2, PG, 4, NODES]) for i in range(2)]
        vs = [sb(f"v{i}", [128, 2 * PG, 4, 2, D0 + 1]) for i in range(2)]
        s = sb("s", [128, 2, H0, NODES])
        mx = sb("mx", [128, 2, H0])
        pt = sb("pt", [128, 2, 4, 128])
        rc = sb("rc", [128, 2, H0])
        ts = [sb(f"t{i}", [128, PG, C]) for i in range(2)]
        y1 = sb("y1", [128, PG, C])
        y1b = sb("y1b", [128, PG, C])
        y1T = sb("y1T", [128, GT])
        hT = sb("hT", [128, GT])
        u = sb("u", [128, PG, C])

        load = take_semaphore(ctx, nc, "g0_load")
        setup = take_semaphore(ctx, nc, "g0_setup")
        gate = sig("gate")
        bn0, ag0, ve0_ready = sig("bn0", PG), sig("ag0", PG), sig("ve0_ready")
        bn1, ag1, ve1_ready = sig("bn1", PG), sig("ag1", PG), sig("ve1_ready")
        bn2, ag2, ve2_ready = sig("bn2", PG), sig("ag2", PG), sig("ve2_ready")
        xn_ready = sig("xn_ready", PG)
        mx_ready = sig("mx_ready", PG)
        s_ready = sig("s_ready", PG)
        rc_ready = sig("rc_ready", PG)
        o_ready = sig("o_ready", PG)
        t_ready = sig("t_ready")
        n1_ready = sig("n1_ready", PG)
        u_ready = sig("u_ready")
        n2_ready = sig("n2_ready", PG)
        dve_signals = [bn0, ag0, ve0_ready, bn1, ag1, ve1_ready, bn2, ag2, ve2_ready, xn_ready, mx_ready,
                       s_ready, rc_ready, o_ready, t_ready, n1_ready, u_ready, n2_ready]
        xT_ready, q_ready, k_ready = sig("xT_ready"), sig("q_ready", 2), sig("k_ready", 4)
        v_ready, e_ready, pt_ready = sig("v_ready", 2), sig("e_ready", PG), sig("pt_ready", PG)
        y1T_ready, hT_ready = sig("y1T_ready"), sig("hT_ready")
        act_signals = [xT_ready, q_ready, k_ready, v_ready, e_ready, pt_ready, y1T_ready, hT_ready]
        rs0_ready, rs1_ready, rs2_ready = sig("rs0_ready"), sig("rs1_ready"), sig("rs2_ready")
        y1m, y1_ready, y1b_ready = sig("y1m"), sig("y1_ready"), sig("y1b_ready")
        fin = sig("fin", 3)
        pool_signals = [rs0_ready, rs1_ready, rs2_ready, y1m, y1_ready, y1b_ready, fin]
        pe_xT, pe_q, pe_k, pe_v = sig("pe_xT"), sig("pe_q", 2), sig("pe_k"), sig("pe_v")
        pe_s, pe_pt, pe_o = sig("pe_s", PG), sig("pe_pt", PG), sig("pe_o", PG)
        pe_y1T, pe_h, pe_f = sig("pe_y1T"), sig("pe_h"), sig("pe_f")
        pe_signals = [pe_xT, pe_q, pe_k, pe_v, pe_s, pe_pt, pe_o, pe_y1T, pe_h, pe_f]

        bT, bQ0, bQ1, bF, bS0, bS1, bPT, bO = banks

        with nc.Block() as block:
            @block.sync
            def _(sp):
                sp.dma_start(wqkv[:, :], A["L0_gnn_w_qkv"]).then_inc(load, 16)
                sp.dma_start(w1[:, :], A["L0_gnn_w1"]).then_inc(load, 16)
                sp.dma_start(w2[:, :], A["L0_gnn_w2"]).then_inc(load, 16)
                for i, name in enumerate(["ln1_g", "ln1_b", "ln2_g", "ln2_b", "b2"]):
                    sp.dma_start(vecs[:, i, :], row_bcast(A["L0_gnn_" + name])).then_inc(load, 16)
                sp.dma_start(b1[:, :], A["L0_gnn_b1"].rearrange("(c a) -> c a", a=1)).then_inc(load, 16)
                sp.wait_ge(load, 16 * 9)

            @block.gpsimd
            def _(pool):
                for i, z in enumerate([wq, wk]):
                    pool.memset(z[:, :, :, :], 0.0).then_inc(setup, 1)
                for i in range(2):
                    pool.memset(ks[i][:, :, :, :, :], 0.0).then_inc(setup, 1)
                    pool.memset(vs[i][:, :, :, :, :], 0.0).then_inc(setup, 1)
                pool.wait_ge(setup, 6)
                for h2 in range(2):
                    for i in range(2):
                        pool.memset(vs[i][64 * h2:64 * h2 + 64, :, :, h2, D0:D0 + 1], 1.0).then_inc(setup, 1)
                    pool.wait_ge(setup, 8 + 2 * h2)
                pool.wait_ge(load, 16 * 9)
                for n, w in enumerate([wq, wk]):
                    for j in range(2):
                        for f in range(2):
                            dst = w[:, j, f, :].rearrange("c (h f d) -> c h f d", h=4, f=2)[:, :, f, :]
                            src = wqkv[:, n * C + 64 * j:n * C + 64 * j + 64].rearrange("c (h d) -> c h d", h=4)
                            pool.tensor_copy(dst, src).then_inc(setup, 1)
                open_signals(pool, pool_signals)

            @block.vector
            def _(dve):
                dve.tensor_scalar(maskb[:, :], adj[:, :], 0.0, -4e9, ALU.is_le, ALU.mult)
                open_signals(dve, dve_signals)

            @block.scalar
            def _(act):
                open_signals(act, act_signals)

            @block.tensor
            def _(pe):
                open_signals(pe, pe_signals)

        def xg(i):
            return x[:, bass.ds(i * PG, PG), :]

        def xp(i, p):
            return x[:, bass.ds(i * PG + p, 1), :].rearrange("p a c -> p (a c)")

        with nc.Block() as block:
            @block.sync
            def _(sp):
                behind(sp)

            @block.tensor
            def _(pe):
                xTv = xT[:, :].rearrange("c (p f n) -> c p f n", p=PG, f=2)

                def head_T(i, b):
                    if not runs(i):
                        return
                    pe.wait_ge(*xn_ready.now(i, PG - 1))
                    pe.wait_ge(*y1T_ready.before(i, turns=3))
                    for p in range(PG):
                        ins = pe.transpose(bT[:, 128 * p:128 * p + 128], xn[b][:, p, :], ident[:, :])
                    ins.then_inc(pe_xT.sem, 1)

                def head_q(i):
                    if not runs(i):
                        return
                    pe.wait_ge(*xT_ready.now(i))
                    pe.wait_ge(*k_ready.before(i))
                    pe.wait_ge(*v_ready.before(i))
                    for j, bank in enumerate([bQ0, bQ1]):
                        bv = bank[:, :].rearrange("c (p f n) -> c p f n", p=PG, f=2)
                        for f in range(2):
                            ins = pe.matmul(bv[:, :, f, :], wq[:, j, f, :], xTv[:, :, f, :], start=(f == 0), stop=True,
                                            skip_group_check=True)
                        ins.then_inc(pe_q.sem, 1)

                def head_k(i):
                    if not runs(i):
                        return
                    pe.wait_ge(*q_ready.now(i, 0))
                    kv = bQ0[:, :].rearrange("c (j p n) -> c j p n", j=2, p=PG)
                    for j in range(2):
                        for f in range(2):
                            ins = pe.matmul(kv[:, j, :, :], wk[:, j, f, :], xTv[:, :, f, :], start=(f == 0), stop=(f == 1),
                                            skip_group_check=True)
                    ins.then_inc(pe_k.sem, 1)

                def head_v(i):
                    if not runs(i):
                        return
                    pe.wait_ge(*q_ready.now(i, 1))
                    wv = wqkv[:, 2 * C:3 * C].rearrange("c (hp h2 d) -> c hp h2 d", hp=4, h2=2)
                    for fr in range(2 * PG):
                        for h2 in range(2):
                            ins = pe.matmul(bQ1[64 * h2:64 * h2 + 64, 64 * fr:64 * fr + 64], xT[:, 64 * fr:64 * fr + 64],
                                            wv[:, :, h2, :], start=(fr == 0), stop=True, skip_group_check=True)
                    ins.then_inc(pe_v.sem, 1)

                def scores(i, p, b):
                    if not runs(i):
                        return
                    bank = [bS0, bS1][p % 2]
                    pe.wait_ge(*k_ready.now(i, 3))
                    pe.wait_ge(*s_ready.now(i, p - 2))
                    mk = bass.AP(maskb, 0, [maskb[:, :].ap[0], [0, H0], [1, NODES]])
                    pe.matmul(bank[:, :], identb[:, :], mk, start=True, stop=False, skip_group_check=True)
                    for j in range(2):
                        ins = pe.matmul(bank[:, 256 * j:256 * j + 256], qs[b][:, j, p, :, :].rearrange("c f n -> c (f n)"),
                                        ks[b][:, j, p, :, :].rearrange("c h m -> c (h m)"), start=False, stop=True,
                                        skip_group_check=True)
                    ins.then_inc(pe_s.sem, 1)

                def probs_T(i, p):
                    if not runs(i):
                        return
                    pe.wait_ge(*e_ready.now(i, p))
                    pe.wait_ge(*pt_ready.now(i, p - 1))
                    for hp in range(4):
                        ins = pe.transpose(bPT[:, 128 * hp:128 * hp + 128],
                                           s[:, p % 2, 2 * hp:2 * hp + 2, :].rearrange("p h m -> p (h m)"), ident[:, :])
                    ins.then_inc(pe_pt.sem, 1)

                def mix(i, p, b):
                    if not runs(i):
                        return
                    pe.wait_ge(*pt_ready.now(i, p))
                    pe.wait_ge(*v_ready.now(i, 1))
                    pe.wait_ge(*o_ready.now(i, p - 1))
                    w = 2 * (D0 + 1)
                    for f in range(2):
                        for hp in range(4):
                            ins = pe.matmul(bO[64 * f:64 * f + 64, w * hp:w * hp + w],
                                            pt[:, p % 2, hp, 64 * f:64 * f + 64],
                                            vs[b][:, 2 * p + f, hp, :, :].rearrange("m h d -> m (h d)"),
                                            start=(hp == 0), stop=True, skip_group_check=True)
                    ins.then_inc(pe_o.sem, 1)

                def ffn_T(i):
                    if not runs(i):
                        return
                    pe.wait_ge(*y1_ready.now(i))
                    if runs(i + 2):
                        pe.wait_ge(*xT_ready.now(i + 2))
                    for p in range(PG):
                        ins = pe.transpose(bT[:, 128 * p:128 * p + 128], y1[:, p, :], ident[:, :])
                    ins.then_inc(pe_y1T.sem, 1)

                def ffn_1(i):
                    if not runs(i):
                        return
                    pe.wait_ge(*y1T_ready.now(i))
                    pe.wait_ge(*u_ready.before(i))
                    pe.matmul(bF[:, :], w1[:, :], y1T[:, :], start=True, stop=True).then_inc(pe_h.sem, 1)

                def ffn_2(i):
                    if not runs(i):
                        return
                    pe.wait_ge(*hT_ready.now(i))
                    for p in range(PG):
                        ins = pe.matmul(bF[:, 128 * p:128 * p + 128], hT[:, 128 * p:128 * p + 128], w2[:, :],
                                        start=(p == 0), stop=True, skip_group_check=True)
                    ins.then_inc(pe_f.sem, 1)

                def step(g, b):
                    scores(g, 0, b)
                    scores(g, 1, b)
                    head_T(g + 1, 1 - b)
                    probs_T(g, 0)
                    head_q(g + 1)
                    mix(g, 0, b)
                    scores(g, 2, b)
                    probs_T(g, 1)
                    head_k(g + 1)
                    mix(g, 1, b)
                    scores(g, 3, b)
                    probs_T(g, 2)
                    ffn_T(g - 1)
                    head_v(g + 1)
                    mix(g, 2, b)
                    probs_T(g, 3)
                    ffn_1(g - 1)
                    mix(g, 3, b)
                    ffn_2(g - 1)
                skewed(pe, step)

            @block.scalar
            def _(act):
                def head_xT(i):
                    if not runs(i):
                        return
                    act.wait_ge(*pe_xT.now(i))
                    act.wait_ge(*pe_v.before(i))
                    act.activation(xT[:, :], bT[:, :], ACT.Copy).then_inc(xT_ready.sem, 1)

                def head_q(i, b):
                    if not runs(i):
                        return
                    for j, bank in enumerate([bQ0, bQ1]):
                        act.wait_ge(*pe_q.now(i, j))
                        act.wait_ge(*pe_s.before(i, turns=2))
                        act.activation(qs[b][:, j, :, :, :].rearrange("c p f n -> c (p f n)"), bank[:, :], ACT.Copy)\
                           .then_inc(q_ready.sem, 1)

                def head_k(i, b):
                    if not runs(i):
                        return
                    kv = bQ0[:, :].rearrange("c (j p n) -> c j p n", j=2, p=PG)
                    act.wait_ge(*pe_k.now(i))
                    act.wait_ge(*pe_s.before(i, turns=2))
                    for h4 in range(4):
                        r = slice(32 * h4, 32 * h4 + 32)
                        act.activation(ks[b][r, :, :, h4, :], kv[r, :, :, :], ACT.Copy).then_inc(k_ready.sem, 1)

                def head_v(i, b):
                    if not runs(i):
                        return
                    act.wait_ge(*pe_o.before(i, turns=2))
                    act.wait_ge(*pe_v.now(i))
                    bv = bQ1[:, :].rearrange("m (f hp d) -> m f hp d", f=2 * PG, hp=4)
                    for h2 in range(2):
                        r = slice(64 * h2, 64 * h2 + 64)
                        act.activation(vs[b][r, :, :, h2, 0:D0], bv[r, :, :, :], ACT.Copy).then_inc(v_ready.sem, 1)

                def exp(i, p):
                    if not runs(i):
                        return
                    act.wait_ge(*s_ready.now(i, p))
                    act.activation(s[:, p % 2, :, :], s[:, p % 2, :, :], ACT.Exp, scale=0.25).then_inc(e_ready.sem, 1)

                def probs_T(i, p):
                    if not runs(i):
                        return
                    act.wait_ge(*pe_pt.now(i, p))
                    act.wait_ge(*pe_o.now(i, p - 2))
                    act.activation(pt[:, p % 2, :, :].rearrange("m h n -> m (h n)"), bPT[:, :], ACT.Copy)\
                       .then_inc(pt_ready.sem, 1)

                def ffn_T(i):
                    if not runs(i):
                        return
                    act.wait_ge(*pe_y1T.now(i))
                    act.wait_ge(*pe_h.before(i))
                    act.activation(y1T[:, :], bT[:, :], ACT.Copy).then_inc(y1T_ready.sem, 1)

                def ffn_h(i):
                    if not runs(i):
                        return
                    act.wait_ge(*pe_h.now(i))
                    act.wait_ge(*pe_f.before(i))
                    act.activation(hT[:, :], bF[:, :], ACT.Relu, bias=b1[:, 0:1]).then_inc(hT_ready.sem, 1)

                def step(g, b):
                    exp(g, 0)
                    head_xT(g + 1)
                    probs_T(g, 0)
                    exp(g, 1)
                    head_q(g + 1, 1 - b)
                    probs_T(g, 1)
                    exp(g, 2)
                    head_k(g + 1, 1 - b)
                    probs_T(g, 2)
                    ffn_T(g - 1)
                    exp(g, 3)
                    head_v(g + 1, 1 - b)
                    probs_T(g, 3)
                    ffn_h(g - 1)
                skewed(act, step)

            @block.vector
            def _(dve):
                def head_stats(i):
                    if runs(i):
                        norm_stats(dve, lambda p: xp(i, p), st0, mv0, ve0, bn0, ag0, ve0_ready, i, EPS_LN, gate,
                                   [rs0_ready.before(i)])

                def head_xn(i, b):
                    if not runs(i):
                        return
                    dve.wait_ge(*rs0_ready.now(i))
                    dve.wait_ge(*pe_xT.before(i, turns=2))
                    dve.wait_ge(*t_ready.before(i, turns=2))
                    for p in range(PG):
                        dve.tensor_scalar(xn[b][:, p, :], xp(i, p), mv0[:, p, 0:1], rs0[:, p:p + 1],
                                          ALU.subtract, ALU.mult).then_inc(xn_ready.sem, 1)

                def soft(i, p):
                    if not runs(i):
                        return
                    bank = [bS0, bS1][p % 2]
                    bv = bank[:, :].rearrange("p (h m) -> p h m", h=H0)
                    dve.wait_ge(*pe_s.now(i, p))
                    dve.wait_ge(*s_ready.now(i, p - 2))
                    dve.tensor_reduce(mx[:, p % 2, :], bv, AX.X, ALU.max).then_inc(mx_ready.sem, 1)
                    dve.wait_ge(*mx_ready.now(i, p))
                    dve.wait_ge(*pe_pt.now(i, p - 2))
                    m = mx[:, p % 2, :]
                    dve.tensor_tensor(s[:, p % 2, :, :], bv, bass.AP(m.tensor, m.offset, [m.ap[0], [1, H0], [0, NODES]]),
                                      ALU.subtract).then_inc(s_ready.sem, 1)

                def norm(i, p, b):
                    if not runs(i):
                        return
                    bv = bO[:, 0:H0 * (D0 + 1)].rearrange("n (h d) -> n h d", h=H0)
                    dve.wait_ge(*pe_o.now(i, p))
                    dve.wait_ge(*o_ready.now(i, p - 2))
                    dve.reciprocal(rc[:, p % 2, :], bv[:, :, D0]).then_inc(rc_ready.sem, 1)
                    dve.wait_ge(*rc_ready.now(i, p))
                    if p == 0:
                        dve.wait_ge(*y1m.before(i, turns=2))
                    m = rc[:, p % 2, :]
                    dve.tensor_tensor(ts[b][:, p, :].rearrange("n (h d) -> n h d", h=H0), bv[:, :, 0:D0],
                                      bass.AP(m.tensor, m.offset, [m.ap[0], [1, H0], [0, D0]]), ALU.mult)\
                       .then_inc(o_ready.sem, 1)

                def ffn_residual(i, b):
                    if not runs(i):
                        return
                    dve.wait_ge(*o_ready.now(i, PG - 1))
                    dve.tensor_tensor(ts[b][:, :, :], ts[b][:, :, :], xn[b][:, :, :], ALU.add).then_inc(t_ready.sem, 1)

                def ffn_stats(i, b):
                    if not runs(i):
                        return
                    norm_stats(dve, lambda p: ts[b][:, p, :], st1, mv1, ve1, bn1, ag1, ve1_ready, i, EPS_LN, gate,
                               [t_ready.now(i), rs1_ready.before(i)])

                def ffn_norm(i, b):
                    if not runs(i):
                        return
                    dve.wait_ge(*rs1_ready.now(i))
                    for p in range(PG):
                        dve.tensor_scalar(ts[b][:, p, :], ts[b][:, p, :], mv1[:, p, 0:1], rs1[:, p:p + 1],
                                          ALU.subtract, ALU.mult).then_inc(n1_ready.sem, 1)

                def last_u(i):
                    if not runs(i):
                        return
                    dve.wait_ge(*pe_f.now(i))
                    dve.wait_ge(*y1b_ready.now(i))
                    dve.wait_ge(*fin.before(i))
                    dve.tensor_tensor(u[:, :, :], bF[:, :].rearrange("p (t c) -> p t c", t=PG), y1b[:, :, :], ALU.add)\
                       .then_inc(u_ready.sem, 1)

                def last_stats(i):
                    if not runs(i):
                        return
                    norm_stats(dve, lambda p: u[:, p, :], st2, mv2, ve2, bn2, ag2, ve2_ready, i, EPS_LN, gate,
                               [u_ready.now(i), rs2_ready.before(i)])

                def last_norm(i):
                    if not runs(i):
                        return
                    dve.wait_ge(*rs2_ready.now(i))
                    for p in range(PG):
                        dve.tensor_scalar(u[:, p, :], u[:, p, :], mv2[:, p, 0:1], rs2[:, p:p + 1],
                                          ALU.subtract, ALU.mult).then_inc(n2_ready.sem, 1)

                def step(g, b):
                    if isinstance(g, int) and g == 1:
                        dve.wait_ge(x_sem, 16 * 4)
                    ffn_residual(g - 1, 1 - b)
                    head_xn(g + 1, 1 - b)
                    soft(g, 0)
                    soft(g, 1)
                    ffn_stats(g - 1, 1 - b)
                    last_u(g - 2)
                    norm(g, 0, b)
                    ffn_norm(g - 1, 1 - b)
                    soft(g, 2)
                    last_stats(g - 2)
                    norm(g, 1, b)
                    soft(g, 3)
                    head_stats(g + 2)
                    norm(g, 2, b)
                    last_norm(g - 2)
                    norm(g, 3, b)
                skewed(dve, step)

            @block.gpsimd
            def _(pool):
                def vec(i):
                    w = vecs[:, i, :]
                    return bass.AP(w.tensor, w.offset, [w.ap[0], [0, PG], [1, C]])

                def head_rs(i):
                    if not runs(i):
                        return
                    pool.wait_ge(*ve0_ready.now(i))
                    pool.wait_ge(*xn_ready.before(i))
                    pool.tensor_tensor(rs0[:, :], ve0[:, :], half[:, 0:PG], ALU.pow).then_inc(rs0_ready.sem, 1)

                def ffn_rs(i):
                    if not runs(i):
                        return
                    pool.wait_ge(*ve1_ready.now(i))
                    pool.wait_ge(*n1_ready.before(i))
                    pool.tensor_tensor(rs1[:, :], ve1[:, :], half[:, 0:PG], ALU.pow).then_inc(rs1_ready.sem, 1)

                def ffn_y1(i, b):
                    if not runs(i):
                        return
                    pool.wait_ge(*n1_ready.now(i, PG - 1))
                    pool.wait_ge(*pe_y1T.before(i))
                    pool.wait_ge(*y1b_ready.before(i))
                    pool.tensor_tensor(y1[:, :, :], ts[b][:, :, :], vec(0), ALU.mult).then_inc(y1m.sem, 1)
                    pool.wait_ge(*y1m.now(i))
                    pool.tensor_tensor(y1[:, :, :], y1[:, :, :], vec(1), ALU.add).then_inc(y1_ready.sem, 1)

                def ffn_y1b(i):
                    if not runs(i):
                        return
                    pool.wait_ge(*y1_ready.now(i))
                    pool.wait_ge(*u_ready.before(i))
                    pool.tensor_tensor(y1b[:, :, :], y1[:, :, :], vec(4), ALU.add).then_inc(y1b_ready.sem, 1)

                def last_rs(i):
                    if not runs(i):
                        return
                    pool.wait_ge(*ve2_ready.now(i))
                    pool.wait_ge(*n2_ready.before(i))
                    pool.tensor_tensor(rs2[:, :], ve2[:, :], half[:, 0:PG], ALU.pow).then_inc(rs2_ready.sem, 1)

                def last_x(i):
                    if not runs(i):
                        return
                    pool.wait_ge(*n2_ready.now(i, PG - 1))
                    pool.tensor_tensor(u[:, :, :], u[:, :, :], vec(2), ALU.mult).then_inc(fin.sem, 1)
                    pool.wait_ge(*fin.now(i, 0))
                    pool.tensor_tensor(u[:, :, :], u[:, :, :], vec(3), ALU.add).then_inc(fin.sem, 1)
                    pool.wait_ge(*fin.now(i, 1))
                    pool.tensor_tensor(xg(i), xg(i), u[:, :, :], ALU.add).then_inc(fin.sem, 1)

                def step(g, b):
                    ffn_rs(g - 1)
                    ffn_y1(g - 1, 1 - b)
                    last_rs(g - 2)
                    ffn_y1b(g - 1)
                    head_rs(g + 2)
                    last_x(g - 2)
                skewed(pool, step)
        clear_taken(nc)


class Routing:

    def __init__(self, ctx, nc, name, consts, state):
        def sb(n, shape, dt=F32):
            return ctx.enter_context(nc.sbuf_tensor(f"{name}_{n}", shape, dt))

        def sig(n, per=1):
            return Signal(take_semaphore(ctx, nc, f"{name}_{n}"), per)

        self.c, self.state = consts, state
        self.lg = sb("lg", [128, PG, NE])
        self.eq = sb("eq", [128, PG, NE])
        self.m = sb("m", [128, 2, PG])
        self.key = sb("key", [128, 2, PG])
        self.oh = sb("oh", [128, 2, PG, NE])
        self.both = sb("both", [128, PG, NE], BF16)
        self.d = sb("d", [128, PAIRS, NE + 1])
        self.z = sb("z", [128, PAIRS])
        self.rows = sb("rows", [128, PG + 1, NE])
        self.pick = sb("pick", [128, 2, PG, NE])
        self.posf = sb("posf", [128, 2, PG])
        self.pos = sb("pos", [128, 2, PG], I32)
        self.step = sig("step", 12)
        self.both_ready = sig("both_ready")
        self.d_ready = sig("d_ready", 2)
        self.e_ready = sig("e_ready")
        self.wstep = sig("wstep", 5)
        self.pstep = sig("pstep", 5)
        self.pe_logits = sig("pe_logits")
        self.pe_rank = sig("pe_rank")
        self.gate = sig("gate")
        self.landed = take_semaphore(ctx, nc, f"{name}_landed")
        self.dve_signals = [self.step, self.both_ready, self.d_ready, self.wstep, self.pstep]
        self.act_signals = [self.e_ready]
        self.pe_signals = [self.pe_logits, self.pe_rank]
        self.tagged = sig("tagged", 2)
        self.pool_signals = [self.tagged]

    def tensor_logits(self, pe, bank, flatT, wr):
        for p in range(PG):
            i = pe.matmul(bank[:, NE * p:NE * p + NE], flatT[:, 128 * p:128 * p + 128], wr[:, :],
                          start=(p == 0), stop=True, skip_group_check=True)
        i.then_inc(self.pe_logits.sem, 1)

    def tensor_rank(self, pe, g, bank):
        pe.wait_ge(*self.both_ready.now(g))
        pe.wait_ge(*self.step.now(g, 0))
        r = bank[:, 64:64 + NE * (PG + 1)]
        pe.matmul(r[:, 0:NE * PG], self.c["tri"][:, :], self.both[:, :, :].rearrange("t p e -> t (p e)"),
                  start=True, stop=False, skip_group_check=True)
        for q in range(PG):
            m = self.both[:, q, :]
            i = pe.matmul(r[:, NE * (q + 1):NE * (PG + 1)], self.c["ones"][:, :],
                          bass.AP(m.tensor, m.offset, [m.ap[0], [0, PG - q], [1, NE]]),
                          start=False, stop=(q == PG - 1), skip_group_check=True)
        i.then_inc(self.pe_rank.sem, 1)

    def vector_choose(self, dve, g, bank, with_z):
        c = self.c

        def over_e(ap):
            return bass.AP(ap.tensor, ap.offset, [ap.ap[0], [1, PG], [0, NE]])

        rev = bass.AP(c["rev"], 0, [c["rev"][:, :].ap[0], [0, PG], [1, NE]])
        s = self.step
        dve.wait_ge(*self.pe_logits.now(g))
        bv = bank[:, 0:NE * PG].rearrange("t (p e) -> t p e", p=PG)
        if self.state.get("bias") is not None:
            b = self.state["bias"]
            dve.tensor_tensor(self.lg[:, :, :], bv, bass.AP(b, 0, [b[:, :].ap[0], [0, PG], [1, NE]]), ALU.add)\
               .then_inc(s.sem, 1)
        else:
            dve.tensor_copy(self.lg[:, :, :], bv).then_inc(s.sem, 1)
        src = self.lg[:, :, :]
        n = 1
        for k in range(2):
            dve.wait_ge(*s.now(g, n - 1))
            if k == 0:
                dve.wait_ge(*self.tagged.before(g))
            dve.tensor_reduce(self.m[:, k, :], src, AX.X, ALU.max).then_inc(s.sem, 1)
            dve.wait_ge(*s.now(g, n))
            dve.tensor_tensor(self.eq[:, :, :], src, over_e(self.m[:, k, :]), ALU.is_equal).then_inc(s.sem, 1)
            dve.wait_ge(*s.now(g, n + 1))
            dve.tensor_tensor(self.eq[:, :, :], self.eq[:, :, :], rev, ALU.mult).then_inc(s.sem, 1)
            dve.wait_ge(*s.now(g, n + 2))
            dve.tensor_reduce(self.key[:, k, :], self.eq[:, :, :], AX.X, ALU.max).then_inc(s.sem, 1)
            dve.wait_ge(*s.now(g, n + 3))
            if k == 0:
                dve.wait_ge(*self.pstep.before(g))
            dve.tensor_tensor(self.oh[:, k, :, :], rev, over_e(self.key[:, k, :]), ALU.is_equal).then_inc(s.sem, 1)
            n += 5
            if k == 0:
                dve.wait_ge(*s.now(g, n - 1))
                dve.scalar_tensor_tensor(out=self.eq[:, :, :].rearrange("t p e -> t (p e)"),
                                         in0=self.oh[:, 0, :, :].rearrange("t p e -> t (p e)"), scalar=-1e30,
                                         in1=self.lg[:, :, :].rearrange("t p e -> t (p e)"),
                                         op0=ALU.mult, op1=ALU.add).then_inc(s.sem, 1)
                n += 1
                src = self.eq[:, :, :]
        dve.wait_ge(*s.now(g, n - 1))
        dve.wait_ge(*self.pe_rank.before(g))
        dve.tensor_tensor(self.both[:, :, :], self.oh[:, 0, :, :], self.oh[:, 1, :, :], ALU.add)\
           .then_inc(self.both_ready.sem, 1)
        d = self.d[:, bass.ds(g * PG, PG), :]
        dve.tensor_tensor(d[:, :, NE], self.m[:, 1, :], self.m[:, 0, :], ALU.subtract).then_inc(self.d_ready.sem, 1)
        if with_z:
            dve.tensor_tensor(d[:, :, 0:NE], self.lg[:, :, :], over_e(self.m[:, 0, :]), ALU.subtract)\
               .then_inc(self.d_ready.sem, 1)
        else:
            dve.sem_inc(self.d_ready.sem, 1)

    def scalar_exp(self, act, with_z):
        act.wait_ge(*self.d_ready.now(GROUPS - 1, 1))
        lo = 0 if with_z else NE
        act.activation(self.d[:, :, lo:NE + 1], self.d[:, :, lo:NE + 1], ACT.Exp).then_inc(self.e_ready.sem, 1)

    def vector_weights(self, dve, with_z):
        w = self.state["w"]
        s = self.wstep
        dve.wait_ge(*self.e_ready.now(0))
        e2 = self.d[:, :, NE]
        if with_z:
            dve.tensor_reduce(self.z[:, :], self.d[:, :, 0:NE], AX.X, ALU.add).then_inc(s.sem, 1)
            dve.wait_ge(*s.now(0, 0))
            dve.scalar_tensor_tensor(out=self.z[:, :], in0=self.z[:, :], scalar=1e-9, in1=e2,
                                     op0=ALU.mult, op1=ALU.add).then_inc(s.sem, 1)
        else:
            dve.sem_inc(s.sem, 1)
            dve.tensor_copy(self.z[:, :], e2).then_inc(s.sem, 1)
        dve.wait_ge(*s.now(0, 1))
        dve.tensor_scalar(self.z[:, :], self.z[:, :], 1.0, None, ALU.add).then_inc(s.sem, 1)
        dve.wait_ge(*s.now(0, 2))
        dve.reciprocal(w[:, 0, :], self.z[:, :]).then_inc(s.sem, 1)
        dve.wait_ge(*s.now(0, 3))
        dve.tensor_tensor(w[:, 1, :], w[:, 0, :], e2, ALU.mult).then_inc(s.sem, 1)
        dve.wait_ge(*s.now(0, 4))

    def vector_rows(self, dve, g, bank):
        base = self.state["base"]
        s = self.pstep
        dve.wait_ge(*self.pe_rank.now(g))
        dve.wait_ge(*s.before(g))
        b = base[:, :]
        dve.tensor_tensor(self.rows[:, :, :], bank[:, 64:64 + NE * (PG + 1)].rearrange("t (p e) -> t p e", e=NE),
                          bass.AP(b.tensor, b.offset, [b.ap[0], [0, PG + 1], [1, NE]]), ALU.add).then_inc(s.sem, 1)
        dve.wait_ge(*s.now(g, 0))
        dve.tensor_copy(base[:, :], self.rows[:, PG, :]).then_inc(s.sem, 1)
        r = self.rows[:, 0:PG, :]
        dve.tensor_tensor(self.pick[:, :, :, :].rearrange("t k p e -> t k (p e)"),
                          self.oh[:, :, :, :].rearrange("t k p e -> t k (p e)"),
                          bass.AP(r.tensor, r.offset, [r.ap[0], [0, 2], [1, PG * NE]]), ALU.mult).then_inc(s.sem, 1)
        dve.wait_ge(*s.now(g, 2))
        dve.tensor_reduce(self.posf[:, :, :], self.pick[:, :, :, :], AX.X, ALU.add).then_inc(s.sem, 1)
        dve.wait_ge(*s.now(g, 3))
        self.wait_landed(dve, g - 1)
        dve.tensor_copy(self.pos[:, :, :], self.posf[:, :, :]).then_inc(s.sem, 1)

    def wait_landed(self, eng, i):
        if not isinstance(i, int) or i >= 0:
            eng.wait_ge(self.landed, (i + 1) * (16 * 2 * PG))

    def pool_scatter(self, pool, g, flat, dest):
        pool.wait_ge(*self.tagged.before(g, turns=2))
        pool.wait_ge(*self.step.now(g, 4))
        pool.sem_inc(self.gate.sem, 1)
        pool.tensor_copy(flat[:, :, C], self.c["ids"][:, bass.ds(g * PG, PG)]).then_inc(self.tagged.sem, 1)
        pool.tensor_copy(flat[:, :, C + 1], self.key[:, 0, :]).then_inc(self.tagged.sem, 1)
        pool.wait_ge(*self.pstep.now(g, 4))
        pool.wait_ge(*self.tagged.now(g, 1))
        pool.sem_inc(self.gate.sem, 1)
        for p in range(PG):
            for k in range(2):
                pool.indirect_dma_start(out=dest, out_offset=bass.IndirectOffsetOnAxis(ap=self.pos[:, k, p:p + 1], axis=0),
                                        in_=flat[:, p, :], in_offset=None).then_inc(self.landed, 16)


def phase_attn1(nc, W, x, banks, c, state, dest):
    ident, identb, half = c["ident"], c["identb"], c["half"]
    with ExitStack() as ctx:
        def sb(name, shape, dt=F32):
            return ctx.enter_context(nc.sbuf_tensor("a1_" + name, shape, dt))

        def sig(name, per=1):
            return Signal(take_semaphore(ctx, nc, "a1_" + name), per)

        FR = 2 * PG
        wq, wk, wv, wo, wr, lnw, ln2w, rope, causal32 = (W[n] for n in "wq wk wv wo wr lnw ln2w rope causal32".split())
        causal = sb("causal", [128, NODES], BF16)
        st, mv = sb("st", [128, PG, 6]), sb("mv", [128, PG, 2])
        ve, rs = sb("ve", [128, PG]), sb("rs", [128, PG])
        rr = sb("rr", [128, 4, PG])
        ms = sb("ms", [128, 3, PG])
        vn = sb("vn", [128, PAIRS, C])
        h = sb("h", [128, PG, C])
        hT = sb("hT", [128, GT])
        q1, q2, q = sb("q1", [128, FR, NODES]), sb("q2", [128, FR, NODES]), sb("q", [128, FR, NODES])
        k1, k2 = sb("k1", [128, FR, NODES]), sb("k2", [128, FR, NODES])
        k = sb("k", [128, FR, H1, NODES])
        v = sb("v", [128, FR, KV1, 2, D1 + 1])
        s = sb("s", [128, 2, 2, H1, NODES])
        mx = sb("mx", [128, 2, 2, H1])
        pt = sb("pt", [128, 2, 2, KV1, 128])
        rc = sb("rc", [128, 2, 2, H1])
        y = sb("y", [128, PG, C])
        yT = sb("yT", [128, GT])
        x2 = sb("x2", [128, PG, C])
        sq = sb("sq", [128, PG, C])
        flat = [sb(f"flat{i}", [128, PG, ROW]) for i in range(2)]
        fT = sb("fT", [128, GT])
        gate = sig("gate")
        setup = take_semaphore(ctx, nc, "a1_setup")
        R = Routing(ctx, nc, "a1r", c, state)

        bn, part, vs = sig("bn", PG), sig("part", PG), sig("vs")
        vn_ready = sig("vn_ready", PG)
        rms_in = sig("rms_in", 3)
        rope_q, rope_k = sig("rope_q", 2), sig("rope_k", 3)
        q_ready = sig("q_ready")
        mx_ready, s_ready = sig("mx_ready", 2), sig("s_ready", 2)
        rc_ready, y_ready = sig("rc_ready", 2), sig("y_ready", 2)
        x2_ready, ms_ready, flat_ready = sig("x2_ready"), sig("ms_ready"), sig("flat_ready", PG)
        dve_signals = [bn, part, vs, vn_ready, rms_in, rope_q, rope_k, q_ready, mx_ready, s_ready,
                       rc_ready, y_ready, x2_ready, ms_ready, flat_ready] + R.dve_signals
        hT_ready, v_ready, e_ready, pt_ready = sig("hT_ready"), sig("v_ready", 2), sig("e_ready", 2), sig("pt_ready", 2)
        yT_ready, fT_ready = sig("yT_ready"), sig("fT_ready")
        h_ready, sq_ready = sig("h_ready", PG), sig("sq_ready", PG)
        k_ready = sig("k_ready", H1)
        act_signals = [k_ready, h_ready, sq_ready, hT_ready, v_ready, e_ready, pt_ready, yT_ready, fT_ready] + R.act_signals
        rs_ready, rh_ready = sig("rs_ready"), sig("rh_ready")
        rms2_ready, fin = sig("rms2_ready"), sig("fin")
        pool_signals = [rs_ready, rh_ready, rms2_ready, fin]
        pe_hT, pe_q, pe_k, pe_v = sig("pe_hT"), sig("pe_q"), sig("pe_k"), sig("pe_v")
        pe_s, pe_pt, pe_o = sig("pe_s", 2), sig("pe_pt", 2), sig("pe_o", 2)
        pe_yT, pe_x, pe_fT = sig("pe_yT"), sig("pe_x"), sig("pe_fT")
        pe_signals = [pe_hT, pe_q, pe_k, pe_v, pe_s, pe_pt, pe_o, pe_yT, pe_x, pe_fT] + R.pe_signals
        bT, bQ, bQr, bK, bKr, bV, bR, bPT = banks
        S_BANKS = [bQ, bQr]
        PT_BANKS = [bPT, bQr]
        bO = bQ

        with nc.Block() as block:
            @block.gpsimd
            def _(pool):
                pool.memset(k[:, :, :, :], 0.0).then_inc(setup, 1)
                pool.memset(v[:, :, :, :, :], 0.0).then_inc(setup, 1)
                pool.wait_ge(setup, 2)
                for h2 in range(2):
                    pool.memset(v[64 * h2:64 * h2 + 64, :, :, h2, D1:D1 + 1], 1.0).then_inc(setup, 1)
                    pool.wait_ge(setup, 3 + h2)
                open_signals(pool, pool_signals)
                open_signals(pool, R.pool_signals)

            @block.vector
            def _(dve):
                dve.tensor_copy(causal[:, :], causal32[:, :])
                for w in [wq[:, :, :], wk[:, :, :], wv[:, :]]:
                    dve.tensor_scalar(w, w, lnw[:, 0:1], None, ALU.mult)
                dve.tensor_scalar(state["base"][:, :], c["rev"][:, :], -float(CAP), float(NE * CAP), ALU.mult, ALU.add)
                open_signals(dve, dve_signals)

            @block.scalar
            def _(act):
                open_signals(act, act_signals)

            @block.tensor
            def _(pe):
                open_signals(pe, pe_signals)

        def xt(i, p):
            return x[:, bass.ds(i * PG + p, 1), :].rearrange("p a c -> p (a c)")

        def vt(i, p):
            return vn[:, bass.ds(i * PG + p, 1), :].rearrange("p a c -> p (a c)")

        with nc.Block() as block:
            @block.tensor
            def _(pe):
                def head_T(i):
                    if not runs(i):
                        return
                    pe.wait_ge(*h_ready.now(i, PG - 1))
                    if not isinstance(i, int) or i > 3:
                        pe.wait_ge(*fT_ready.before(i, turns=4))
                    for p in range(PG):
                        ins = pe.transpose(bT[:, 128 * p:128 * p + 128], h[:, p, :], ident[:, :])
                    ins.then_inc(pe_hT.sem, 1)

                def head_k(i):
                    if not runs(i):
                        return
                    pe.wait_ge(*hT_ready.now(i))
                    pe.wait_ge(*rope_k.before(i))
                    for n, bank in enumerate([bK, bKr]):
                        ins = pe.matmul(bank[:, :], wk[:, n, :], hT[:, :], start=True, stop=True)
                    ins.then_inc(pe_k.sem, 1)

                def head_v(i):
                    if not runs(i):
                        return
                    pe.wait_ge(*x2_ready.before(i, turns=2))
                    for fr in range(FR):
                        for h2 in range(2):
                            ins = pe.matmul(bV[64 * h2:64 * h2 + 64, 64 * fr:64 * fr + 64], hT[:, 64 * fr:64 * fr + 64],
                                            wv[:, :], start=(fr == 0), stop=True, skip_group_check=True)
                    ins.then_inc(pe_v.sem, 1)

                def head_q(i):
                    if not runs(i):
                        return
                    pe.wait_ge(*s_ready.before(i))
                    pe.wait_ge(*pt_ready.before(i))
                    pe.wait_ge(*y_ready.before(i))
                    for n, bank in enumerate([bQ, bQr]):
                        ins = pe.matmul(bank[:, :], wq[:, n, :], hT[:, :], start=True, stop=True)
                    ins.then_inc(pe_q.sem, 1)

                def scores(i):
                    if not runs(i):
                        return
                    pe.wait_ge(*k_ready.now(i, H1 - 1))
                    pe.wait_ge(*q_ready.now(i))
                    for u in range(2):
                        mk = bass.AP(causal, 0, [causal[:, :].ap[0], [0, 2 * H1], [1, NODES]])
                        pe.matmul(S_BANKS[u][:, :], identb[:, :], mk, start=True, stop=False, skip_group_check=True)
                        for fr in range(4):
                            f, pr = fr % 2, fr // 2
                            ins = pe.matmul(S_BANKS[u][64 * f:64 * f + 64, 256 * pr:256 * pr + 256], q[:, 4 * u + fr, :],
                                            k[:, 4 * u + fr, :, :].rearrange("c h m -> c (h m)"), start=False, stop=True,
                                            skip_group_check=True)
                        ins.then_inc(pe_s.sem, 1)

                def probs_T(i, u):
                    if not runs(i):
                        return
                    pe.wait_ge(*e_ready.now(i, u))
                    pe.wait_ge(*(pt_ready.before(i, 0) if u == 0 else s_ready.now(i, 1)))
                    for pr in range(2):
                        for kv in range(KV1):
                            n = 2 * pr + kv
                            ins = pe.transpose(PT_BANKS[u][:, 128 * n:128 * n + 128],
                                               s[:, u, pr, 2 * kv:2 * kv + 2, :].rearrange("n h m -> n (h m)"), ident[:, :])
                    ins.then_inc(pe_pt.sem, 1)

                def mix(i, u):
                    if not runs(i):
                        return
                    pe.wait_ge(*v_ready.now(i, 1))
                    pe.wait_ge(*pt_ready.now(i, u))
                    pe.wait_ge(*(s_ready.now(i, 0) if u == 0 else y_ready.now(i, 0)))
                    w = 2 * (D1 + 1)
                    for pr in range(2):
                        for kv in range(KV1):
                            for f in range(2):
                                o = w * (KV1 * pr + kv)
                                ins = pe.matmul(bO[64 * f:64 * f + 64, o:o + w], pt[:, u, pr, kv, 64 * f:64 * f + 64],
                                                v[:, 4 * u + 2 * pr + f, kv, :, :].rearrange("m h d -> m (h d)"),
                                                start=(pr == 0 and kv == 0), stop=True, skip_group_check=True)
                    ins.then_inc(pe_o.sem, 1)

                def out_T(i):
                    if not runs(i):
                        return
                    pe.wait_ge(*y_ready.now(i, 1))
                    if runs(i + 2):
                        pe.wait_ge(*hT_ready.now(i + 2))
                    else:
                        pe.wait_ge(*fT_ready.before(i, turns=2))
                    for p in range(PG):
                        ins = pe.transpose(bT[:, 128 * p:128 * p + 128], y[:, p, :], ident[:, :])
                    ins.then_inc(pe_yT.sem, 1)

                def out_product(i):
                    if not runs(i):
                        return
                    pe.wait_ge(*yT_ready.now(i))
                    if runs(i + 1):
                        pe.wait_ge(*v_ready.now(i + 1, 1))
                    for p in range(PG):
                        ins = pe.matmul(bV[:, 128 * p:128 * p + 128], yT[:, 128 * p:128 * p + 128], wo[:, :],
                                        start=(p == 0), stop=True, skip_group_check=True)
                    ins.then_inc(pe_x.sem, 1)

                def flat_T(i, b):
                    if not runs(i):
                        return
                    pe.wait_ge(*flat_ready.now(i, PG - 1))
                    if runs(i + 1):
                        pe.wait_ge(*yT_ready.now(i + 1))
                    for p in range(PG):
                        ins = pe.transpose(bT[:, 128 * p:128 * p + 128], flat[b][:, p, 0:C], ident[:, :])
                    ins.then_inc(pe_fT.sem, 1)

                def logits(i):
                    if not runs(i):
                        return
                    pe.wait_ge(*fT_ready.now(i))
                    pe.wait_ge(*R.pstep.before(i, 0))
                    R.tensor_logits(pe, bR, fT, wr)

                def step(g, b):
                    scores(g)
                    head_T(g + 1)
                    head_k(g + 1)
                    out_T(g - 1)
                    probs_T(g, 0)
                    if runs(g - 3):
                        R.tensor_rank(pe, g - 3, bR)
                    probs_T(g, 1)
                    mix(g, 0)
                    out_product(g - 1)
                    mix(g, 1)
                    head_q(g + 1)
                    flat_T(g - 2, b)
                    logits(g - 2)
                    head_v(g + 1)
                skewed(pe, step, first=4)

            @block.scalar
            def _(act):
                def head_T(i):
                    if not runs(i):
                        return
                    act.wait_ge(*pe_hT.now(i))
                    act.wait_ge(*pe_v.before(i))
                    act.activation(hT[:, :], bT[:, :], ACT.Copy).then_inc(hT_ready.sem, 1)

                def head_v(i):
                    if not runs(i):
                        return
                    act.wait_ge(*pe_v.now(i))
                    act.wait_ge(*pe_o.before(i))
                    bv = bV[:, :].rearrange("m (f kv d) -> m f kv d", f=FR, kv=KV1)
                    for h2 in range(2):
                        r = slice(64 * h2, 64 * h2 + 64)
                        act.activation(v[r, :, :, h2, 0:D1], bv[r, :, :, :], ACT.Copy).then_inc(v_ready.sem, 1)

                def exp(i, u):
                    if not runs(i):
                        return
                    act.wait_ge(*s_ready.now(i, u))
                    su = s[:, u, :, :, :].rearrange("n p h m -> n (p h m)")
                    act.activation(su, su, ACT.Exp, scale=float(D1) ** -0.5).then_inc(e_ready.sem, 1)

                def probs_T(i, u):
                    if not runs(i):
                        return
                    act.wait_ge(*pe_pt.now(i, u))
                    act.wait_ge(*pe_o.before(i, u))
                    act.activation(pt[:, u, :, :, :].rearrange("m p k n -> m (p k n)"), PT_BANKS[u][:, :], ACT.Copy)\
                       .then_inc(pt_ready.sem, 1)

                def out_T(i):
                    if not runs(i):
                        return
                    act.wait_ge(*pe_yT.now(i))
                    act.wait_ge(*pe_x.before(i))
                    act.activation(yT[:, :], bT[:, :], ACT.Copy).then_inc(yT_ready.sem, 1)

                def head_k(i):
                    if not runs(i):
                        return
                    act.wait_ge(*rope_k.now(i, 2))
                    act.wait_ge(*pe_s.before(i))
                    for h4 in range(H1):
                        rows = slice(D1 * h4, D1 * h4 + D1)
                        act.activation(k[rows, :, h4, :], k2[rows, :, :], ACT.Copy).then_inc(k_ready.sem, 1)

                def head_h(i):
                    if not runs(i):
                        return
                    act.wait_ge(*rh_ready.now(i))
                    act.wait_ge(*vn_ready.now(i, PG - 1))
                    act.wait_ge(*pe_hT.before(i))
                    for p in range(PG):
                        act.activation(h[:, p, :], vt(i, p), ACT.Copy, scale=rr[:, 3, p:p + 1]).then_inc(h_ready.sem, 1)

                def out_squares(i):
                    if not runs(i):
                        return
                    act.wait_ge(*x2_ready.now(i))
                    act.wait_ge(*ms_ready.before(i))
                    act.wait_ge(*sq_ready.before(i))
                    for p in range(PG):
                        act.activation(sq[:, p, :], x2[:, p, :], ACT.Square, accum_out=ms[:, 0, p:p + 1]).then_inc(sq_ready.sem, 1)

                def flat_T(i):
                    if not runs(i):
                        return
                    act.wait_ge(*pe_fT.now(i))
                    act.wait_ge(*R.pe_logits.before(i))
                    act.activation(fT[:, :], bT[:, :], ACT.Copy).then_inc(fT_ready.sem, 1)

                def step(g, b):
                    head_T(g + 1)
                    exp(g, 0)
                    exp(g, 1)
                    out_T(g - 1)
                    probs_T(g, 0)
                    probs_T(g, 1)
                    head_k(g + 1)
                    flat_T(g - 2)
                    head_h(g + 2)
                    out_squares(g - 1)
                    head_v(g + 1)
                skewed(act, step)
                R.scalar_exp(act, True)

            @block.vector
            def _(dve):
                def table(i, rows=slice(0, 128), n=FR):
                    t = rope[rows, i, :]
                    return bass.AP(t.tensor, t.offset, [t.ap[0], [0, n], [1, NODES]])

                def fview(bank):
                    return bank[:, :].rearrange("c (f n) -> c f n", f=FR)

                def head_stats(i):
                    if not runs(i):
                        return
                    norm_stats(dve, lambda p: xt(i, p), st, mv, ve, bn, part, vs, i, EPS_LN, gate,
                               [rs_ready.before(i), rms_in.before(i)])

                def head_vn(i):
                    if not runs(i):
                        return
                    dve.wait_ge(*rs_ready.now(i))

                    def norm_pair(p):
                        dve.tensor_scalar(vt(i, p), xt(i, p), mv[:, p, 0:1], rs[:, p:p + 1],
                                          ALU.subtract, ALU.mult).then_inc(vn_ready.sem, 1)

                    dve.tensor_tensor(rr[:, 0, :], rs[:, :], rs[:, :], ALU.mult).then_inc(rms_in.sem, 1)
                    norm_pair(0)
                    dve.wait_ge(*rms_in.now(i, 0))
                    dve.wait_ge(*vs.now(i))
                    dve.scalar_tensor_tensor(out=rr[:, 1, :], in0=ve[:, :], scalar=-EPS_LN, in1=rr[:, 0, :],
                                             op0=ALU.add, op1=ALU.mult).then_inc(rms_in.sem, 1)
                    norm_pair(1)
                    dve.wait_ge(*rms_in.now(i, 1))
                    dve.wait_ge(*rh_ready.before(i))
                    dve.tensor_scalar(rr[:, 2, :], rr[:, 1, :], EPS_RMS, None, ALU.add).then_inc(rms_in.sem, 1)
                    norm_pair(2)
                    norm_pair(3)

                def rotate_k(i):
                    if not runs(i):
                        return
                    dve.wait_ge(*pe_k.now(i))
                    dve.wait_ge(*k_ready.before(i))
                    dve.tensor_tensor(k1[:, :, :], fview(bK), table(0), ALU.mult).then_inc(rope_k.sem, 1)
                    dve.tensor_tensor(k2[:, :, :], fview(bKr), table(1), ALU.mult).then_inc(rope_k.sem, 1)
                    dve.wait_ge(*rope_k.now(i, 1))
                    dve.tensor_tensor(k2[:, :, :], k1[:, :, :], k2[:, :, :], ALU.add).then_inc(rope_k.sem, 1)

                def rotate_q(i):
                    if not runs(i):
                        return
                    dve.wait_ge(*pe_q.now(i))
                    dve.wait_ge(*q_ready.before(i))
                    dve.tensor_tensor(q1[:, :, :], fview(bQ), table(0), ALU.mult).then_inc(rope_q.sem, 1)
                    dve.tensor_tensor(q2[:, :, :], fview(bQr), table(1), ALU.mult).then_inc(rope_q.sem, 1)
                    dve.wait_ge(*rope_q.now(i, 1))
                    dve.wait_ge(*pe_s.before(i))
                    dve.tensor_tensor(q[:, :, :], q1[:, :, :], q2[:, :, :], ALU.add).then_inc(q_ready.sem, 1)

                def soft(i, u):
                    if not runs(i):
                        return
                    sv = S_BANKS[u][:, :].rearrange("n (h m) -> n h m", m=NODES)
                    m = mx[:, u, :, :].rearrange("n p h -> n (p h)")
                    dve.wait_ge(*pe_s.now(i, u))
                    dve.wait_ge(*s_ready.before(i, u))
                    dve.tensor_reduce(m, sv, AX.X, ALU.max).then_inc(mx_ready.sem, 1)
                    dve.wait_ge(*mx_ready.now(i, u))
                    dve.wait_ge(*pe_pt.before(i, u))
                    dve.tensor_tensor(s[:, u, :, :, :].rearrange("n p h m -> n (p h) m"), sv,
                                      bass.AP(m.tensor, m.offset, [m.ap[0], [1, 2 * H1], [0, NODES]]), ALU.subtract)\
                       .then_inc(s_ready.sem, 1)

                def norm(i, u):
                    if not runs(i):
                        return
                    ov = bO[:, 0:2 * H1 * (D1 + 1)].rearrange("n (h d) -> n h d", d=D1 + 1)
                    m = rc[:, u, :, :].rearrange("n p h -> n (p h)")
                    dve.wait_ge(*pe_o.now(i, u))
                    dve.wait_ge(*y_ready.before(i, u))
                    dve.reciprocal(m, ov[:, :, D1]).then_inc(rc_ready.sem, 1)
                    dve.wait_ge(*rc_ready.now(i, u))
                    dve.wait_ge(*pe_yT.before(i))
                    dve.tensor_tensor(y[:, 2 * u:2 * u + 2, :].rearrange("n p (h d) -> n (p h) d", h=H1), ov[:, :, 0:D1],
                                      bass.AP(m.tensor, m.offset, [m.ap[0], [1, 2 * H1], [0, D1]]), ALU.mult)\
                       .then_inc(y_ready.sem, 1)

                def out_x2(i):
                    if not runs(i):
                        return
                    dve.wait_ge(*pe_x.now(i))
                    dve.wait_ge(*fin.before(i))
                    dve.wait_ge(*flat_ready.before(i))
                    dve.wait_ge(*sq_ready.before(i))
                    dve.tensor_tensor(x2[:, :, :], bV[:, :].rearrange("n (p c) -> n p c", p=PG), vn[:, bass.ds(i * PG, PG), :], ALU.add)\
                       .then_inc(x2_ready.sem, 1)

                def out_ms(i):
                    if not runs(i):
                        return
                    dve.wait_ge(*sq_ready.now(i, PG - 1))
                    dve.wait_ge(*rms2_ready.before(i))
                    dve.tensor_scalar(ms[:, 1, :], ms[:, 0, :], 1.0 / C, EPS_RMS, ALU.mult, ALU.add).then_inc(ms_ready.sem, 1)

                def out_flat(i, b):
                    if not runs(i):
                        return
                    dve.wait_ge(*rms2_ready.now(i))
                    dve.wait_ge(*pe_fT.before(i))
                    R.wait_landed(dve, i - 2)
                    w = ln2w[:, :]
                    for p in range(PG):
                        dve.scalar_tensor_tensor(out=flat[b][:, p, 0:C], in0=x2[:, p, :], scalar=ms[:, 2, p:p + 1], in1=w,
                                                 op0=ALU.mult, op1=ALU.mult).then_inc(flat_ready.sem, 1)

                def step(g, b):
                    soft(g, 0)
                    soft(g, 1)
                    head_vn(g + 2)
                    rotate_k(g + 1)
                    norm(g, 0)
                    if runs(g - 3):
                        R.vector_rows(dve, g - 3, bR)
                    norm(g, 1)
                    out_flat(g - 2, b)
                    out_x2(g - 1)
                    head_stats(g + 3)
                    rotate_q(g + 1)
                    out_ms(g - 1)
                    if runs(g - 2):
                        R.vector_choose(dve, g - 2, bR, True)
                skewed(dve, step, first=4, ahead=3)
                R.vector_weights(dve, True)

            @block.gpsimd
            def _(pool):
                def head_rs(i):
                    if not runs(i):
                        return
                    pool.wait_ge(*vs.now(i))
                    pool.wait_ge(*vn_ready.before(i))
                    pool.wait_ge(*rms_in.before(i, 0))
                    pool.tensor_tensor(rs[:, :], ve[:, :], half[:, 0:PG], ALU.pow).then_inc(rs_ready.sem, 1)

                def head_rh(i):
                    if not runs(i):
                        return
                    pool.wait_ge(*rms_in.now(i, 2))
                    pool.wait_ge(*h_ready.before(i))
                    pool.tensor_tensor(rr[:, 3, :], rr[:, 2, :], half[:, 0:PG], ALU.pow).then_inc(rh_ready.sem, 1)

                def out_rms(i):
                    if not runs(i):
                        return
                    pool.wait_ge(*ms_ready.now(i))
                    pool.wait_ge(*flat_ready.before(i))
                    pool.tensor_tensor(ms[:, 2, :], ms[:, 1, :], half[:, 0:PG], ALU.pow).then_inc(rms2_ready.sem, 1)

                def out_x(i):
                    if not runs(i):
                        return
                    xg = x[:, bass.ds(i * PG, PG), :]
                    pool.wait_ge(*x2_ready.now(i))
                    pool.tensor_tensor(xg, xg, x2[:, :, :], ALU.add).then_inc(fin.sem, 1)

                def step(g, b):
                    out_rms(g - 2)
                    head_rh(g + 2)
                    if runs(g - 3):
                        R.pool_scatter(pool, g - 3, flat[1 - b], dest)
                    head_rs(g + 3)
                    out_x(g - 1)
                skewed(pool, step, first=4, ahead=3)
                R.wait_landed(pool, GROUPS - 1)
        clear_taken(nc)


def phase_experts(nc, banks, c, state, rows_in, rows_out, wall, swiglu, name):
    chunks = CH1 if swiglu else CH2
    HID = HID1 if swiglu else HID2
    NK = len(chunks)
    NW = wall.shape[-1]
    W2 = 2 * HID if swiglu else HID
    ident = c["ident"]
    with ExitStack() as ctx:
        def sb(n, shape, dt=F32):
            return ctx.enter_context(nc.sbuf_tensor(f"{name}_{n}", shape, dt))

        def sig(n, per=UN):
            return Signal(take_semaphore(ctx, nc, f"{name}_{n}"), per)

        def raw(n):
            return take_semaphore(ctx, nc, f"{name}_{n}")

        w = [sb(f"w{i}", [128, NW]) for i in range(UN)]
        xg = [sb(f"xg{i}", [128, 2, ROW]) for i in range(UN)]
        yb = [sb(f"yb{i}", [128, 2, C]) for i in range(UN)]
        xT = [sb(f"xT{i}", [128, TILE]) for i in range(2)]
        sg = [sb(f"sg{i}", [128, NK, TILE]) for i in range(2)]
        hT = [sb(f"hT{i}", [128, NK, TILE]) for i in range(2)] if swiglu else sg
        dst = [sb(f"dst{i}", [128, 2]) for i in range(UN)]
        dsti = [sb(f"dsti{i}", [128, 2], I32) for i in range(UN)]
        nobody = c["nobody"]
        tail = sb("tail", [128, NE], I32)
        le, iota = c["le"], c["iota"]
        cneg = sb("cneg", [128, NE])
        ti, tj = sb("ti", [128, NE], I32), sb("tj", [128, NE], I32)
        tf = sb("tf", [128, NE])
        cm, cum = sb("cm", [128, NE, NE]), sb("cum", [128, NE])
        ge, go = sb("ge", [128, TILES, NE]), sb("go", [128, TILES, NE])
        ei, off = sb("ei", [128, TILES]), sb("off", [128, TILES])
        rv = sb("rv", [128, TILES])
        table = sb("table", [128, 2, TILES], I32)
        chain, filled = raw("chain"), raw("filled")
        loaded = [raw(f"loaded{i}") for i in range(UN)]
        stored = [raw(f"stored{i}") for i in range(UN)]
        pe_x, pe_up, pe_down = sig("pe_x"), sig("pe_up", UN * NK), sig("pe_down")
        xT_ready, act_done = sig("xT_ready"), sig("act_done", UN * NK)
        h_ready = sig("h_ready", UN * NK) if swiglu else act_done
        y_ready = sig("y_ready")
        dst_ready = sig("dst_ready", 3 * UN)
        gate, read_gate = raw("gate"), raw("read_gate")
        list_tiles = rows_in.rearrange("(a t p) c -> a p t c", t=2, p=128)
        TPE = CAP // TILE

        def fill(eng, experts):
            eng.wait_ge(chain, 1)
            for e in experts:
                row = eng.value_load(tail[0:1, e:e + 1], min_val=0, max_val=NE * CAP)
                eng.dma_start(rows_in[bass.ds(row, TILE), :].rearrange("(t p) c -> p t c", t=2), nobody[:, 2 * e:2 * e + 2, :])\
                   .then_inc(filled, 16)

        with nc.Block() as block:
            @block.sync
            def _(sp):
                fill(sp, range(0, NE // 2))
                sp.wait_ge(filled, 16 * NE)

            @block.scalar
            def _(act):
                open_signals(act, [xT_ready, act_done])
                fill(act, range(NE // 2, NE))

            @block.vector
            def _(dve):
                base = state["base"]
                n = [0]

                def then(ins):
                    n[0] += 1
                    ins.then_inc(chain, 1)
                    dve.wait_ge(chain, n[0])

                then(dve.tensor_copy(tail[:, :], base[:, :]))
                then(dve.tensor_scalar(cneg[:, :], c["rev"][:, :], float(CAP), float(TILE - 1 - NE * CAP), ALU.mult, ALU.add))
                then(dve.tensor_tensor(ti[:, :], base[:, :], cneg[:, :], ALU.add))
                then(dve.tensor_scalar(tj[:, :], ti[:, :], TILE.bit_length() - 1, None, ALU.logical_shift_right))
                then(dve.tensor_copy(tf[:, :], tj[:, :]))
                t = tf[:, :]
                then(dve.tensor_tensor(cm[:, :, :], le[:, :, :], bass.AP(t.tensor, t.offset, [t.ap[0], [0, NE], [1, NE]]), ALU.mult))
                then(dve.tensor_reduce(cum[:, :], cm[:, :, :], AX.X, ALU.add))
                u, v = iota[:, :], cum[:, :]
                then(dve.tensor_tensor(ge[:, :, :], bass.AP(u.tensor, u.offset, [u.ap[0], [1, TILES], [0, NE]]),
                                       bass.AP(v.tensor, v.offset, [v.ap[0], [0, TILES], [1, NE]]), ALU.is_ge))
                then(dve.tensor_reduce(ei[:, :], ge[:, :, :], AX.X, ALU.add))
                then(dve.tensor_tensor(go[:, :, :], ge[:, :, :], bass.AP(t.tensor, t.offset, [t.ap[0], [0, TILES], [1, NE]]), ALU.mult))
                then(dve.tensor_reduce(off[:, :], go[:, :, :], AX.X, ALU.add))
                then(dve.tensor_tensor(off[:, :], iota[:, :], off[:, :], ALU.subtract))
                then(dve.scalar_tensor_tensor(out=table[:, 0, :], in0=ei[:, :], scalar=float(TPE), in1=off[:, :],
                                              op0=ALU.mult, op1=ALU.add))
                then(dve.tensor_scalar(off[:, :], ei[:, :], float(NE - 1), None, ALU.min))
                then(dve.tensor_copy(table[:, 1, :], off[:, :]))
                then(dve.tensor_scalar(rv[:, :], off[:, :], -1.0, float(NE), ALU.mult, ALU.add))
                open_signals(dve, [y_ready, dst_ready])
                if swiglu:
                    open_signals(dve, [h_ready])

            @block.tensor
            def _(pe):
                open_signals(pe, [pe_x, pe_up, pe_down])

        bT, bY = banks[0], banks[7]
        NB = 3 if swiglu else 2
        up_banks = [banks[1:1 + NB], banks[4:4 + NB]]
        TURNS = TILES // UN

        with nc.Block() as block:
            @block.sync
            def _(sp):
                def read(g, j):
                    at = sp.value_load(table[0:1, 0, bass.ds(g * UN + j, 1)], min_val=0, max_val=(NE + 1) * TPE - 1)
                    ex = sp.value_load(table[0:1, 1, bass.ds(g * UN + j, 1)], min_val=0, max_val=NE - 1)
                    sp.wait_ge(*y_ready.now(g, j - UN))
                    sp.sem_inc(read_gate, 1)
                    sp.dma_start(w[j][:, :], wall[bass.ds(ex, 1), :, :].rearrange("a p n -> p (a n)")).then_inc(loaded[j], 16)
                    sp.dma_start(xg[j][:, :, :], list_tiles[bass.ds(at, 1), :, :, :].rearrange("a p t c -> p (a t) c")).then_inc(loaded[j], 16)

                turns(sp, 0, TURNS, lambda g: [read(g, j) for j in range(UN)])

            @block.gpsimd
            def _(pool):
                def body(g):
                    for j in range(UN):
                        pool.wait_ge(*y_ready.now(g, j))
                        pool.wait_ge(*dst_ready.now(g, 3 * j + 2))
                        pool.sem_inc(gate, 1)
                        for t in range(2):
                            pool.indirect_dma_start(
                                out=rows_out, out_offset=bass.IndirectOffsetOnAxis(ap=dsti[j][:, t:t + 1], axis=0),
                                in_=yb[j][:, t, :], in_offset=None).then_inc(stored[j], 16)
                turns(pool, 0, TURNS, body)
                for j in range(UN):
                    pool.wait_ge(stored[j], 32 * TURNS)

            @block.tensor
            def _(pe):
                def x_T(g, j):
                    jj = j % UN
                    gg = g + 1 if j == UN else g
                    pe.wait_ge(loaded[jj], (gg + 1) * 32)
                    pe.wait_ge(*xT_ready.now(g, j - 1))
                    for t in range(2):
                        i = pe.transpose(bT[:, 128 * t:128 * t + 128], xg[jj][:, t, 0:C], ident[:, :])
                    i.then_inc(pe_x.sem, 1)

                def up(g, j):
                    pe.wait_ge(*xT_ready.now(g, j))
                    pe.wait_ge(*h_ready.now(g, NK * (j - 2) + NK - 1))
                    for k, (c0, cn) in enumerate(chunks):
                        if swiglu:
                            bank = up_banks[j % 2][k]
                            for m in range(2):
                                i = pe.matmul(bank[0:cn, TILE * m:TILE * m + TILE], w[j][:, HID * m + c0:HID * m + c0 + cn],
                                              xT[j % 2][:, :], start=(m == 0), stop=True, skip_group_check=True)
                            i.then_inc(pe_up.sem, 1)
                        else:
                            bank = up_banks[j % 2][k // 2]
                            i = pe.matmul(bank[0:cn, TILE * (k % 2):TILE * (k % 2) + TILE], w[j][:, c0:c0 + cn],
                                          xT[j % 2][:, :], start=(k % 2 == 0), stop=True, skip_group_check=True)
                            i.then_inc(pe_up.sem, 1)

                def down(g, j):
                    jj = j % UN
                    pe.wait_ge(*h_ready.now(g, NK * j + NK - 1))
                    pe.wait_ge(*y_ready.now(g, j - 1))
                    for t in range(2):
                        for k, (c0, cn) in enumerate(chunks):
                            i = pe.matmul(bY[:, 128 * t:128 * t + 128], hT[jj % 2][0:cn, k, 128 * t:128 * t + 128],
                                          w[jj][0:cn, W2 + 128 * k:W2 + 128 * k + 128], start=(k == 0), stop=(k == NK - 1),
                                          skip_group_check=True)
                    i.then_inc(pe_down.sem, 1)

                def body(g, first=False, last=False):
                    for j in range(UN):
                        up(g, j)
                        if not (last and j == UN - 1):
                            x_T(g, j + 1)
                        if not (first and j == 0):
                            down(g, j - 1)
                x_T(0, 0)
                body(0, first=True)
                turns(pe, 1, TURNS - 1, body)
                body(TURNS - 1, last=True)
                down(TURNS - 1, UN - 1)

            @block.scalar
            def _(act):
                def x_T(g, j):
                    act.wait_ge(*pe_x.now(g, j))
                    act.wait_ge(*pe_up.now(g, NK * (j - 2) + NK - 1))
                    act.activation(xT[j % 2][:, :], bT[:, 0:TILE], ACT.Copy).then_inc(xT_ready.sem, 1)

                def body(g, last=False):
                    for j in range(UN):
                        for k, (c0, cn) in enumerate(chunks):
                            if swiglu:
                                act.wait_ge(*pe_up.now(g, NK * j + k))
                                act.wait_ge(*h_ready.now(g, NK * (j - 2) + k))
                                act.activation(sg[j % 2][0:cn, k, :], up_banks[j % 2][k][0:cn, 0:TILE], ACT.Silu)\
                                   .then_inc(act_done.sem, 1)
                            else:
                                act.wait_ge(*pe_up.now(g, NK * j + k // 2 * 2 + 1))
                                act.wait_ge(*pe_down.now(g, j - 2))
                                bank = up_banks[j % 2][k // 2]
                                b1 = W2 + NK * C + k
                                act.activation(sg[j % 2][0:cn, k, :], bank[0:cn, TILE * (k % 2):TILE * (k % 2) + TILE], ACT.Gelu,
                                               bias=w[j][:, b1:b1 + 1]).then_inc(act_done.sem, 1)
                        if not (last and j == UN - 1):
                            x_T(g, j + 1)
                x_T(0, 0)
                turns(act, 0, TURNS - 1, body)
                body(TURNS - 1, last=True)

            @block.vector
            def _(dve):
                def out(g, j):
                    jj = j % UN
                    dve.wait_ge(*pe_down.now(g, j))
                    src = bY[:, 0:2 * C].rearrange("r (t c) -> r t c", t=2)
                    if swiglu:
                        dve.tensor_copy(yb[jj][:, :, :], src).then_inc(y_ready.sem, 1)
                    else:
                        b = w[jj][:, W2 + NK * C + NK:W2 + NK * C + NK + C]
                        dve.tensor_tensor(yb[jj][:, :, :], src, bass.AP(b.tensor, b.offset, [b.ap[0], [0, 2], [1, C]]), ALU.add)\
                           .then_inc(y_ready.sem, 1)

                def body(g, first=False):
                    for j in range(UN):
                        if swiglu:
                            for k, (c0, cn) in enumerate(chunks):
                                dve.wait_ge(*act_done.now(g, NK * j + k))
                                dve.wait_ge(*pe_down.now(g, j - 2))
                                dve.tensor_tensor(hT[j % 2][0:cn, k, :], up_banks[j % 2][k][0:cn, TILE:2 * TILE],
                                                  sg[j % 2][0:cn, k, :], ALU.mult).then_inc(h_ready.sem, 1)
                        if not (first and j == 0):
                            stored_before(g, j - 1)
                            out(g, j - 1)
                        where(g, j)

                def where(g, j):
                    dve.wait_ge(loaded[j], (g + 1) * 32)
                    if not isinstance(g, int) or g > 0:
                        dve.wait_ge(stored[j], g * 32)
                    dve.tensor_scalar(dst[j][:, :], xg[j][:, :, C + 1], rv[:, bass.ds(g * UN + j, 1)], float(TOKENS),
                                      ALU.not_equal, ALU.mult).then_inc(dst_ready.sem, 1)
                    dve.wait_ge(*dst_ready.now(g, 3 * j))
                    dve.tensor_tensor(dst[j][:, :], dst[j][:, :], xg[j][:, :, C], ALU.add).then_inc(dst_ready.sem, 1)
                    dve.wait_ge(*dst_ready.now(g, 3 * j + 1))
                    dve.tensor_copy(dsti[j][:, :], dst[j][:, :]).then_inc(dst_ready.sem, 1)

                def stored_before(g, j):
                    gg = g - 1 if j < 0 else g
                    if isinstance(gg, int):
                        if gg > 0:
                            dve.wait_ge(stored[j % UN], 32 * gg)
                    else:
                        dve.wait_ge(stored[j % UN], gg * 32)
                body(0, first=True)
                body(1)
                turns(dve, 2, TURNS, body)
                stored_before(TURNS - 1, UN - 1)
                out(TURNS - 1, UN - 1)
        clear_taken(nc)


class Combine:

    def __init__(self, ctx, nc, name, state, rows):
        self.state = state
        self.rows = rows[0:2 * TOKENS, :].rearrange("(k t p) c -> p k t c", k=2, p=128)
        self.ys = [ctx.enter_context(nc.sbuf_tensor(f"{name}_y{i}", [128, 2, PG, C], F32)) for i in range(2)]
        self.landed = [take_semaphore(ctx, nc, f"{name}_landed{i}") for i in range(2)]
        self.mixed = Signal(take_semaphore(ctx, nc, f"{name}_mixed"), 2 * PG)
        self.gate = take_semaphore(ctx, nc, f"{name}_gate")
        self.dve_signals = [self.mixed]

    def fetch(self, eng, turn):
        for b in range(2):
            g = turn * 2 + b
            eng.wait_ge(*self.mixed.before(g, turns=2))
            eng.sem_inc(self.gate, 1)
            for k in range(2):
                eng.dma_start(self.ys[b][:, k, :, :], self.rows[:, k, bass.ds(g * PG, PG), :]).then_inc(self.landed[b], 16)

    def vector_mix(self, dve, g, b, x):
        w = self.state["w"]
        dve.wait_ge(self.landed[b], (g - b) * 16 + 32)
        for k in range(2):
            if k:
                dve.wait_ge(*self.mixed.now(g, PG - 1))
            for p in range(PG):
                xt = x[:, bass.ds(g * PG + p, 1), :].rearrange("p a c -> p (a c)")
                dve.scalar_tensor_tensor(out=xt, in0=self.ys[b][:, k, p, :], scalar=w[:, k, bass.ds(g * PG + p, 1)], in1=xt,
                                         op0=ALU.mult, op1=ALU.add).then_inc(self.mixed.sem, 1)


def phase_gnn1(nc, W, x, banks, c, state1, rows1, state2, dest):
    ident, half, adj = c["ident"], c["half"], c["adj"]
    with ExitStack() as ctx:
        def sb(name, shape, dt=F32):
            return ctx.enter_context(nc.sbuf_tensor("g1_" + name, shape, dt))

        def sig(name, per=1):
            return Signal(take_semaphore(ctx, nc, "g1_" + name), per)

        w1, w2, w3, wg, bg = (W[n] for n in "w1 w2 w3 wg bg".split())
        mask = sb("mask", [128, NODES])
        st, mv = sb("st", [128, 2, PG, 6]), sb("mv", [128, 2, PG, 2])
        ve, rs = sb("ve", [128, 2, PG]), sb("rs", [128, 2, PG])
        xn = sb("xn", [128, PG, C])
        xT = sb("xT", [128, GT])
        h1, h2 = sb("h1", [128, GT]), sb("h2", [128, GT])
        h3 = sb("h3", [128, PG, C + 1])
        e0 = sb("e0", [128, PG, NODES])
        e1 = sb("e1", [128, PG, NODES])
        e2 = sb("e2", [128, PG, NODES])
        mx = sb("mx", [128, PG])
        s = sb("s", [128, PG, NODES])
        pr = sb("pr", [128, PG, 2, NODES])
        pt = sb("pt", [128, PG, 128])
        rc = sb("rc", [128, PG])
        o = sb("o", [128, PG, C])
        flat = [sb(f"flat{i}", [128, PG, ROW]) for i in range(2)]
        fT = sb("fT", [128, GT])
        setup = take_semaphore(ctx, nc, "g1_setup")
        R = Routing(ctx, nc, "g1r", c, dict(state2, bias=bg))
        M = Combine(ctx, nc, "g1c", state1, rows1)

        bn, part, vs = [sig("bn0", PG), sig("bn1", PG)], [sig("part0", PG), sig("part1", PG)], [sig("vs0"), sig("vs1")]
        xn_ready, h3_ready = sig("xn_ready", PG), sig("h3_ready")
        e_steps = sig("e_steps", 4)
        rc_ready, o_ready, x3_ready = sig("rc_ready", 2), sig("o_ready", PG), sig("x3_ready")
        flat_ready = sig("flat_ready", PG)
        gate = sig("gate")
        dve_signals = bn + part + vs + [xn_ready, e_steps, rc_ready, x3_ready, flat_ready]\
            + R.dve_signals + M.dve_signals
        xT_ready, h12_ready, p_ready, pt_ready, fT_ready = sig("xT_ready"), sig("h12_ready", 2), sig("p_ready", 2), sig("pt_ready"), sig("fT_ready")
        low_ready = sig("low_ready")
        act_signals = [xT_ready, h12_ready, h3_ready, low_ready, p_ready, pt_ready, o_ready, fT_ready] + R.act_signals
        rs_ready = [sig("rs0_ready"), sig("rs1_ready")]
        pool_signals = rs_ready + R.pool_signals
        pe_xT, pe_h, pe_e, pe_pt, pe_o, pe_fT = sig("pe_xT"), sig("pe_h", 3), sig("pe_e"), sig("pe_pt"), sig("pe_o", 2), sig("pe_fT")
        pe_signals = [pe_xT, pe_h, pe_e, pe_pt, pe_o, pe_fT] + R.pe_signals
        bT, bH1, bH2, bH3, bE, bO0, bO1, bR = banks

        with nc.Block() as block:
            @block.gpsimd
            def _(pool):
                pool.memset(pr[:, :, :, :], 0.0).then_inc(setup, 1)
                pool.memset(h3[:, :, C:C + 1], 1.0).then_inc(setup, 1)
                open_signals(pool, pool_signals)

            @block.vector
            def _(dve):
                dve.tensor_scalar(mask[:, :], adj[:, :], 0.0, -1e12, ALU.is_le, ALU.mult)
                b = state2["base"]
                dve.tensor_scalar(b[:, :], c["rev"][:, :], -float(CAP), float(NE * CAP), ALU.mult, ALU.add)
                open_signals(dve, dve_signals)

            @block.scalar
            def _(act):
                open_signals(act, act_signals)

            @block.tensor
            def _(pe):
                open_signals(pe, pe_signals)

        def xt(i, p):
            return x[:, bass.ds(i * PG + p, 1), :].rearrange("p a c -> p (a c)")

        with nc.Block() as block:
            @block.tensor
            def _(pe):
                def head_T(i):
                    if not runs(i):
                        return
                    pe.wait_ge(*xn_ready.now(i, PG - 1))
                    pe.wait_ge(*fT_ready.before(i, turns=3))
                    for p in range(PG):
                        ins = pe.transpose(bT[:, 128 * p:128 * p + 128], xn[:, p, :], ident[:, :])
                    ins.then_inc(pe_xT.sem, 1)

                def head_h(i):
                    if not runs(i):
                        return
                    pe.wait_ge(*xT_ready.now(i))
                    pe.wait_ge(*h12_ready.before(i))
                    pe.matmul(bH1[:, :], w1[:, :], xT[:, :], start=True, stop=True).then_inc(pe_h.sem, 1)
                    pe.matmul(bH2[:, :], w2[:, :], xT[:, :], start=True, stop=True).then_inc(pe_h.sem, 1)
                    pe.wait_ge(*h3_ready.before(i))
                    for p in range(PG):
                        ins = pe.matmul(bH3[:, 128 * p:128 * p + 128], xT[:, 128 * p:128 * p + 128], w3[:, :],
                                        start=(p == 0), stop=True, skip_group_check=True)
                    ins.then_inc(pe_h.sem, 1)

                def scores(i):
                    if not runs(i):
                        return
                    pe.wait_ge(*h12_ready.now(i, 1))
                    pe.wait_ge(*pt_ready.before(i))
                    for fr in range(2 * PG):
                        f, p = fr % 2, fr // 2
                        t = slice(64 * fr, 64 * fr + 64)
                        ins = pe.matmul(bE[64 * f:64 * f + 64, 64 * p:64 * p + 64], h1[:, t], h2[:, t],
                                        start=(p == 0), stop=True, skip_group_check=True)
                    ins.then_inc(pe_e.sem, 1)

                def probs_T(i):
                    if not runs(i):
                        return
                    pe.wait_ge(*p_ready.now(i, 1))
                    for p in range(PG):
                        ins = pe.transpose(bE[:, 128 * p:128 * p + 128], pr[:, p, :, :].rearrange("n f m -> n (f m)"), ident[:, :])
                    ins.then_inc(pe_pt.sem, 1)

                def mix(i):
                    if not runs(i):
                        return
                    pe.wait_ge(*pt_ready.now(i))
                    pe.wait_ge(*h3_ready.now(i))
                    pe.wait_ge(*o_ready.before(i))
                    for u, bank in enumerate([bO0, bO1]):
                        for n in range(2):
                            p = 2 * u + n
                            ins = pe.matmul(bank[:, (C + 1) * n:(C + 1) * n + C + 1], pt[:, p, :], h3[:, p, :],
                                            start=(n == 0), stop=True, skip_group_check=True)
                        ins.then_inc(pe_o.sem, 1)

                def flat_T(i, b):
                    if not runs(i):
                        return
                    pe.wait_ge(*flat_ready.now(i, PG - 1))
                    if runs(i + 2):
                        pe.wait_ge(*xT_ready.now(i + 2))
                    for p in range(PG):
                        ins = pe.transpose(bT[:, 128 * p:128 * p + 128], flat[b][:, p, 0:C], ident[:, :])
                    ins.then_inc(pe_fT.sem, 1)

                def logits(i):
                    if not runs(i):
                        return
                    pe.wait_ge(*fT_ready.now(i))
                    pe.wait_ge(*R.pstep.before(i, 0))
                    R.tensor_logits(pe, bR, fT, wg)

                def step(g, b):
                    scores(g)
                    head_T(g + 1)
                    head_h(g + 1)
                    if runs(g - 2):
                        R.tensor_rank(pe, g - 2, bR)
                    probs_T(g)
                    flat_T(g - 1, 1 - b)
                    mix(g)
                    logits(g - 1)
                skewed(pe, step)

            @block.scalar
            def _(act):
                def head(i):
                    if not runs(i):
                        return
                    act.wait_ge(*pe_xT.now(i))
                    act.wait_ge(*pe_h.before(i))
                    act.activation(xT[:, :], bT[:, :], ACT.Copy).then_inc(xT_ready.sem, 1)
                    for n, (bank, h) in enumerate([(bH1, h1), (bH2, h2)]):
                        act.wait_ge(*pe_h.now(i, n))
                        act.wait_ge(*pe_e.before(i))
                        act.activation(h[:, :], bank[:, :], ACT.Copy).then_inc(h12_ready.sem, 1)

                def head_h3(i):
                    if not runs(i):
                        return
                    act.wait_ge(*pe_h.now(i, 2))
                    act.wait_ge(*pe_o.before(i))
                    act.activation(h3[:, :, 0:C], bH3[:, :].rearrange("m (p c) -> m p c", p=PG), ACT.Copy).then_inc(h3_ready.sem, 1)

                def mixed_out(i):
                    if not runs(i):
                        return
                    for u, bank in enumerate([bO0, bO1]):
                        act.wait_ge(*rc_ready.now(i, u))
                        act.wait_ge(*x3_ready.before(i))
                        ov = bank[:, 0:2 * (C + 1)].rearrange("n (p c) -> n p c", p=2)
                        for n in range(2):
                            p = 2 * u + n
                            act.activation(o[:, p, :], ov[:, n, 0:C], ACT.Relu, scale=rc[:, p:p + 1]).then_inc(o_ready.sem, 1)

                def low(i):
                    if not runs(i):
                        return
                    act.wait_ge(*pe_e.now(i))
                    act.wait_ge(*e_steps.before(i, 0))
                    act.activation(e0[:, :, :].rearrange("n p m -> n (p m)"), bE[:, 0:PG * NODES], ACT.Copy, scale=0.2)\
                       .then_inc(low_ready.sem, 1)

                def exp(i):
                    if not runs(i):
                        return
                    act.wait_ge(*e_steps.now(i, 3))
                    act.wait_ge(*pe_pt.before(i))
                    for f in range(2):
                        r = slice(64 * f, 64 * f + 64)
                        act.activation(pr[r, :, f, :], s[r, :, :], ACT.Exp).then_inc(p_ready.sem, 1)

                def probs_T(i):
                    if not runs(i):
                        return
                    act.wait_ge(*pe_pt.now(i))
                    act.wait_ge(*pe_o.before(i))
                    act.activation(pt[:, :, :].rearrange("m p n -> m (p n)"), bE[:, :], ACT.Copy).then_inc(pt_ready.sem, 1)

                def flat_T(i):
                    if not runs(i):
                        return
                    act.wait_ge(*pe_fT.now(i))
                    act.wait_ge(*R.pe_logits.before(i))
                    act.activation(fT[:, :], bT[:, :], ACT.Copy).then_inc(fT_ready.sem, 1)

                def step(g, b):
                    low(g)
                    head(g + 1)
                    exp(g)
                    probs_T(g)
                    flat_T(g - 1)
                    mixed_out(g)
                    head_h3(g + 1)
                skewed(act, step)
                R.scalar_exp(act, False)

            @block.vector
            def _(dve):
                def head_x(i, b):
                    if runs(i):
                        M.vector_mix(dve, i, b, x)

                def head_stats(i):
                    if not runs(i):
                        return
                    norm_stats(dve, lambda p: xt(i, p), st[:, 0, :, :], mv[:, 0, :, :], ve[:, 0, :], bn[0], part[0],
                               vs[0], i, EPS_LN, gate, [M.mixed.now(i, 2 * PG - 1), rs_ready[0].before(i)])

                def head_xn(i):
                    if not runs(i):
                        return
                    dve.wait_ge(*rs_ready[0].now(i))
                    dve.wait_ge(*pe_xT.before(i))
                    for p in range(PG):
                        dve.tensor_scalar(xn[:, p, :], xt(i, p), mv[:, 0, p, 0:1], rs[:, 0, p:p + 1],
                                          ALU.subtract, ALU.mult).then_inc(xn_ready.sem, 1)

                def soft(i):
                    if not runs(i):
                        return
                    ev = bE[:, 0:PG * NODES].rearrange("n (p m) -> n p m", p=PG)
                    dve.wait_ge(*low_ready.now(i))
                    dve.wait_ge(*e_steps.before(i))
                    dve.tensor_tensor(e1[:, :, :], ev, e0[:, :, :], ALU.max).then_inc(e_steps.sem, 1)
                    dve.wait_ge(*e_steps.now(i, 0))
                    mk = mask[:, :]
                    dve.tensor_tensor(e2[:, :, :], e1[:, :, :], bass.AP(mk.tensor, mk.offset, [mk.ap[0], [0, PG], [1, NODES]]), ALU.add)\
                       .then_inc(e_steps.sem, 1)
                    dve.wait_ge(*e_steps.now(i, 1))
                    dve.tensor_reduce(mx[:, :], e2[:, :, :], AX.X, ALU.max).then_inc(e_steps.sem, 1)
                    dve.wait_ge(*e_steps.now(i, 2))
                    dve.wait_ge(*p_ready.before(i))
                    m = mx[:, :]
                    dve.tensor_tensor(s[:, :, :], e2[:, :, :], bass.AP(m.tensor, m.offset, [m.ap[0], [1, PG], [0, NODES]]), ALU.subtract)\
                       .then_inc(e_steps.sem, 1)

                def norm(i):
                    if not runs(i):
                        return
                    for u, bank in enumerate([bO0, bO1]):
                        dve.wait_ge(*pe_o.now(i, u))
                        ov = bank[:, 0:2 * (C + 1)].rearrange("n (p c) -> n p c", p=2)
                        dve.wait_ge(*o_ready.before(i))
                        dve.reciprocal(rc[:, 2 * u:2 * u + 2], ov[:, :, C]).then_inc(rc_ready.sem, 1)

                def residual(i):
                    if not runs(i):
                        return
                    dve.wait_ge(*o_ready.now(i, PG - 1))
                    xg = x[:, bass.ds(i * PG, PG), :]
                    dve.tensor_tensor(xg, xg, o[:, :, :], ALU.add).then_inc(x3_ready.sem, 1)

                def flat_stats(i):
                    if not runs(i):
                        return
                    norm_stats(dve, lambda p: xt(i, p), st[:, 1, :, :], mv[:, 1, :, :], ve[:, 1, :], bn[1], part[1],
                               vs[1], i, EPS_LN, gate, [x3_ready.now(i), rs_ready[1].before(i)])

                def flat_norm(i, b):
                    if not runs(i):
                        return
                    dve.wait_ge(*rs_ready[1].now(i))
                    dve.wait_ge(*pe_fT.before(i))
                    R.wait_landed(dve, i - 2)
                    for p in range(PG):
                        dve.tensor_scalar(flat[b][:, p, 0:C], xt(i, p), mv[:, 1, p, 0:1], rs[:, 1, p:p + 1],
                                          ALU.subtract, ALU.mult).then_inc(flat_ready.sem, 1)

                def step(g, b):
                    flat_stats(g - 1)
                    if runs(g - 2):
                        R.vector_choose(dve, g - 2, bR, False)
                    soft(g)
                    if runs(g - 2):
                        R.vector_rows(dve, g - 2, bR)
                    flat_norm(g - 1, 1 - b)
                    head_xn(g + 2)
                    head_x(g + 3, 1 - b)
                    norm(g)
                    head_stats(g + 3)
                    residual(g)
                skewed(dve, step, first=4, ahead=3)
                R.vector_weights(dve, False)

            @block.gpsimd
            def _(pool):
                def head_rs(i):
                    if not runs(i):
                        return
                    pool.wait_ge(*vs[0].now(i))
                    pool.wait_ge(*xn_ready.before(i))
                    pool.tensor_tensor(rs[:, 0, :], ve[:, 0, :], half[:, 0:PG], ALU.pow).then_inc(rs_ready[0].sem, 1)

                def flat_rs(i):
                    if not runs(i):
                        return
                    pool.wait_ge(*vs[1].now(i))
                    pool.wait_ge(*flat_ready.before(i))
                    pool.tensor_tensor(rs[:, 1, :], ve[:, 1, :], half[:, 0:PG], ALU.pow).then_inc(rs_ready[1].sem, 1)

                def step(g, b):
                    flat_rs(g - 1)
                    if runs(g - 2):
                        R.pool_scatter(pool, g - 2, flat[b], dest)
                    head_rs(g + 3)
                skewed(pool, step, ahead=3)
                R.wait_landed(pool, GROUPS - 1)

            @block.sync
            def _(sp):
                turns(sp, 0, GROUPS // 2, lambda turn: M.fetch(sp, turn))
        clear_taken(nc)


def phase_finish(nc, x, state, rows, out_dram):
    with ExitStack() as ctx:
        M = Combine(ctx, nc, "fin", state, rows)
        stored = take_semaphore(ctx, nc, "fin_stored")
        with nc.Block() as block:
            @block.vector
            def _(dve):
                open_signals(dve, M.dve_signals)

        with nc.Block() as block:
            @block.scalar
            def _(act):
                turns(act, 0, GROUPS // 2, lambda turn: M.fetch(act, turn))

            @block.vector
            def _(dve):
                turns(dve, 0, GROUPS // 2, lambda turn: [M.vector_mix(dve, turn * 2 + b, b, x) for b in range(2)])

            @block.sync
            def _(sp):
                def body(g):
                    sp.wait_ge(*M.mixed.now(g, 2 * PG - 1))
                    sp.dma_start(out_dram[:, bass.ds(g * PG, PG), :], x[:, bass.ds(g * PG, PG), :]).then_inc(stored, 16)
                turns(sp, 0, GROUPS, body)
                sp.wait_ge(stored, 16 * GROUPS)


_INS = ['x', 'adj', 'L0_gnn_w_qkv', 'L0_gnn_ln1_g', 'L0_gnn_ln1_b', 'L0_gnn_ln2_g', 'L0_gnn_ln2_b', 'L0_gnn_w1',
        'L0_gnn_b1', 'L0_gnn_w2', 'L0_gnn_b2', 'L0_ffn_ln1_w', 'L0_ffn_ln2_w', 'L1_gnn_W1', 'L1_gnn_W2', 'L1_gnn_W3',
        'L1_ffn_Wg', 'L1_ffn_bg']


def laid_out(inputs):
    import numpy as np

    def T(w):
        return np.ascontiguousarray(np.asarray(w).T)

    eye = np.eye(128, dtype=np.float32)
    a = {"c_ident": eye}
    a["c_rev"] = np.ascontiguousarray(np.broadcast_to(NE - np.arange(NE, dtype=np.float32), (128, NE)))
    a["c_ids"] = (np.arange(128)[:, None] + 128 * np.arange(PAIRS)[None]).astype(np.float32)
    a["c_trash"] = (TOKENS + np.arange(128)[:, None] + 128 * np.arange(TRASH // 128)[None]).astype(np.float32)
    a["c_tri"] = np.triu(np.ones((128, 128), np.float32), 1)
    inv_freq = 1.0 / 10000.0 ** (np.arange(0, D1, 2, dtype=np.float32) / D1)
    ang = np.outer(np.arange(NODES, dtype=np.float32), inv_freq)
    cos, sin = np.cos(ang).T, np.sin(ang).T
    a["c_rope"] = np.ascontiguousarray(np.stack([np.tile(np.concatenate([cos, cos]), (H1, 1)),
                                                 np.tile(np.concatenate([-sin, sin]), (H1, 1))], axis=1), dtype=np.float32)
    n, m = np.arange(128)[:, None] % NODES, np.arange(NODES)[None, :]
    a["c_causal"] = np.where(m > n, np.float32(-1e30 * D1 ** 0.5), np.float32(0))
    swap = np.arange(D1) ^ (D1 // 2)
    wq = T(inputs["L0_ffn_wq"]).reshape(C, H1, D1)
    wk = np.repeat(T(inputs["L0_ffn_wk"]).reshape(C, KV1, D1), H1 // KV1, axis=1)
    for name, w in [("c_wq", wq), ("c_wk", wk)]:
        a[name] = np.ascontiguousarray(w.reshape(C, 128))
        a[name + "_x"] = np.ascontiguousarray(w[:, :, swap].reshape(C, 128))
    a["c_wv"] = T(inputs["L0_ffn_wv"])
    a["c_wo"] = T(inputs["L0_ffn_wo"])
    a["c_wr"] = T(inputs["L0_ffn_router_w"])
    e = np.arange(NE)
    a["c_le"] = np.ascontiguousarray(np.broadcast_to(e[None, :] <= e[:, None], (128, NE, NE)), dtype=np.float32)
    a["c_iota"] = np.arange(TILES, dtype=np.float32)

    def by_chunk(w):
        chunks = -(-w.shape[1] // 128)
        full = np.zeros((NE, chunks * 128, C), np.float32)
        full[:, :w.shape[1]] = w
        return full.reshape(NE, chunks, 128, C).transpose(0, 2, 1, 3).reshape(NE, 128, chunks * C)

    w1, w2, w3 = (np.asarray(inputs[f"L0_ffn_w{i}"]).transpose(0, 2, 1) for i in (1, 2, 3))
    a["c_wall1"] = np.ascontiguousarray(np.concatenate([w1, w3, by_chunk(w2)], axis=2))
    w1, w2, b1, b2 = (np.asarray(inputs["L1_ffn_" + n]) for n in ("W1", "W2", "b1", "b2"))
    a["c_wall2"] = np.ascontiguousarray(np.concatenate(
        [w1, by_chunk(w2), b1.reshape(NE, len(CH2), 128).transpose(0, 2, 1), np.broadcast_to(b2[:, None], (NE, 128, C))], axis=2))
    return a


def kernel(**inputs):
    import numpy as np
    import concourse.bacc as bacc
    from concourse import mybir as mb
    from concourse.bass_utils import run_bass_kernel_spmd as run

    nc = bacc.Bacc("TRN2", target_bir_lowering=False, num_devices=1)
    arrays = {n: np.ascontiguousarray(inputs[n]) for n in _INS}
    arrays.update(laid_out(inputs))
    A = {}
    for n, a in arrays.items():
        A[n] = nc.dram_tensor(f"in_{n}", a.shape, mb.dt.from_np(a.dtype), kind="ExternalInput").ap()
    out = nc.dram_tensor("out_0", (FRAMES, NODES, C), mb.dt.float32, kind="ExternalOutput").ap()
    build(nc, A, out)
    r = run(nc, [{f"in_{n}": a for n, a in arrays.items()}], core_ids=[0])
    return r.results[0]["out_0"]
```
